# Optimizing a Trainium2 kernel written in Bass

```python
import numpy as np
import jax
import jax.numpy as jnp

def _softmax(x, axis=-1):
    return jax.nn.softmax(x, axis=axis)

def _gelu(x):
    return jax.nn.gelu(x, approximate=True)

def _silu(x):
    return jax.nn.silu(x)

def _sigmoid(x):
    return jax.nn.sigmoid(x)

def _layernorm(x, axis=-1, eps=1e-05):
    m = jnp.mean(x, axis=axis, keepdims=True)
    v = jnp.var(x, axis=axis, keepdims=True)
    return (x - m) / jnp.sqrt(v + eps)

def _scatter_add(tgt, idx, src, axis=0):
    return tgt.at[idx].add(src)

def _segment_sum(src, seg, n):
    return jax.ops.segment_sum(src, seg, n)
kernel_name = 'mk_flamingo_gated_d4_seqx_r8_45713e'

def setup_inputs(seed: int=0):
    np.random.seed(seed)
    _w = jnp.asarray

    def _rec_inputs():
        import jax
        import jax.numpy as jnp
        _rk = jax.random.key(seed)
        x = -0.0003929 + 0.9999 * jax.random.normal(jax.random.fold_in(_rk, 1), (2, 512, 128), jnp.float32)
        _lenS = 512 - jax.random.randint(jax.random.fold_in(_rk, 7), (2,), 0, max(1, 512 // 4) + 1, jnp.int32)
        _lenS2 = 77 - jax.random.randint(jax.random.fold_in(_rk, 8), (2,), 0, max(1, 77 // 4) + 1, jnp.int32)
        _ctx_1024P = jax.random.normal(jax.random.fold_in(_rk, 11), (2, 16, 128), jnp.float32)
        _ctx_1024c = jax.random.dirichlet(jax.random.fold_in(_rk, 511), 0.3 * jnp.ones((16,), jnp.float32), (2, 77))
        _ctx_1024t = jnp.einsum('bsk,bkd->bsd', _ctx_1024c, _ctx_1024P)
        _ctx_1024t = _ctx_1024t * jax.lax.rsqrt(jnp.mean(jnp.square(_ctx_1024t)) + 1e-12) * 0.953939
        ctx_1024 = 2.81802e-05 + 1.00001 * (_ctx_1024t + 0.3 * jax.random.normal(jax.random.fold_in(_rk, 611), (2, 77, 128), jnp.float32))
        _g = jax.random.normal(jax.random.fold_in(_rk, 9001), (2, 4), jnp.float32)
        _g = jnp.sign(_g) * jnp.maximum(jnp.abs(_g), 1.0) + (_g == 0) * 1.0
        g_xattn = _g[0]
        g_ffn = _g[1]
        return (x, ctx_1024, g_xattn, g_ffn)
    x, ctx_1024, g_xattn, g_ffn = _rec_inputs()

    def _L0_xattn_setup():
        import jax, jax.numpy as jnp
        import numpy as np
        B, N, D = (4, 512, 128)
        H = 16
        HD = D // H
        EPS = 1e-06
        BASE_SPARSITY = 0.3
        KEEP = max(int((1.0 - BASE_SPARSITY) * HD), 1)
        LEAKY_SLOPE = 0.01

        def _focus(x, focusing_factor):
            x = jnp.abs(jnp.where(x >= 0, x, LEAKY_SLOPE * x)) + EPS
            nrm = x.mean(axis=-1, keepdims=True)
            return jax.nn.softmax(jnp.log(x) * focusing_factor, axis=-1) * nrm

        def _to_heads(x):
            b, n, d = x.shape
            return x.reshape(b, n, H, HD).transpose(0, 2, 1, 3).reshape(b * H, n, HD)

        def _topk_sparsify(x):
            c = x.shape[-1]
            flat = x.reshape(-1, c)
            _, idx = jax.lax.top_k(jnp.abs(flat), KEEP)
            rows = jnp.arange(flat.shape[0])[:, None]
            mask = jnp.zeros(flat.shape, dtype=bool).at[rows, idx].set(True)
            return (flat * mask).reshape(x.shape)
        key = jax.random.key(seed)
        ks = jax.random.split(key, 8)
        mk = lambda k_, shp, s: jax.random.normal(k_, shp, dtype=jnp.float32) * s
        return {'q': mk(ks[0], (B, N, D), 1.0), 'k': mk(ks[1], (B, N, D), 1.0), 'v': mk(ks[2], (B, N, D), 1.0), 'Wq': mk(ks[3], (D, D), 0.02), 'Wk': mk(ks[4], (D, D), 0.02), 'Wv': mk(ks[5], (D, D), 0.02), 'Wp': mk(ks[6], (D, D), 0.02), 'focusing_factor': jnp.asarray(3.0, dtype=jnp.float32)}
    _L0_xattn_all = _L0_xattn_setup()
    _L0_xattn_in = {k: v for k, v in _L0_xattn_all.items() if k in ('Wq', 'Wk', 'Wv', 'Wp', 'focusing_factor')}
    del _L0_xattn_all

    def _L0_ffn_setup():
        import jax, jax.numpy as jnp
        import numpy as np
        import math
        B, L, D = (4, 512, 128)
        F = 512
        E = 16
        CAP_FACTOR = 1.0
        EPS = 1e-05
        key = jax.random.key(seed)
        ks = jax.random.split(key, 8)
        std = 0.02
        return {'x': jax.random.normal(ks[0], (B, L, D), dtype=jnp.float32), 'norm_weight': jnp.ones((D,), dtype=jnp.float32), 'router_weight': jax.random.normal(ks[1], (E, D), dtype=jnp.float32) * std, 'router_bias': jnp.zeros((E,), dtype=jnp.float32), 'fc1_weight': jax.random.normal(ks[2], (E, F, D), dtype=jnp.float32) * std, 'fc1_bias': jnp.zeros((E, F), dtype=jnp.float32), 'fc2_weight': jax.random.normal(ks[3], (E, D, F), dtype=jnp.float32) * std, 'fc2_bias': jnp.zeros((E, D), dtype=jnp.float32)}
    _L0_ffn_all = _L0_ffn_setup()
    _L0_ffn_in = {k: v for k, v in _L0_ffn_all.items() if k in ('norm_weight', 'router_weight', 'router_bias', 'fc1_weight', 'fc1_bias', 'fc2_weight', 'fc2_bias')}
    del _L0_ffn_all

    def _L1_xattn_setup():
        import jax, jax.numpy as jnp
        import numpy as np
        import math
        D = 128
        H = 8
        HD = D // H
        TEMP = math.sqrt(D)
        EPS = 1e-05

        def _layernorm(x, g, b):
            mu = jnp.mean(x, axis=-1, keepdims=True)
            var = jnp.var(x, axis=-1, keepdims=True)
            return (x - mu) * jax.lax.rsqrt(var + EPS) * g + b
        key = jax.random.key(seed)
        ks = jax.random.split(key, 8)
        B, Lq, Lk = (4, 256, 256)
        Q = jax.random.normal(ks[0], (B, Lq, D), dtype=jnp.float32)
        K = jax.random.normal(ks[1], (B, Lk, D), dtype=jnp.float32)
        V = jax.random.normal(ks[2], (B, Lk, D), dtype=jnp.float32)
        Wq = jax.random.normal(ks[3], (D, D), dtype=jnp.float32) * 0.02
        Wk = jax.random.normal(ks[4], (D, D), dtype=jnp.float32) * 0.02
        Wv = jax.random.normal(ks[5], (D, D), dtype=jnp.float32) * 0.02
        Wo = jax.random.normal(ks[6], (D, D), dtype=jnp.float32) * 0.02
        pre_g = jnp.ones((D,), jnp.float32)
        pre_b = jnp.zeros((D,), jnp.float32)
        ln_g = jnp.ones((D,), jnp.float32)
        ln_b = jnp.zeros((D,), jnp.float32)
        return {'Q': Q, 'K': K, 'V': V, 'Wq': Wq, 'Wk': Wk, 'Wv': Wv, 'Wo': Wo, 'pre_g': pre_g, 'pre_b': pre_b, 'ln_g': ln_g, 'ln_b': ln_b}
    _L1_xattn_all = _L1_xattn_setup()
    _L1_xattn_in = {k: v for k, v in _L1_xattn_all.items() if k in ('Wq', 'Wk', 'Wv', 'Wo', 'pre_g', 'pre_b', 'ln_g', 'ln_b')}
    del _L1_xattn_all

    def _L1_ffn_setup():
        import jax, jax.numpy as jnp
        import numpy as np
        from math import sqrt
        B, S, D, H, E, K, FF = (2, 128, 128, 16, 8, 2, 512)
        HD = D // H
        EPS = 1e-05

        def _rope_cache(seq_len, hd):
            inv_freq = 1.0 / 10000.0 ** (jnp.arange(0, hd, 2, dtype=jnp.float32) / hd)
            t = jnp.arange(seq_len, dtype=jnp.float32)
            freqs = t[:, None] * inv_freq[None, :]
            emb = jnp.concatenate([freqs, freqs], axis=-1)
            return (jnp.cos(emb), jnp.sin(emb))

        def _rotate_half(x):
            x1, x2 = jnp.split(x, 2, axis=-1)
            return jnp.concatenate([-x2, x1], axis=-1)

        def _layernorm(x, g, b):
            m = jnp.mean(x, axis=-1, keepdims=True)
            v = jnp.var(x, axis=-1, keepdims=True)
            return (x - m) * jax.lax.rsqrt(v + EPS) * g + b

        def _forward(x, Wq, bq, Wk, bk, Wv, bv, Wo, bo, Wg, bg, W1, b1, W2, b2, g1, be1, g2, be2):
            bsz, seq, d = x.shape
            q = (x @ Wq + bq).reshape(bsz, seq, H, HD).transpose(0, 2, 1, 3)
            k = (x @ Wk + bk).reshape(bsz, seq, H, HD).transpose(0, 2, 1, 3)
            v = (x @ Wv + bv).reshape(bsz, seq, H, HD).transpose(0, 2, 1, 3)
            cos, sin = _rope_cache(seq, HD)
            cos = cos[None, None]
            sin = sin[None, None]
            q = q * cos + _rotate_half(q) * sin
            k = k * cos + _rotate_half(k) * sin
            scores = jnp.einsum('bhqd,bhkd->bhqk', q, k) / sqrt(HD)
            attn = jax.nn.softmax(scores, axis=-1)
            ao = jnp.einsum('bhqk,bhkd->bhqd', attn, v)
            ao = ao.transpose(0, 2, 1, 3).reshape(bsz, seq, d)
            attn_out = ao @ Wo + bo
            x1 = _layernorm(x + attn_out, g1, be1)
            gate_logits = x1 @ Wg + bg
            gate_probs = jax.nn.softmax(gate_logits, axis=-1)
            topk_p, topk_i = jax.lax.top_k(gate_probs, K)
            topk_p = topk_p / jnp.sum(topk_p, axis=-1, keepdims=True)
            comb = jnp.sum(jax.nn.one_hot(topk_i, E, dtype=x.dtype) * topk_p[..., None], axis=-2)
            h = jax.nn.gelu(jnp.einsum('bsd,edf->bsef', x1, W1) + b1, approximate=False)
            y = jnp.einsum('bsef,efd->bsed', h, W2) + b2
            moe_out = jnp.einsum('bse,bsed->bsd', comb, y)
            return _layernorm(x1 + moe_out, g2, be2)
        key = jax.random.key(seed)
        ks = jax.random.split(key, 20)
        std = 0.02
        p = lambda k, sh: jax.random.normal(k, sh, dtype=jnp.float32) * std
        return {'x': jax.random.normal(ks[0], (B, S, D), dtype=jnp.float32), 'Wq': p(ks[1], (D, D)), 'bq': jnp.zeros((D,), jnp.float32), 'Wk': p(ks[2], (D, D)), 'bk': jnp.zeros((D,), jnp.float32), 'Wv': p(ks[3], (D, D)), 'bv': jnp.zeros((D,), jnp.float32), 'Wo': p(ks[4], (D, D)), 'bo': jnp.zeros((D,), jnp.float32), 'Wg': p(ks[5], (D, E)), 'bg': jnp.zeros((E,), jnp.float32), 'W1': p(ks[6], (E, D, FF)), 'b1': jnp.zeros((E, FF), jnp.float32), 'W2': p(ks[7], (E, FF, D)), 'b2': jnp.zeros((E, D), jnp.float32), 'g1': jnp.ones((D,), jnp.float32), 'be1': jnp.zeros((D,), jnp.float32), 'g2': jnp.ones((D,), jnp.float32), 'be2': jnp.zeros((D,), jnp.float32)}
    _L1_ffn_all = _L1_ffn_setup()
    _L1_ffn_in = {k: v for k, v in _L1_ffn_all.items() if k in ('Wq', 'bq', 'Wk', 'bk', 'Wv', 'bv', 'Wo', 'bo', 'Wg', 'bg', 'W1', 'b1', 'W2', 'b2', 'g1', 'be1', 'g2', 'be2')}
    del _L1_ffn_all

    def _L2_xattn_setup():
        import jax, jax.numpy as jnp
        import numpy as np
        EMBED = 128
        HEADS = 16
        HEAD_DIM = EMBED // HEADS
        key = jax.random.key(seed)
        ks = jax.random.split(key, 7)
        B, Sd, Se = (4, 256, 256)
        dec = jax.random.normal(ks[0], (B, Sd, EMBED), dtype=jnp.float32)
        enc = jax.random.normal(ks[1], (B, Se, EMBED), dtype=jnp.float32)
        scale = 1.0 / np.sqrt(EMBED)
        W_q = jax.random.normal(ks[2], (EMBED, EMBED), dtype=jnp.float32) * scale
        W_k = jax.random.normal(ks[3], (EMBED, EMBED), dtype=jnp.float32) * scale
        W_v = jax.random.normal(ks[4], (EMBED, EMBED), dtype=jnp.float32) * scale
        W_o = jax.random.normal(ks[5], (EMBED, EMBED), dtype=jnp.float32) * scale
        b_o = jax.random.normal(ks[6], (EMBED,), dtype=jnp.float32) * 0.01
        return {'decoder_input': dec, 'encoder_output': enc, 'W_q': W_q, 'W_k': W_k, 'W_v': W_v, 'W_o': W_o, 'b_o': b_o}
    _L2_xattn_all = _L2_xattn_setup()
    _L2_xattn_in = {k: v for k, v in _L2_xattn_all.items() if k in ('W_q', 'W_k', 'W_v', 'W_o', 'b_o')}
    del _L2_xattn_all

    def _L2_ffn_setup():
        import jax, jax.numpy as jnp
        import numpy as np
        TOP_K = 2
        key = jax.random.key(seed)
        ks = jax.random.split(key, 5)
        B, T, D, F, E = (2, 256, 128, 512, 8)
        x = jax.random.normal(ks[0], (B, T, D), dtype=jnp.float32)
        router_w = jax.random.normal(ks[1], (D, E + 1), dtype=jnp.float32) * 0.02
        router_b = jax.random.normal(ks[2], (E + 1,), dtype=jnp.float32) * 0.02
        w1 = jax.random.normal(ks[3], (E, D, F), dtype=jnp.float32) * 0.02
        w2 = jax.random.normal(ks[4], (E, F, D), dtype=jnp.float32) * 0.02
        return {'x': x, 'router_w': router_w, 'router_b': router_b, 'w1': w1, 'w2': w2}
    _L2_ffn_all = _L2_ffn_setup()
    _L2_ffn_in = {k: v for k, v in _L2_ffn_all.items() if k in ('router_w', 'router_b', 'w1', 'w2')}
    del _L2_ffn_all

    def _L3_xattn_setup():
        import jax, jax.numpy as jnp
        import numpy as np
        DIM = 128
        NUM_HEADS = 16
        DIM_HEAD = 64
        INNER = NUM_HEADS * DIM_HEAD
        SCALE = DIM_HEAD ** (-0.5)

        def _layernorm(x, gamma, beta, eps=1e-05):
            mu = jnp.mean(x, axis=-1, keepdims=True)
            var = jnp.mean(jnp.square(x - mu), axis=-1, keepdims=True)
            return (x - mu) * jax.lax.rsqrt(var + eps) * gamma + beta
        key = jax.random.key(seed)
        ks = jax.random.split(key, 8)
        B, SQ, SK = (2, 256, 512)
        x = jax.random.normal(ks[0], (B, SQ, DIM), dtype=jnp.float32)
        context = jax.random.normal(ks[1], (B, SK, DIM), dtype=jnp.float32)
        ln_gamma = jnp.ones((DIM,), jnp.float32)
        ln_beta = jnp.zeros((DIM,), jnp.float32)
        w_q = jax.random.normal(ks[2], (DIM, INNER), dtype=jnp.float32) / np.sqrt(DIM)
        w_kv = jax.random.normal(ks[3], (DIM, 2 * INNER), dtype=jnp.float32) / np.sqrt(DIM)
        w_out = jax.random.normal(ks[4], (INNER, DIM), dtype=jnp.float32) / np.sqrt(INNER)
        b_out = jnp.zeros((DIM,), jnp.float32)
        gate = jnp.array([0.5], jnp.float32)
        return {'x': x, 'context': context, 'ln_gamma': ln_gamma, 'ln_beta': ln_beta, 'w_q': w_q, 'w_kv': w_kv, 'w_out': w_out, 'b_out': b_out, 'gate': gate}
    _L3_xattn_all = _L3_xattn_setup()
    _L3_xattn_in = {k: v for k, v in _L3_xattn_all.items() if k in ('ln_gamma', 'ln_beta', 'w_q', 'w_kv', 'w_out', 'b_out', 'gate')}
    del _L3_xattn_all

    def _L3_ffn_setup():
        import jax, jax.numpy as jnp
        import numpy as np
        EMBED_DIM = 128
        HIDDEN_DIM = 512
        NUM_EXPERTS = 8
        TOP_K = 2
        key = jax.random.key(seed)
        ks = jax.random.split(key, 4)
        std1 = float(np.sqrt(2.0 / EMBED_DIM))
        std2 = float(np.sqrt(2.0 / HIDDEN_DIM))
        x = jax.random.normal(ks[0], (1, 256, EMBED_DIM), dtype=jnp.float32)
        w_router = jax.random.normal(ks[1], (EMBED_DIM, NUM_EXPERTS), dtype=jnp.float32) * 0.02
        w1 = jax.random.normal(ks[2], (NUM_EXPERTS, EMBED_DIM, HIDDEN_DIM), dtype=jnp.float32) * std1
        b1 = jnp.zeros((NUM_EXPERTS, HIDDEN_DIM), dtype=jnp.float32)
        w2 = jax.random.normal(ks[3], (NUM_EXPERTS, HIDDEN_DIM, EMBED_DIM), dtype=jnp.float32) * std2
        b2 = jnp.zeros((NUM_EXPERTS, EMBED_DIM), dtype=jnp.float32)
        return {'x': x, 'w_router': w_router, 'w1': w1, 'b1': b1, 'w2': w2, 'b2': b2}
    _L3_ffn_all = _L3_ffn_setup()
    _L3_ffn_in = {k: v for k, v in _L3_ffn_all.items() if k in ('w_router', 'w1', 'b1', 'w2', 'b2')}
    del _L3_ffn_all
    return {'x': x, 'ctx_1024': ctx_1024, 'g_xattn': g_xattn, 'g_ffn': g_ffn, 'L0_xattn_Wq': _L0_xattn_in['Wq'], 'L0_xattn_Wk': _L0_xattn_in['Wk'], 'L0_xattn_Wv': _L0_xattn_in['Wv'], 'L0_xattn_Wp': _L0_xattn_in['Wp'], 'L0_xattn_focusing_factor': _L0_xattn_in['focusing_factor'], 'L0_ffn_norm_weight': _L0_ffn_in['norm_weight'], 'L0_ffn_router_weight': _L0_ffn_in['router_weight'], 'L0_ffn_router_bias': _L0_ffn_in['router_bias'], 'L0_ffn_fc1_weight': _L0_ffn_in['fc1_weight'], 'L0_ffn_fc1_bias': _L0_ffn_in['fc1_bias'], 'L0_ffn_fc2_weight': _L0_ffn_in['fc2_weight'], 'L0_ffn_fc2_bias': _L0_ffn_in['fc2_bias'], 'L1_xattn_Wq': _L1_xattn_in['Wq'], 'L1_xattn_Wk': _L1_xattn_in['Wk'], 'L1_xattn_Wv': _L1_xattn_in['Wv'], 'L1_xattn_Wo': _L1_xattn_in['Wo'], 'L1_xattn_pre_g': _L1_xattn_in['pre_g'], 'L1_xattn_pre_b': _L1_xattn_in['pre_b'], 'L1_xattn_ln_g': _L1_xattn_in['ln_g'], 'L1_xattn_ln_b': _L1_xattn_in['ln_b'], 'L1_ffn_Wq': _L1_ffn_in['Wq'], 'L1_ffn_bq': _L1_ffn_in['bq'], 'L1_ffn_Wk': _L1_ffn_in['Wk'], 'L1_ffn_bk': _L1_ffn_in['bk'], 'L1_ffn_Wv': _L1_ffn_in['Wv'], 'L1_ffn_bv': _L1_ffn_in['bv'], 'L1_ffn_Wo': _L1_ffn_in['Wo'], 'L1_ffn_bo': _L1_ffn_in['bo'], 'L1_ffn_Wg': _L1_ffn_in['Wg'], 'L1_ffn_bg': _L1_ffn_in['bg'], 'L1_ffn_W1': _L1_ffn_in['W1'], 'L1_ffn_b1': _L1_ffn_in['b1'], 'L1_ffn_W2': _L1_ffn_in['W2'], 'L1_ffn_b2': _L1_ffn_in['b2'], 'L1_ffn_g1': _L1_ffn_in['g1'], 'L1_ffn_be1': _L1_ffn_in['be1'], 'L1_ffn_g2': _L1_ffn_in['g2'], 'L1_ffn_be2': _L1_ffn_in['be2'], 'L2_xattn_W_q': _L2_xattn_in['W_q'], 'L2_xattn_W_k': _L2_xattn_in['W_k'], 'L2_xattn_W_v': _L2_xattn_in['W_v'], 'L2_xattn_W_o': _L2_xattn_in['W_o'], 'L2_xattn_b_o': _L2_xattn_in['b_o'], 'L2_ffn_router_w': _L2_ffn_in['router_w'], 'L2_ffn_router_b': _L2_ffn_in['router_b'], 'L2_ffn_w1': _L2_ffn_in['w1'], 'L2_ffn_w2': _L2_ffn_in['w2'], 'L3_xattn_ln_gamma': _L3_xattn_in['ln_gamma'], 'L3_xattn_ln_beta': _L3_xattn_in['ln_beta'], 'L3_xattn_w_q': _L3_xattn_in['w_q'], 'L3_xattn_w_kv': _L3_xattn_in['w_kv'], 'L3_xattn_w_out': _L3_xattn_in['w_out'], 'L3_xattn_b_out': _L3_xattn_in['b_out'], 'L3_xattn_gate': _L3_xattn_in['gate'], 'L3_ffn_w_router': _L3_ffn_in['w_router'], 'L3_ffn_w1': _L3_ffn_in['w1'], 'L3_ffn_b1': _L3_ffn_in['b1'], 'L3_ffn_w2': _L3_ffn_in['w2'], 'L3_ffn_b2': _L3_ffn_in['b2']}

def reference(x, ctx_1024, g_xattn, g_ffn, L0_xattn_Wq, L0_xattn_Wk, L0_xattn_Wv, L0_xattn_Wp, L0_xattn_focusing_factor, L0_ffn_norm_weight, L0_ffn_router_weight, L0_ffn_router_bias, L0_ffn_fc1_weight, L0_ffn_fc1_bias, L0_ffn_fc2_weight, L0_ffn_fc2_bias, L1_xattn_Wq, L1_xattn_Wk, L1_xattn_Wv, L1_xattn_Wo, L1_xattn_pre_g, L1_xattn_pre_b, L1_xattn_ln_g, L1_xattn_ln_b, L1_ffn_Wq, L1_ffn_bq, L1_ffn_Wk, L1_ffn_bk, L1_ffn_Wv, L1_ffn_bv, L1_ffn_Wo, L1_ffn_bo, L1_ffn_Wg, L1_ffn_bg, L1_ffn_W1, L1_ffn_b1, L1_ffn_W2, L1_ffn_b2, L1_ffn_g1, L1_ffn_be1, L1_ffn_g2, L1_ffn_be2, L2_xattn_W_q, L2_xattn_W_k, L2_xattn_W_v, L2_xattn_W_o, L2_xattn_b_o, L2_ffn_router_w, L2_ffn_router_b, L2_ffn_w1, L2_ffn_w2, L3_xattn_ln_gamma, L3_xattn_ln_beta, L3_xattn_w_q, L3_xattn_w_kv, L3_xattn_w_out, L3_xattn_b_out, L3_xattn_gate, L3_ffn_w_router, L3_ffn_w1, L3_ffn_b1, L3_ffn_w2, L3_ffn_b2):
    import jax
    import jax.numpy as jnp

    def _L0_xattn_ref(q, k, v, Wq, Wk, Wv, Wp, focusing_factor):
        import jax, jax.numpy as jnp
        import numpy as np
        B, N, D = (4, 512, 128)
        H = 16
        HD = D // H
        EPS = 1e-06
        BASE_SPARSITY = 0.3
        KEEP = max(int((1.0 - BASE_SPARSITY) * HD), 1)
        LEAKY_SLOPE = 0.01

        def _focus(x, focusing_factor):
            x = jnp.abs(jnp.where(x >= 0, x, LEAKY_SLOPE * x)) + EPS
            nrm = x.mean(axis=-1, keepdims=True)
            return jax.nn.softmax(jnp.log(x) * focusing_factor, axis=-1) * nrm

        def _to_heads(x):
            b, n, d = x.shape
            return x.reshape(b, n, H, HD).transpose(0, 2, 1, 3).reshape(b * H, n, HD)

        def _topk_sparsify(x):
            c = x.shape[-1]
            flat = x.reshape(-1, c)
            _, idx = jax.lax.top_k(jnp.abs(flat), KEEP)
            rows = jnp.arange(flat.shape[0])[:, None]
            mask = jnp.zeros(flat.shape, dtype=bool).at[rows, idx].set(True)
            return (flat * mask).reshape(x.shape)
        b, n, d = q.shape
        q = q @ Wq.T
        k = k @ Wk.T
        v = v @ Wv.T
        q = _focus(q, focusing_factor)
        k = _focus(k, focusing_factor)
        qh, kh, vh = (_to_heads(q), _to_heads(k), _to_heads(v))
        qh = _topk_sparsify(qh)
        kh = _topk_sparsify(kh)
        length_k = float(n)
        sqrt_l = jnp.sqrt(jnp.asarray(length_k, dtype=q.dtype))
        k_mean = kh.mean(axis=1)
        z_inv = jnp.einsum('bnd,bd->bn', qh, k_mean) + EPS
        kv = jnp.einsum('bnc,bnd->bcd', kh / sqrt_l, vh / sqrt_l)
        y = jnp.einsum('bnc,bcd->bnd', qh, kv) / z_inv[..., None]
        y = y.reshape(b, H, n, HD).transpose(0, 2, 1, 3).reshape(b, n, d)
        return y @ Wp.T

    def _L0_ffn_ref(x, norm_weight, router_weight, router_bias, fc1_weight, fc1_bias, fc2_weight, fc2_bias):
        import jax, jax.numpy as jnp
        import numpy as np
        import math
        B, L, D = (4, 512, 128)
        F = 512
        E = 16
        CAP_FACTOR = 1.0
        EPS = 1e-05
        b, l, d = x.shape
        n_tokens = b * l
        n_experts = router_weight.shape[0]
        capacity = max(1, math.ceil(CAP_FACTOR * n_tokens / n_experts))
        top_k = min(capacity, n_tokens)
        xf = x.reshape(n_tokens, d)
        rms = jnp.sqrt(jnp.mean(xf * xf, axis=-1, keepdims=True) + EPS)
        xn = xf / rms * norm_weight
        logits = xn @ router_weight.T + router_bias
        probs = jax.nn.softmax(logits, axis=-1)
        _, idx = jax.lax.top_k(logits.T, top_k)
        xe = xn[idx]
        h = jnp.einsum('ecd,efd->ecf', xe, fc1_weight) + fc1_bias[:, None, :]
        h = jax.nn.gelu(h, approximate=False)
        y = jnp.einsum('ecf,edf->ecd', h, fc2_weight) + fc2_bias[:, None, :]
        gates = jnp.take_along_axis(probs.T, idx, axis=1)
        flat_idx = idx.reshape(-1)
        contrib = (y * gates[:, :, None]).reshape(-1, d)
        output = jnp.zeros((n_tokens, d), dtype=x.dtype).at[flat_idx].add(contrib)
        gate_sums = jnp.zeros((n_tokens, 1), dtype=x.dtype).at[flat_idx].add(gates.reshape(-1, 1))
        assigned = gate_sums > 0
        output = jnp.where(assigned, output / jnp.where(assigned, gate_sums, 1.0), output)
        return output.reshape(b, l, d)

    def _L1_xattn_ref(Q, K, V, Wq, Wk, Wv, Wo, pre_g, pre_b, ln_g, ln_b):
        import jax, jax.numpy as jnp
        import numpy as np
        import math
        D = 128
        H = 8
        HD = D // H
        TEMP = math.sqrt(D)
        EPS = 1e-05

        def _layernorm(x, g, b):
            mu = jnp.mean(x, axis=-1, keepdims=True)
            var = jnp.var(x, axis=-1, keepdims=True)
            return (x - mu) * jax.lax.rsqrt(var + EPS) * g + b
        B, Lq, _ = Q.shape
        Lk = K.shape[1]
        Qn = _layernorm(Q, pre_g, pre_b)
        Kn = _layernorm(K, pre_g, pre_b)
        q = (Qn @ Wq).reshape(B, Lq, H, HD)
        k = (Kn @ Wk).reshape(B, Lk, H, HD)
        v = (V @ Wv).reshape(B, Lk, H, HD)
        scores = jnp.einsum('bqhd,bkhd->bhqk', q, k) / TEMP
        scores = jnp.clip(scores, -10000.0, 10000.0)
        A = jax.nn.softmax(scores, axis=-1)
        O = jnp.einsum('bhqk,bkhd->bqhd', A, v).reshape(B, Lq, D)
        O = _layernorm(O, ln_g, ln_b)
        O = O + jax.nn.gelu(O @ Wo, approximate=False)
        return O

    def _L1_ffn_ref(x, Wq, bq, Wk, bk, Wv, bv, Wo, bo, Wg, bg, W1, b1, W2, b2, g1, be1, g2, be2):
        import jax, jax.numpy as jnp
        import numpy as np
        from math import sqrt
        B, S, D, H, E, K, FF = (2, 128, 128, 16, 8, 2, 512)
        HD = D // H
        EPS = 1e-05

        def _rope_cache(seq_len, hd):
            inv_freq = 1.0 / 10000.0 ** (jnp.arange(0, hd, 2, dtype=jnp.float32) / hd)
            t = jnp.arange(seq_len, dtype=jnp.float32)
            freqs = t[:, None] * inv_freq[None, :]
            emb = jnp.concatenate([freqs, freqs], axis=-1)
            return (jnp.cos(emb), jnp.sin(emb))

        def _rotate_half(x):
            x1, x2 = jnp.split(x, 2, axis=-1)
            return jnp.concatenate([-x2, x1], axis=-1)

        def _layernorm(x, g, b):
            m = jnp.mean(x, axis=-1, keepdims=True)
            v = jnp.var(x, axis=-1, keepdims=True)
            return (x - m) * jax.lax.rsqrt(v + EPS) * g + b

        def _forward(x, Wq, bq, Wk, bk, Wv, bv, Wo, bo, Wg, bg, W1, b1, W2, b2, g1, be1, g2, be2):
            bsz, seq, d = x.shape
            q = (x @ Wq + bq).reshape(bsz, seq, H, HD).transpose(0, 2, 1, 3)
            k = (x @ Wk + bk).reshape(bsz, seq, H, HD).transpose(0, 2, 1, 3)
            v = (x @ Wv + bv).reshape(bsz, seq, H, HD).transpose(0, 2, 1, 3)
            cos, sin = _rope_cache(seq, HD)
            cos = cos[None, None]
            sin = sin[None, None]
            q = q * cos + _rotate_half(q) * sin
            k = k * cos + _rotate_half(k) * sin
            scores = jnp.einsum('bhqd,bhkd->bhqk', q, k) / sqrt(HD)
            attn = jax.nn.softmax(scores, axis=-1)
            ao = jnp.einsum('bhqk,bhkd->bhqd', attn, v)
            ao = ao.transpose(0, 2, 1, 3).reshape(bsz, seq, d)
            attn_out = ao @ Wo + bo
            x1 = _layernorm(x + attn_out, g1, be1)
            gate_logits = x1 @ Wg + bg
            gate_probs = jax.nn.softmax(gate_logits, axis=-1)
            topk_p, topk_i = jax.lax.top_k(gate_probs, K)
            topk_p = topk_p / jnp.sum(topk_p, axis=-1, keepdims=True)
            comb = jnp.sum(jax.nn.one_hot(topk_i, E, dtype=x.dtype) * topk_p[..., None], axis=-2)
            h = jax.nn.gelu(jnp.einsum('bsd,edf->bsef', x1, W1) + b1, approximate=False)
            y = jnp.einsum('bsef,efd->bsed', h, W2) + b2
            moe_out = jnp.einsum('bse,bsed->bsd', comb, y)
            return _layernorm(x1 + moe_out, g2, be2)
        return _forward(x, Wq, bq, Wk, bk, Wv, bv, Wo, bo, Wg, bg, W1, b1, W2, b2, g1, be1, g2, be2)

    def _L2_xattn_ref(decoder_input, encoder_output, W_q, W_k, W_v, W_o, b_o):
        import jax, jax.numpy as jnp
        import numpy as np
        EMBED = 128
        HEADS = 16
        HEAD_DIM = EMBED // HEADS
        B, Sd, E = decoder_input.shape
        Se = encoder_output.shape[1]
        Q = (decoder_input @ W_q).reshape(B, Sd, HEADS, HEAD_DIM)
        K = (encoder_output @ W_k).reshape(B, Se, HEADS, HEAD_DIM)
        V = (encoder_output @ W_v).reshape(B, Se, HEADS, HEAD_DIM)
        scores = jnp.einsum('bqhd,bkhd->bhqk', Q, K) / jnp.sqrt(jnp.float32(HEAD_DIM))
        attn = jax.nn.softmax(scores, axis=-1)
        out = jnp.einsum('bhqk,bkhd->bqhd', attn, V).reshape(B, Sd, E)
        return out @ W_o + b_o

    def _L2_ffn_ref(x, router_w, router_b, w1, w2):
        import jax, jax.numpy as jnp
        import numpy as np
        TOP_K = 2
        E = w1.shape[0]
        logits = x @ router_w + router_b
        probs = jax.nn.softmax(logits, axis=-1)
        top_v, top_i = jax.lax.top_k(probs, TOP_K)
        gates = jnp.sum(jax.nn.one_hot(top_i, E + 1, dtype=x.dtype) * top_v[..., None], axis=-2)
        h = jax.nn.gelu(jnp.einsum('btd,edf->ebtf', x, w1), approximate=False)
        y = jnp.einsum('ebtf,efd->ebtd', h, w2)
        out = jnp.einsum('bte,ebtd->btd', gates[..., :E], y) + gates[..., E:] * x
        return out

    def _L3_xattn_ref(x, context, ln_gamma, ln_beta, w_q, w_kv, w_out, b_out, gate):
        import jax, jax.numpy as jnp
        import numpy as np
        DIM = 128
        NUM_HEADS = 16
        DIM_HEAD = 64
        INNER = NUM_HEADS * DIM_HEAD
        SCALE = DIM_HEAD ** (-0.5)

        def _layernorm(x, gamma, beta, eps=1e-05):
            mu = jnp.mean(x, axis=-1, keepdims=True)
            var = jnp.mean(jnp.square(x - mu), axis=-1, keepdims=True)
            return (x - mu) * jax.lax.rsqrt(var + eps) * gamma + beta
        B, SQ, _ = x.shape
        SK = context.shape[1]
        xn = _layernorm(x, ln_gamma, ln_beta)
        q = (xn @ w_q).reshape(B, SQ, NUM_HEADS, DIM_HEAD)
        kv = context @ w_kv
        k, v = jnp.split(kv, 2, axis=-1)
        k = k.reshape(B, SK, NUM_HEADS, DIM_HEAD)
        v = v.reshape(B, SK, NUM_HEADS, DIM_HEAD)
        scores = jnp.einsum('bqhd,bkhd->bhqk', q * SCALE, k)
        attn = jax.nn.softmax(scores, axis=-1)
        out = jnp.einsum('bhqk,bkhd->bqhd', attn, v).reshape(B, SQ, INNER)
        out = out @ w_out + b_out
        return out * jnp.tanh(gate[0])

    def _L3_ffn_ref(x, w_router, w1, b1, w2, b2):
        import jax, jax.numpy as jnp
        import numpy as np
        EMBED_DIM = 128
        HIDDEN_DIM = 512
        NUM_EXPERTS = 8
        TOP_K = 2
        orig_shape = x.shape
        xf = x.reshape(-1, EMBED_DIM)
        logits = xf @ w_router
        probs = jax.nn.softmax(logits, axis=-1)
        topk_w, topk_idx = jax.lax.top_k(probs, TOP_K)
        mask = jax.nn.one_hot(topk_idx, NUM_EXPERTS, dtype=xf.dtype)
        weights = jnp.sum(topk_w[..., None] * mask, axis=1)
        h = jnp.einsum('te,ieh->tih', xf, w1) + b1
        h = jax.nn.gelu(h)
        out = jnp.einsum('tih,ihe->tie', h, w2) + b2
        out = jnp.sum(out * weights[..., None], axis=1)
        return out.reshape(orig_shape)
    x = x + jnp.tanh(g_xattn[0]) * _L0_xattn_ref(_layernorm(x, axis=-1), ctx_1024, ctx_1024, L0_xattn_Wq, L0_xattn_Wk, L0_xattn_Wv, L0_xattn_Wp, L0_xattn_focusing_factor)
    x = x + jnp.tanh(g_ffn[0]) * _L0_ffn_ref(_layernorm(x, axis=-1), L0_ffn_norm_weight, L0_ffn_router_weight, L0_ffn_router_bias, L0_ffn_fc1_weight, L0_ffn_fc1_bias, L0_ffn_fc2_weight, L0_ffn_fc2_bias)
    x = x + jnp.tanh(g_xattn[1]) * _L1_xattn_ref(_layernorm(x, axis=-1), ctx_1024, ctx_1024, L1_xattn_Wq, L1_xattn_Wk, L1_xattn_Wv, L1_xattn_Wo, L1_xattn_pre_g, L1_xattn_pre_b, L1_xattn_ln_g, L1_xattn_ln_b)
    x = x + jnp.tanh(g_ffn[1]) * _L1_ffn_ref(_layernorm(x, axis=-1), L1_ffn_Wq, L1_ffn_bq, L1_ffn_Wk, L1_ffn_bk, L1_ffn_Wv, L1_ffn_bv, L1_ffn_Wo, L1_ffn_bo, L1_ffn_Wg, L1_ffn_bg, L1_ffn_W1, L1_ffn_b1, L1_ffn_W2, L1_ffn_b2, L1_ffn_g1, L1_ffn_be1, L1_ffn_g2, L1_ffn_be2)
    x = x + jnp.tanh(g_xattn[2]) * _L2_xattn_ref(_layernorm(x, axis=-1), ctx_1024, L2_xattn_W_q, L2_xattn_W_k, L2_xattn_W_v, L2_xattn_W_o, L2_xattn_b_o)
    x = x + jnp.tanh(g_ffn[2]) * _L2_ffn_ref(_layernorm(x, axis=-1), L2_ffn_router_w, L2_ffn_router_b, L2_ffn_w1, L2_ffn_w2)
    x = x + jnp.tanh(g_xattn[3]) * _L3_xattn_ref(_layernorm(x, axis=-1), ctx_1024, L3_xattn_ln_gamma, L3_xattn_ln_beta, L3_xattn_w_q, L3_xattn_w_kv, L3_xattn_w_out, L3_xattn_b_out, L3_xattn_gate)
    x = x + jnp.tanh(g_ffn[3]) * _L3_ffn_ref(_layernorm(x, axis=-1), L3_ffn_w_router, L3_ffn_w1, L3_ffn_b1, L3_ffn_w2, L3_ffn_b2)
    return x

_drawn_inputs = setup_inputs


def setup_inputs(seed=0):
    import zlib

    import numpy as np

    out = dict(_drawn_inputs(seed))
    spreads = {'L0_ffn_norm_weight': (1.0, 0.2),
     'L0_ffn_router_bias': (0.0, 0.8),
     'L0_ffn_fc1_bias': (0.0, 0.519),
     'L0_ffn_fc2_bias': (0.0, 0.1),
     'L1_xattn_pre_g': (1.0, 0.6),
     'L1_xattn_pre_b': (0.0, 0.8),
     'L1_xattn_ln_g': (1.0, 0.2),
     'L1_xattn_ln_b': (0.0, 0.1),
     'L1_ffn_bq': (0.0, 0.8),
     'L1_ffn_bk': (0.0, 0.8),
     'L1_ffn_bv': (0.0, 0.51),
     'L1_ffn_bo': (0.0, 0.1),
     'L1_ffn_bg': (0.0, 0.299),
     'L1_ffn_b1': (0.0, 0.78),
     'L1_ffn_b2': (0.0, 0.1),
     'L1_ffn_g1': (1.0, 0.2),
     'L1_ffn_be1': (0.0, 0.1),
     'L1_ffn_g2': (1.0, 0.2),
     'L1_ffn_be2': (0.0, 0.1),
     'L3_xattn_ln_gamma': (1.0, 0.6),
     'L3_xattn_ln_beta': (0.0, 0.8),
     'L3_xattn_b_out': (0.0, 0.395),
     'L3_ffn_b1': (0.0, 0.8),
     'L3_ffn_b2': (0.0, 0.8)}
    factors = {'g_ffn': 24.712,
     'L0_xattn_Wq': 8.0,
     'L0_xattn_Wk': 8.0,
     'L0_xattn_Wv': 8.0,
     'L0_xattn_Wp': 8.0,
     'L1_xattn_Wq': 6.003,
     'L1_xattn_Wk': 5.924,
     'L1_ffn_Wq': 8.0,
     'L1_ffn_Wk': 8.0,
     'L1_ffn_Wv': 3.191,
     'L1_ffn_Wo': 2.803,
     'L1_ffn_W1': 2.923,
     'L1_ffn_W2': 2.782,
     'L2_xattn_b_o': 6.846,
     'L2_ffn_router_b': 8.0,
     'L2_ffn_w1': 8.0,
     'L2_ffn_w2': 8.0}
    for name, (base, spread) in spreads.items():
        noise = np.random.default_rng([zlib.crc32(name.encode()), seed]).standard_normal(out[name].shape)
        drawn = base * np.exp(spread * noise) if base else spread * noise
        out[name] = jnp.asarray(drawn.astype(out[name].dtype))
    for name, factor in factors.items():
        out[name] = (out[name] * factor).astype(out[name].dtype)
    return out
```

```python
from contextlib import ExitStack

import numpy as np
import concourse.bass as bass
from concourse import mybir

F32 = mybir.dt.float32
BF16 = mybir.dt.bfloat16
ALU = mybir.AluOpType
ACT = mybir.ActivationFunctionType
AX = mybir.AxisListType

P = 128
D = 128
B = 2
N = 512
T = B * N
NT = T // P
HT = NT // B
C = 77
F = 512
FC = F // P
SLOTS = 64
E0 = 16
E = 8
PAIRS = E0 // 2
KEEP = 5
EPS = 1e-5
RING = 4
NEG = -3.0e38

W_PARTS = [("L0_WqT", D), ("L0_WkT", D), ("L0_WvT", D), ("L0_WpT", D), ("L0_routerT", E0),
           ("L1x_Wq", D), ("L1x_Wk", D), ("L1x_Wv", D), ("L1x_Wo", D),
           ("L1f_Wq", D), ("L1f_WqR", D), ("L1f_Wk", D), ("L1f_WkR", D), ("L1f_Wv", D), ("L1f_Wo", D),
           ("L1f_Wg", E), ("L2x_Wq", D), ("L2x_Wk", D), ("L2x_Wv", D), ("L2x_Wo", D), ("L2f_router", E + 1),
           ("L3x_wq", 1024), ("L3x_wk", 1024), ("L3x_wv", 1024), ("L3x_wout", 1024), ("L3f_router", E),
           ("pre_g", 1), ("pre_b", 1), ("L3_gamma", 1), ("L3_beta", 1),
           ("bq", 1), ("bqR", 1), ("bk", 1), ("bkR", 1),
           ("L1_b1", E * FC), ("L3_b1", E * FC), ("ctxT", B * C)]
R_PARTS = [("g_xattn", 4), ("g_ffn", 4), ("gate", 1), ("focus", 1), ("norm_weight", D), ("ln_g", D), ("ln_b", D),
           ("bv", D), ("bo", D), ("g1", D), ("be1", D), ("g2", D), ("be2", D), ("bg", E),
           ("L2_bo", D), ("L2_router_b", E + 1), ("b_out", D)]
C_PARTS = [("ident", P), ("mask16", 16), ("mask8", 8), ("mask2", 2), ("blocks", D), ("order8", 8), ("order9", 9),
           ("cos", N), ("sin", N), ("iota", SLOTS), ("diag", T), ("pairsel", PAIRS * P)]


def columns(parts):
    at, out = 0, {}
    for name, n in parts:
        out[name] = (at, n)
        at += n
    return out, at


W_AT, W_COLS = columns(W_PARTS)
R_AT, R_COLS = columns(R_PARTS)
C_AT, C_COLS = columns(C_PARTS)


def shape_constants():
    c = np.zeros((P, C_COLS), np.float32)

    def put(name, a):
        at, n = C_AT[name]
        c[0:a.shape[0], at:at + n] = a

    p = np.arange(P)
    put("ident", np.eye(P))
    put("mask16", p[:, None] // 8 == np.arange(16)[None])
    put("mask8", p[:, None] // 16 == np.arange(8)[None])
    put("mask2", p[:, None] // 64 == np.arange(2)[None])
    put("blocks", p[:, None] // 8 == p[None] // 8)
    put("order8", np.tile(7 - np.arange(8), (P, 1)))
    put("order9", np.tile(8 - np.arange(9), (P, 1)))
    inv = 1.0 / 10000.0 ** (np.arange(0, 8, 2, dtype=np.float32) / np.float32(8))
    freqs = np.arange(N, dtype=np.float32)[:, None] * inv.astype(np.float32)[None]
    emb = np.concatenate([freqs, freqs], -1).astype(np.float32)
    sign = np.where(np.arange(8) < 4, -1.0, 1.0)
    put("cos", np.tile(np.cos(emb).T, (16, 1)))
    put("sin", np.tile((np.sin(emb) * sign).T, (16, 1)))
    put("iota", np.tile(1 + np.arange(SLOTS), (P, 1)))
    slot_expert = np.arange(T) // SLOTS
    put("diag", np.tile(np.arange(E0)[:, None] == slot_expert[None], (3, 1)))
    sel = np.zeros((E0, PAIRS, P))
    for pair in range(PAIRS):
        for m in range(P):
            sel[2 * pair + m // SLOTS, pair, m] = 1
    put("pairsel", sel.reshape(E0, PAIRS * P))
    return c


def build(nc, wpack, rpack, cpack, ones_in, ctx_rows, x_in, up0, up, b_l0, b2_l1, b2_l3, scratch, out):
    with ExitStack() as ctx:
        def sb(name, shape, dt=F32):
            return ctx.enter_context(nc.sbuf_tensor(name, shape, dt))

        sems = {}

        def sem(name):
            if name not in sems:
                sems[name] = ctx.enter_context(nc.semaphore(name))
            return sems[name]

        Wt = sb("Wt", [P, W_COLS])
        Rt = sb("Rt", [P, R_COLS])
        Ct = sb("Ct", [P, C_COLS])
        CX = sb("CX", [C, B, D])
        B0 = sb("B0", [E0, F + D + 1])
        B2 = sb("B2", [E, 2, D])
        RINGW = sb("RINGW", [P, RING, 2 * F])

        X = sb("X", [P, NT, D])
        XH = sb("XH", [P, NT, D])
        HTR = sb("HTR", [P, T])
        Y = sb("Y", [P, NT, D])
        YT = sb("YT", [P, T])
        ACC = sb("ACC", [P, NT, D])
        TG = sb("TG", [P, 9])
        ST6 = sb("ST6", [P, NT, 6])
        MV = sb("MV", [P, NT, 2])
        RS = sb("RS", [P, NT, 4])
        HALFNEG = sb("HALFNEG", [P, HT])
        GL = sb("GL", [P, NT, 16])
        GM = sb("GM", [P, NT, 16])
        GR = sb("GR", [P, NT, 16])
        GC = sb("GC", [P, NT, 16])
        GS = sb("GS", [P, NT, 16])
        G1 = sb("G1", [P, NT])
        G2 = sb("G2", [P, NT])
        COMBT = sb("COMBT", [16, T])
        TMP = sb("TMP", [P, N])
        TMP2 = sb("TMP2", [P, N])
        RK = sb("RK", [P, N])
        RG = sb("RG", [P, N])
        SM = sb("SM", [P, 64])
        BIG = sb("BIG", [P, 22528])
        PS = ctx.enter_context(nc.psum_tensor("PS", [P, 8, 512], F32))

        def w(name, a=0, b=None):
            at, n = W_AT[name]
            return Wt[:, at + a:at + (n if b is None else b)]

        def r(name, rows=P):
            at, n = R_AT[name]
            return Rt[0:rows, at:at + n]

        def c(name, rows=P):
            at, n = C_AT[name]
            return Ct[0:rows, at:at + n]

        ident = c("ident")
        big_at = [0]

        def big(rows, cols, dt=F32):
            n = cols if dt == F32 else (cols + 1) // 2
            a = BIG[0:rows, big_at[0]:big_at[0] + n]
            big_at[0] += n
            assert big_at[0] <= 22528, big_at[0]
            return a if dt == F32 else a.bitcast(dt)

        big_at[0] = 0
        KF = big(C, B * D).rearrange("p (b d) -> p b d", b=B)
        KZ = big(C, B * D).rearrange("p (b d) -> p b d", b=B)
        VA = big(C, B * (D + 2)).rearrange("p (b d) -> p b d", b=B)
        KVM = big(P, B * (D + 16)).rearrange("p (b d) -> p b d", b=B)
        QF = big(P, T).rearrange("p (t d) -> p t d", t=NT)
        QT = big(P, T)
        big_at[0] = 0
        LG = big(E0, T)
        LW = big(E0, T)
        CUM = big(E0, T)
        ONESR = big(E0, T)
        M8 = big(E0, 8)
        S0 = big(P, NT * T, BF16).rearrange("p (t s) -> p t s", t=NT)
        S0T = big(P, PAIRS * T, BF16).rearrange("p (q t) -> p q t", q=PAIRS)
        XP = big(P, NT * 3 * D, BF16).rearrange("p (t i d) -> p t i d", t=NT, i=3)
        WP = big(P, NT * 48, BF16).rearrange("p (t i e) -> p t i e", t=NT, i=3)
        XET = YT
        GM48 = big(48, T)
        GSL = big(P, PAIRS)
        HS = XH[:, 0:HT, :].rearrange("p t d -> p (t d)")
        HST = XH[:, HT:NT, :].rearrange("p t d -> p (t d)")
        YP = big(P, PAIRS * 3 * D, BF16).rearrange("p (q i d) -> p q i d", q=PAIRS, i=3)
        big_at[0] = 0
        KTM = big(P, B * 16 * C).rearrange("p (b h k) -> p b h k", b=B, h=16)
        VTM = big(P, B * 16 * C).rearrange("p (b h k) -> p b h k", b=B, h=16)
        VW = big(C, B * 16 * D).rearrange("p (b h d) -> p b h d", b=B, h=16)
        SC = [big(P, 16 * C).rearrange("p (h k) -> p h k", h=16) for _ in range(2)]
        PT = big(C, 16 * P).rearrange("p (h q) -> p h q", h=16)
        QC = big(P, 1024).rearrange("p (c q) -> p c q", c=8)
        CTXN = big(P, B * C)
        big_at[0] = 0
        QS = big(75, 16 * T, BF16).rearrange("p (h t) -> p h t", h=16)
        KS = big(75, 16 * T, BF16).rearrange("p (h t) -> p h t", h=16)
        VS = big(P, NT * 16 * 32).rearrange("p (t h d) -> p t h d", t=NT, h=16)
        flat_y = Y[:, :, :].rearrange("p t d -> p (t d)")
        flat_acc = ACC[:, :, :].rearrange("p t d -> p (t d)")
        PIE = [a[:, n * 512:(n + 1) * 512].bitcast(BF16) for a in (flat_y, YT[:, :], flat_acc) for n in (0, 1)]
        PR = [a[:, n * N:(n + 1) * N] for a in (YT[:, :], flat_acc) for n in (0, 1)] + [big(P, N) for _ in range(4)]
        big_at[0] = 0
        HB = [big(P, FC * N).rearrange("p (c n) -> p c n", c=FC) for _ in range(2)]

        IDB = sb("IDB", [P, P], BF16)
        MX = sb("MX", [P, HT, 4])
        MPB = sb("MPB", [P, HT, 3, 4], BF16)
        MT = TMP2[0:12, 0:256].bitcast(BF16)

        def bc(ap, n, axis):
            a = ap.unsqueeze(axis)
            shape = list(a.shape)
            shape[axis] = n
            return a.to_broadcast(shape)

        def half(b):
            return slice(HT * b, HT * b + HT)

        def cols(b):
            return slice(N * b, N * b + N)

        def tiles(bank):
            return PS[:, bank, :].rearrange("p (t d) -> p t d", t=HT)

        def expert_ready(eng, n):
            eng.wait_ge(sem(f"expert_loaded{n % RING}"), 16 * (n // RING + 1))

        def inputs_ready(eng):
            for name in ("x_loaded", "consts_loaded", "weights_loaded"):
                eng.wait_ge(sem(name), 16)
            eng.wait_ge(sem("rows_loaded"), 16 * 5)

        class Steps:
            def __init__(self, eng, s):
                self.eng, self.s, self.n, self.told = eng, s, 0, {}

            def do(self, ins):
                ins.then_inc(self.s, 1)
                self.n += 1
                self.eng.wait_ge(self.s, self.n)

            def settle(self, name):
                self.told[name] = self.told.get(name, 0) + 1
                self.eng.wait_ge(sem(name), self.told[name])

        block = ctx.enter_context(nc.Block())

        @block.sync
        def _(sp):
            sp.dma_start(X[:, :, :], x_in).then_inc(sem("x_loaded"), 16)
            sp.dma_start(Ct[:, :], cpack).then_inc(sem("consts_loaded"), 16)
            sp.dma_start(Wt[:, :], wpack).then_inc(sem("weights_loaded"), 16)
            sp.dma_start(Rt[:, :], rpack.to_broadcast([P, R_COLS])).then_inc(sem("rows_loaded"), 16)
            sp.dma_start(CX[:, :, :], ctx_rows).then_inc(sem("rows_loaded"), 16)
            sp.dma_start(B0[:, :], b_l0).then_inc(sem("rows_loaded"), 16)
            sp.dma_start(B2[:, 0, :], b2_l1).then_inc(sem("rows_loaded"), 16)
            sp.dma_start(B2[:, 1, :], b2_l3).then_inc(sem("rows_loaded"), 16)

            def load_experts(lo, hi):
                for n in range(lo, hi):
                    if n >= RING:
                        sp.wait_ge(sem("expert_used"), n - RING + 1)
                    src = up0[n] if n < E0 else up[n - E0]
                    sp.dma_start(RINGW[:, n % RING, :], src).then_inc(sem(f"expert_loaded{n % RING}"), 16)

            load_experts(0, E0 + RING)
            sp.wait_ge(sem("qk_pieces"), 1)
            sp.dma_start(KS[72:75, :, :].rearrange("p h t -> p (h t)").bitcast(F32), ones_in).then_inc(sem("ones_stacked"), 16)
            for b in range(B):
                sp.wait_ge(sem("qk_pieces"), 2 * b + 2)
                for j in range(6):
                    sp.dma_start(scratch[j, :, cols(b)], PIE[j][:, cols(b)]).then_inc(sem(f"spilled{b}"), 16)
                sp.wait_ge(sem(f"spilled{b}"), 16 * 6)
                for i in range(3):
                    for j in range(3):
                        row = 8 * (3 * i + j)
                        for S, piece in ((QS, j), (KS, 3 + i)):
                            src = scratch[piece, :, cols(b)].rearrange("(h d) t -> d h t", d=8)
                            sp.dma_start(S[row:row + 8, :, cols(b)], src).then_inc(sem(f"stacked{b}"), 16)
            for g in range(8):
                sp.wait_ge(sem("max_rows"), g + 1)
                b, h0 = g // 4, 4 * (g % 4)
                for i in range(3):
                    for h in range(4):
                        sp.dma_start(QS[72 + i:73 + i, h0 + h, cols(b)], MT[4 * i + h:4 * i + h + 1, :])\
                            .then_inc(sem(f"max_stacked{g % 2}"), 16)
                sp.wait_ge(sem(f"max_stacked{g % 2}"), 16 * 12 * (g // 2 + 1))
            load_experts(E0 + RING, E0 + 3 * E)
            for b in range(B):
                sp.wait_ge(sem("x_final"), b + 1)
                sp.dma_start(out[:, half(b), :], X[:, half(b), :]).then_inc(sem("stored"), 16)
            sp.wait_ge(sem("stored"), 16 * B)

        @block.gpsimd
        def _(pool):
            st = Steps(pool, sem("pool_step"))
            st.do(nc.gpsimd.memset(HALFNEG[:, :], -0.5))

            def inv_root(dst, var, rows=P, n=HT):
                st.do(nc.gpsimd.tensor_scalar(dst, var, EPS, None, ALU.add))
                return nc.gpsimd.tensor_tensor(dst, dst, HALFNEG[0:rows, 0:n], ALU.pow)

            def ln(n, b, double=False):
                pool.wait_ge(sem("ln_var"), 2 * n + b + 1)
                h = half(b)
                if not double:
                    inv_root(RS[:, h, 0], MV[:, h, 1]).then_inc(sem("ln_rstd"), 1)
                    return
                st.do(inv_root(RS[:, h, 1], MV[:, h, 1]))
                st.do(nc.gpsimd.tensor_tensor(RS[:, h, 2], RS[:, h, 1], RS[:, h, 1], ALU.mult))
                st.do(nc.gpsimd.tensor_tensor(RS[:, h, 2], RS[:, h, 2], MV[:, h, 1], ALU.mult))
                st.do(inv_root(RS[:, h, 3], RS[:, h, 2]))
                nc.gpsimd.tensor_tensor(RS[:, h, 0], RS[:, h, 1], RS[:, h, 3], ALU.mult).then_inc(sem("ln_rstd"), 1)

            for b in range(B):
                ln(0, b)
            for b in range(B):
                ln(1, b, double=True)
            pool.wait_ge(sem("xn_ready"), 2)
            st.do(nc.gpsimd.tensor_copy(XP[:, :, 0, :], XH[:, :, :]))
            st.do(nc.gpsimd.tensor_tensor(ACC[:, :, :], XH[:, :, :], XP[:, :, 0, :], ALU.subtract))
            st.do(nc.gpsimd.tensor_copy(XP[:, :, 1, :], ACC[:, :, :]))
            st.do(nc.gpsimd.tensor_tensor(ACC[:, :, :], ACC[:, :, :], XP[:, :, 1, :], ALU.subtract))
            nc.gpsimd.tensor_copy(XP[:, :, 2, :], ACC[:, :, :]).then_inc(sem("xp_ready"), 1)
            for b in range(B):
                ln(2, b, True)
            pool.wait_ge(sem("ctx_var"), 1)
            inv_root(SM[0:C, 40:42], SM[0:C, 32:36].rearrange("p (b v) -> p b v", v=2)[:, :, 1], C, B)\
                .then_inc(sem("ctx_rstd"), 1)
            for n, double in ((3, False), (4, False), (5, False), (6, False), (7, False), (8, False),
                              (9, True), (10, False)):
                for b in range(B):
                    ln(n, b, double)

        @block.scalar
        def _(act):
            st = Steps(act, sem("act_step"))
            inputs_ready(act)
            nc.scalar.activation(IDB[:, :], ident, ACT.Copy).then_inc(sem("idb_ready"), 1)
            at = R_AT["g_xattn"][0]
            nc.scalar.activation(TG[:, :], Rt[:, at:at + 9], ACT.Tanh).then_inc(sem("tg_ready"), 1)

            def transposed(m, b, dst, scale=None, bias=None):
                act.wait_ge(sem("tp_done"), 2 * m + b + 1)
                if scale is None:
                    ins = nc.scalar.activation(dst[:, cols(b)], PS[:, 6 + b, :], ACT.Copy)
                else:
                    ins = nc.scalar.activation(dst[:, cols(b)], PS[:, 6 + b, :], ACT.Identity, bias=bias, scale=scale)
                ins.then_inc(sem("tr_ready"), 1)

            def focus(fi, rows, groups):
                act.wait_ge(sem("focus_abs"), fi + 1)
                nc.scalar.activation(TMP[0:rows, 0:groups * D], TMP2[0:rows, 0:groups * D], ACT.Ln,
                                     bias=SM[0:rows, 63:64]).then_inc(sem("focus_ln"), 1)
                act.wait_ge(sem("focus_max"), fi + 1)
                for g in range(groups):
                    ins = nc.scalar.activation(TMP2[0:rows, g * D:(g + 1) * D], TMP[0:rows, g * D:(g + 1) * D], ACT.Exp,
                                               bias=SM[0:rows, 8 + g:9 + g], accum_out=SM[0:rows, 16 + g:17 + g])
                ins.then_inc(sem("focus_exp"), 1)

            for b in range(B):
                transposed(0, b, HTR)
            for b in range(B):
                focus(b, C, 1)
            for b in range(B):
                focus(2 + b, P, HT)
                if b:
                    transposed(1, 0, QT)
            transposed(1, 1, QT)
            for b in range(B):
                transposed(2, b, YT)
            for b in range(B):
                transposed(3, b, HTR)
                act.wait_ge(sem("l0_logits"), b + 1)
                nc.scalar.activation(LG[:, cols(b)], PS[0:E0, b, :], ACT.Identity, bias=B0[:, F + D:F + D + 1])\
                    .then_inc(sem("l0_logits_ready"), 1)

            def router_exp(k, n):
                act.wait_ge(sem("router_shifted"), k + 1)
                nc.scalar.activation(GM[:, :, 0:n], GL[:, :, 0:n], ACT.Exp).then_inc(sem("router_exp"), 1)

            router_exp(0, E0)
            for q in range(PAIRS):
                act.wait_ge(sem("slots_turned"), q + 1)
                nc.scalar.activation(S0T[:, q, :], PS[:, 2 + q % 2, :].bitcast(BF16), ACT.Copy)\
                    .then_inc(sem("slots_turned_ready"), 1)
            for n in range(2):
                act.wait_ge(sem("gathered"), n + 1)
                nc.scalar.activation(XET[:, cols(n)], PS[:, 4 + n, :], ACT.Copy).then_inc(sem("gathered_ready"), 1)
            for q in range(PAIRS):
                act.wait_ge(sem("l0_hidden"), q + 1)
                nc.scalar.activation(HS, PS[:, q % 2, :], ACT.Gelu).then_inc(sem("l0_gelu"), 1)
                act.wait_ge(sem("l0_hidden_turned"), q + 1)
                nc.scalar.activation(HST, PS[:, 2, :], ACT.Copy).then_inc(sem("l0_hidden_ready"), 1)

            def cross(k, heads, chunks, scale):
                if k:
                    for n in range(8):
                        act.wait_ge(sem("vw_done"), 8 * (k - 2) + n + 1)
                        nc.scalar.activation(VW[:, n // 4, 4 * (n % 4):4 * (n % 4) + 4, :],
                                             PS[0:C, n % 4, :].rearrange("p (h d) -> p h d", h=4), ACT.Copy)\
                            .then_inc(sem("vw_ready"), 1)

            def cross_tiles(k, heads, chunks, scale):
                turns = heads // 4
                for t in range(NT + 1):
                    if t < NT:
                        for n in range((chunks + 3) // 4):
                            act.wait_ge(sem(f"q{k}_done"), t * ((chunks + 3) // 4) + n + 1)
                            m = min(4, chunks)
                            nc.scalar.activation(QC[:, 4 * n:4 * n + m, :],
                                                 PS[:, 6, 0:m * P].rearrange("p (c q) -> p c q", c=m),
                                                 ACT.Copy).then_inc(sem(f"q{k}_ready"), 1)
                        act.wait_ge(sem(f"s{k}_shifted"), t + 1)
                        nc.scalar.activation(SC[t % 2][:, 0:heads, :], SC[t % 2][:, 0:heads, :], ACT.Exp,
                                             scale=scale).then_inc(sem(f"s{k}_exp"), 1)
                    if t >= 1:
                        for n in range(turns):
                            i = (t - 1) * turns + n
                            act.wait_ge(sem(f"p{k}_turned"), i + 1)
                            nc.scalar.activation(PT[:, 4 * n:4 * n + 4, :],
                                                 PS[0:C, 4 + i % 2, :].rearrange("p (h q) -> p h q", h=4),
                                                 ACT.Copy).then_inc(sem(f"p{k}_ready"), 1)

            def moe(k, func, b1, second):
                router_exp(k, E + 1 if k == 2 else E)
                for i in range(2 * E):
                    g = 16 * (k - 1) + i
                    for ch in range(FC):
                        act.wait_ge(sem("moe_hidden"), 4 * g + ch + 1)
                        if g >= 2:
                            act.wait_ge(sem("moe_out"), g - 1)
                        col = b1[:, i // 2 * FC + ch:i // 2 * FC + ch + 1] if b1 is not None else 0.0
                        nc.scalar.activation(HB[g % 2][:, ch, :], PS[:, ch, :], func, bias=col)\
                            .then_inc(sem("moe_gelu"), 1)
                    if i == 7 and second is not None:
                        for b in range(B):
                            act.wait_ge(sem("comb_turned"), 2 * second + b + 1)
                            nc.scalar.activation(COMBT[0:E, cols(b)], PS[0:E, 6 + b, :], ACT.Copy)\
                                .then_inc(sem("combt_ready"), 1)

            act.wait_ge(sem("ctx_turned"), 1)
            nc.scalar.activation(CTXN[:, :], PS[:, 5, 0:B * C], ACT.Identity, bias=w("pre_b"), scale=w("pre_g"))\
                .then_inc(sem("ctxn_ready"), 1)
            for b in range(B):
                transposed(4, b, HTR, w("pre_g"), w("pre_b"))
            cross_tiles(1, 8, 1, 1.0 / np.sqrt(128.0))
            for b in range(B):
                transposed(5, b, YT)
            for b in range(B):
                act.wait_ge(sem("l1_wo"), b + 1)
                nc.scalar.activation(ACC[:, half(b), :], tiles(b), ACT.Gelu).then_inc(sem("l1_wo_gelu"), 1)
            for b in range(B):
                transposed(6, b, HTR)
            for idx in range(8 * 16):
                act.wait_ge(sem("scores"), idx + 1)
                if idx >= 8:
                    act.wait_ge(sem("pv_done"), (idx - 8) // 4 + 1)
                nc.scalar.activation(PR[idx % 8], PS[:, 4 + idx % 2, :], ACT.Exp, scale=1.0 / np.sqrt(8.0))\
                    .then_inc(sem("probs"), 1)
            for b in range(B):
                transposed(7, b, YT)
            for b in range(B):
                transposed(8, b, HTR)
            moe(1, ACT.Gelu, w("L1_b1"), 0)
            cross(2, 16, 1, None)
            for b in range(B):
                transposed(9, b, HTR)
            cross_tiles(2, 16, 1, 1.0 / np.sqrt(8.0))
            for b in range(B):
                transposed(10, b, HTR)
            moe(2, ACT.Gelu, None, None)
            cross(3, 16, 8, None)
            for b in range(B):
                transposed(11, b, HTR, w("L3_gamma"), w("L3_beta"))
            cross_tiles(3, 16, 8, 64.0 ** -0.5)
            for b in range(B):
                transposed(12, b, HTR)
            moe(3, ACT.Gelu_apprx_tanh, w("L3_b1"), 1)

        @block.vector
        def _(dve):
            v = nc.vector
            st = Steps(dve, sem("dve_step"))
            inputs_ready(dve)
            st.do(v.memset(SM[:, 63:64], 1e-6))

            def ln(n, b, src):
                h = range(HT * b, HT * b + HT)
                for t in h:
                    ins = v.bn_stats(ST6[:, t, :], src[:, t, :])
                st.do(ins)
                for t in h:
                    ins = v.bn_aggr(MV[:, t, :], ST6[:, t, :])
                ins.then_inc(sem("ln_var"), 1)
                st.settle("ln_var")
                dve.wait_ge(sem("ln_rstd"), 2 * n + b + 1)
                dve.wait_ge(sem("ln_var"), 2 * n + b + 1)
                for t in h:
                    ins = v.tensor_scalar(XH[:, t, :], src[:, t, :], MV[:, t, 0:1], RS[:, t, 0:1],
                                          ALU.subtract, ALU.mult)
                return ins

            def gain(b, name, name2):
                st.do(v.tensor_tensor(XH[:, half(b), :], XH[:, half(b), :], bc(r(name), HT, 1), ALU.mult))
                return v.tensor_tensor(XH[:, half(b), :], XH[:, half(b), :], bc(r(name2), HT, 1), ALU.add)

            def keep_largest(dst, val, rows, groups, n, order, keep):
                R = RK[0:rows, 0:groups * n].rearrange("p (g i) -> p g i", i=n)
                G = RG[0:rows, 0:groups * n].rearrange("p (g i) -> p g i", i=n)
                st.do(v.tensor_copy(R, bc(order, groups, 1)))
                for s in range(1, n):
                    st.do(v.tensor_tensor(G[:, :, 0:n - s], val[:, :, 0:n - s], val[:, :, s:n], ALU.is_ge))
                    st.do(v.tensor_tensor(R[:, :, s:n], R[:, :, s:n], G[:, :, 0:n - s], ALU.add))
                    st.do(v.tensor_tensor(R[:, :, 0:n - s], R[:, :, 0:n - s], G[:, :, 0:n - s], ALU.subtract))
                return v.scalar_tensor_tensor(out=dst, in0=R, scalar=keep - 0.5, in1=val, op0=ALU.is_lt, op1=ALU.mult)

            def split3(dsts, src, left):
                st.do(v.tensor_copy(dsts[0], src))
                st.do(v.tensor_tensor(left, src, dsts[0], ALU.subtract))
                st.do(v.tensor_copy(dsts[1], left))
                st.do(v.tensor_tensor(left, left, dsts[1], ALU.subtract))
                return v.tensor_copy(dsts[2], left)

            def add_to_x(b, src, gate):
                st.do(v.scalar_tensor_tensor(out=X[:, half(b), :], in0=src, scalar=TG[:, gate:gate + 1],
                                             in1=X[:, half(b), :], op0=ALU.mult, op1=ALU.add))

            for b in range(B):
                ln(0, b, X).then_inc(sem("xh0"), 1)
                st.settle("xh0")

            def focus(fi, src, dst, rows, groups):
                n = groups * D
                t1 = TMP[0:rows, 0:n].rearrange("p (g d) -> p g d", d=D)
                t2 = TMP2[0:rows, 0:n].rearrange("p (g d) -> p g d", d=D)
                sm = SM[0:rows, :]
                st.do(v.tensor_scalar(t1, src, -0.01, None, ALU.mult))
                v.tensor_tensor(t2, src, t1, ALU.max).then_inc(sem("focus_abs"), 1)
                st.settle("focus_abs")
                dve.wait_ge(sem("focus_abs"), fi + 1)
                st.do(v.tensor_reduce(sm[:, 0:groups], t2, AX.X, ALU.add))
                dve.wait_ge(sem("focus_ln"), fi + 1)
                st.do(v.tensor_scalar(t1, t1, r("focus", rows), None, ALU.mult))
                v.tensor_reduce(sm[:, 8:8 + groups], t1, AX.X, ALU.max, negate=True).then_inc(sem("focus_max"), 1)
                st.settle("focus_max")
                dve.wait_ge(sem("focus_exp"), fi + 1)
                st.do(v.reciprocal(sm[:, 16:16 + groups], sm[:, 16:16 + groups]))
                st.do(v.tensor_scalar(sm[:, 0:groups], sm[:, 0:groups], 1.0 / D, 1e-6, ALU.mult, ALU.add))
                st.do(v.tensor_tensor(sm[:, 0:groups], sm[:, 0:groups], sm[:, 16:16 + groups], ALU.mult))
                for g in range(groups):
                    ins = v.tensor_scalar(t2[:, g, :], t2[:, g, :], sm[:, g:g + 1], None, ALU.mult)
                st.do(ins)
                flat = t2.rearrange("p g (h i) -> p (g h) i", i=8)
                return keep_largest(dst, flat, rows, groups * 16, 8, c("order8", rows), KEEP)

            for b in range(B):
                dve.wait_ge(sem("l0_kv"), b + 1)
                st.do(v.tensor_copy(VA[:, b, 0:D], PS[0:C, b, D:2 * D]))
                st.do(v.memset(VA[:, b, D:D + 1], 1.0))
                focus(b, PS[0:C, b, 0:D].rearrange("p (g d) -> p g d", g=1), 
                      KF[:, b, :].rearrange("p (h i) -> p h i", i=8), C, 1).then_inc(sem("l0_k_ready"), 1)
                st.settle("l0_k_ready")
            for b in range(B):
                dve.wait_ge(sem("l0_sums"), b + 1)
                st.do(v.scalar_tensor_tensor(out=KVM[:, b, 0:D], in0=PS[:, 2 + b, 0:D], scalar=1.0 / N,
                                             in1=c("blocks"), op0=ALU.mult, op1=ALU.mult))
                st.do(v.tensor_scalar(SM[:, 24:25], PS[:, 2 + b, D:D + 1], 1.0 / C, None, ALU.mult))
                v.tensor_scalar(KVM[:, b, D:D + 16], c("mask16"), SM[:, 24:25], None, ALU.mult)\
                    .then_inc(sem("l0_state_ready"), 1)
                st.settle("l0_state_ready")
            for b in range(B):
                dve.wait_ge(sem("l0_q"), b + 1)
                focus(2 + b, tiles(4 + b), QF[:, half(b), :].rearrange("p t (h i) -> p (t h) i", i=8), P, HT)\
                    .then_inc(sem("qf_ready"), 1)
                st.settle("qf_ready")
            for b in range(B):
                dve.wait_ge(sem("l0_y"), b + 1)
                y = PS[:, 2 * b:2 * b + 2, :].rearrange("p k (j n) -> p (k j) n", n=256)
                z = RG[:, 0:64].rearrange("p (t h) -> p t h", t=HT)
                st.do(v.tensor_scalar(z, y[:, :, D:D + 16], 1e-6, None, ALU.add))
                st.do(v.reciprocal(z, z))
                v.tensor_tensor(Y[:, half(b), :].rearrange("p t (h i) -> p t h i", i=8),
                                y[:, :, 0:D].rearrange("p t (h i) -> p t h i", i=8), bc(z, 8, 3), ALU.mult)\
                    .then_inc(sem("y_ready"), 1)
                st.settle("y_ready")
            dve.wait_ge(sem("tg_ready"), 1)
            for b in range(B):
                dve.wait_ge(sem("l0_o"), b + 1)
                add_to_x(b, tiles(4 + b), 0)
                st.do(ln(1, b, X))
                v.tensor_tensor(XH[:, half(b), :], XH[:, half(b), :], bc(r("norm_weight"), HT, 1), ALU.mult)\
                    .then_inc(sem("xn_ready"), 1)
                st.settle("xn_ready")

            def router(k, n, src, bias):
                gl = GL[:, :, 0:n]
                if bias is None:
                    st.do(v.tensor_copy(gl, src))
                else:
                    st.do(v.tensor_tensor(gl, src, bc(bias, NT, 1), ALU.add))
                st.do(v.tensor_reduce(G1[:, :], gl, AX.X, ALU.max))
                v.tensor_tensor(gl, gl, bc(G1[:, :], n, 2), ALU.subtract).then_inc(sem("router_shifted"), 1)
                st.settle("router_shifted")
                dve.wait_ge(sem("router_exp"), k + 1)
                st.do(v.tensor_reduce(G1[:, :], GM[:, :, 0:n], AX.X, ALU.add))
                st.do(v.reciprocal(G1[:, :], G1[:, :]))
                st.do(v.tensor_tensor(GR[:, :, 0:n], GM[:, :, 0:n], bc(G1[:, :], n, 2), ALU.mult))

            st.do(v.memset(ONESR[:, :], 1.0))
            dve.wait_ge(sem("l0_logits_ready"), 2)
            src = LG
            for n in range(SLOTS // 8):
                st.do(v.max(M8[:, :], src))
                st.do(v.match_replace(LW, M8[:, :], src, NEG))
                src = LW
            st.do(v.tensor_tensor(LW, LW, LG, ALU.not_equal))
            st.do(v.tensor_tensor_scan(CUM, ONESR, LW, 0.0, ALU.mult, ALU.add))
            v.tensor_tensor(CUM, CUM, LW, ALU.mult).then_inc(sem("places_ready"), 1)
            st.settle("places_ready")
            dve.wait_ge(sem("l0_logits_turned"), 1)
            router(0, E0, PS[:, 2, 0:NT * E0].rearrange("p (t e) -> p t e", t=NT), None)
            dve.wait_ge(sem("places_turned"), 1)
            places = PS[:, 3, 0:NT * E0].rearrange("p (t e) -> p t e", t=NT)
            st.do(v.tensor_copy(GC[:, :, :], places))
            for t in range(NT):
                v.tensor_tensor(S0[:, t, :].rearrange("p (e s) -> p e s", e=E0), bc(c("iota"), E0, 1),
                                bc(GC[:, t, :], SLOTS, 2), ALU.is_equal).then_inc(sem("slots_ready"), 1)
                st.settle("slots_ready")
            st.do(v.scalar_tensor_tensor(out=GS[:, :, :], in0=GC[:, :, :], scalar=0.0, in1=GR[:, :, :], op0=ALU.is_gt, op1=ALU.mult))
            st.do(v.tensor_reduce(G2[:, :], GS[:, :, :], AX.X, ALU.add))
            st.do(v.tensor_scalar(G2[:, :], G2[:, :], 1e-37, None, ALU.max))
            st.do(v.reciprocal(G2[:, :], G2[:, :]))
            st.do(v.tensor_tensor(GS[:, :, :], GS[:, :, :], bc(G2[:, :], E0, 2), ALU.mult))
            split3([WP[:, :, i, :] for i in range(3)], GS[:, :, :], GM[:, :, :]).then_inc(sem("shares_ready"), 1)
            st.settle("shares_ready")
            for n in range(2):
                dve.wait_ge(sem("shares_gathered"), n + 1)
                v.tensor_tensor(GM48[:, cols(n)], PS[0:48, n, :], c("diag", 48)[:, cols(n)], ALU.mult)\
                    .then_inc(sem("shares_own"), 1)
                st.settle("shares_own")
            dve.wait_ge(sem("shares_turned"), 1)
            st.do(v.tensor_copy(GSL[:, :], PS[:, 7, 0:PAIRS]))
            for q in range(PAIRS):
                dve.wait_ge(sem("expert_used"), 2 * q + 2)
                st.do(v.tensor_scalar(TMP[:, 0:D], PS[:, 3, 0:D], GSL[:, q:q + 1], None, ALU.mult))
                split3([YP[:, q, i, :] for i in range(3)], TMP[:, 0:D], TMP2[:, 0:D]).then_inc(sem("yp_ready"), 1)
                st.settle("yp_ready")
            for b in range(B):
                dve.wait_ge(sem("scattered"), b + 1)
                add_to_x(b, tiles(4 + b), 4)
                ln(2, b, X).then_inc(sem("xh2"), 1)
                st.settle("xh2")

            def mask_heads(dst, k, src, heads, chunks, ch):
                for b in range(B):
                    if chunks == 1:
                        hs, m = slice(0, heads), c("mask16" if heads == 16 else "mask8")
                    else:
                        hs, m = slice(2 * ch, 2 * ch + 2), c("mask2")
                    n = hs.stop - hs.start
                    ins = v.tensor_tensor(dst[:, b, hs, :], bc(src[:, b, :], n, 1), bc(m, C, 2), ALU.mult)
                return ins

            def cross_setup(k, heads, chunks):
                for ch in range(chunks):
                    for dst in ((KTM,) if k == 1 else (KTM, VTM)):
                        i = ch * 2 + (dst is VTM)
                        dve.wait_ge(sem(f"kv{k}_done"), i + 1)
                        src = PS[:, 4 + i % 2, 0:B * C].rearrange("p (b k) -> p b k", b=B)
                        mask_heads(dst, k, src, heads, chunks, ch).then_inc(sem(f"kv{k}_ready"), 1)
                        st.settle(f"kv{k}_ready")

            def cross_tiles(k, heads, scale, tail):
                turns = heads // 4
                for t in range(NT + 2):
                    if t < NT:
                        s = SC[t % 2][:, 0:heads, :]
                        dve.wait_ge(sem(f"s{k}_done"), t + 1)
                        raw = PS[:, 0:turns, 0:4 * C].rearrange("p n (h k) -> p n h k", k=C)
                        top = SM[:, 0:heads].rearrange("p (n h) -> p n h", h=4)
                        if t >= 2:
                            dve.wait_ge(sem(f"p{k}_turned"), turns * (t - 1))
                        if k == 1:
                            lim = 10000.0 * float(np.sqrt(128.0))
                            s4 = s.rearrange("p (n h) k -> p n h k", h=4)
                            st.do(v.tensor_scalar(s4, raw, lim, -lim, ALU.min, ALU.max))
                            st.do(v.tensor_reduce(top, s4, AX.X, ALU.max))
                            v.tensor_tensor(s, s, bc(SM[:, 0:heads], C, 2), ALU.subtract).then_inc(sem(f"s{k}_shifted"), 1)
                            st.settle(f"s{k}_shifted")
                        else:
                            st.do(v.tensor_reduce(top, raw, AX.X, ALU.max))
                            v.tensor_tensor(s.rearrange("p (n h) k -> p n h k", h=4), raw, bc(top, C, 3), ALU.subtract)\
                                .then_inc(sem(f"s{k}_shifted"), 1)
                            st.settle(f"s{k}_shifted")
                    if 1 <= t <= NT:
                        s = SC[(t - 1) % 2][:, 0:heads, :]
                        dve.wait_ge(sem(f"s{k}_exp"), t)
                        st.do(v.tensor_reduce(SM[:, 24:24 + heads], s, AX.X, ALU.add))
                        st.do(v.reciprocal(SM[:, 24:24 + heads], SM[:, 24:24 + heads]))
                        v.tensor_tensor(s, s, bc(SM[:, 24:24 + heads], C, 2), ALU.mult).then_inc(sem(f"p{k}_normed"), 1)
                        st.settle(f"p{k}_normed")
                    if t >= 2:
                        dve.wait_ge(sem(f"o{k}_done"), t - 1)
                        tail(t - 2, PS[:, 7, (t % 2) * D:(t % 2) * D + D])

            def top2(k, n):
                sem_in = sem("router_done")
                dve.wait_ge(sem_in, k)
                src = PS[:, 4, 0:NT * 16].rearrange("p (t e) -> p t e", t=NT)[:, :, 0:n]
                router(k, n, src, {1: r("bg"), 2: r("L2_router_b"), 3: None}[k])
                st.do(keep_largest(GC[:, :, 0:n], GR[:, :, 0:n], P, NT, n, c("order9" if n == 9 else "order8"), 2))
                if k == 1:
                    st.do(v.tensor_reduce(G1[:, :], GC[:, :, 0:n], AX.X, ALU.add))
                    st.do(v.reciprocal(G1[:, :], G1[:, :]))
                    st.do(v.tensor_tensor(GC[:, :, 0:n], GC[:, :, 0:n], bc(G1[:, :], n, 2), ALU.mult))
                if k == 1:
                    ins = v.tensor_copy(ACC[:, :, :], XH[:, :, :])
                elif k == 2:
                    ins = v.tensor_tensor(ACC[:, :, :], XH[:, :, :], bc(GC[:, :, E], D, 2), ALU.mult)
                else:
                    ins = v.memset(ACC[:, :, :], 0.0)
                ins.then_inc(sem("comb_ready"), 1)
                st.settle("comb_ready")
                dve.wait_ge(sem("comb_ready"), k)

            def moe(k, second):
                top2(k, E + 1 if k == 2 else E)
                for i in range(2 * E):
                    g = 16 * (k - 1) + i
                    e, b = i // 2, i % 2
                    dve.wait_ge(sem("moe_out"), g + 1)
                    if i >= 2:
                        dve.wait_ge(sem("moe_summed"), g - 1)
                    for j in range(HT):
                        t = HT * b + j
                        ins = v.scalar_tensor_tensor(out=ACC[:, t, :], in0=PS[:, 4 + g % 2, j * D:(j + 1) * D],
                                                     scalar=GC[:, t, e:e + 1], in1=ACC[:, t, :], op0=ALU.mult, op1=ALU.add)
                    ins.then_inc(sem("moe_summed"), 1)
                    st.settle("moe_summed")
                    if i == 7 and second is not None:
                        for b2 in range(B):
                            dve.wait_ge(sem("moe_bias"), 2 * second + b2 + 1)
                            dve.wait_ge(sem("moe_summed"), g + 1)
                            st.do(v.tensor_tensor(ACC[:, half(b2), :], tiles(6 + b2), ACC[:, half(b2), :], ALU.add))
                dve.wait_ge(sem("moe_summed"), 16 * k)

            for b in range(B):
                st.do(v.bn_stats(ST6[0:C, b, :], CX[:, b, :]))
                ins = v.bn_aggr(SM[0:C, 32 + 2 * b:34 + 2 * b], ST6[0:C, b, :])
            ins.then_inc(sem("ctx_var"), 1)
            st.settle("ctx_var")
            dve.wait_ge(sem("ctx_var"), 1)
            dve.wait_ge(sem("ctx_rstd"), 1)
            for b in range(B):
                ins = v.tensor_scalar(TMP[0:C, b * D:(b + 1) * D], CX[:, b, :], SM[0:C, 32 + 2 * b:33 + 2 * b],
                                      SM[0:C, 40 + b:41 + b], ALU.subtract, ALU.mult)
            ins.then_inc(sem("ctx_normed"), 1)
            st.settle("ctx_normed")
            for b in range(B):
                st.do(v.memset(VW[:, b, 0:8, :], 0.0))
                dve.wait_ge(sem("v1_done"), b + 1)
                for h in range(8):
                    ins = v.tensor_copy(VW[:, b, h, 16 * h:16 * h + 16], PS[0:C, b, 16 * h:16 * h + 16])
                ins.then_inc(sem("v1_ready"), 1)
                st.settle("v1_ready")
            cross_setup(1, 8, 1)

            def keep_o(t, o):
                v.tensor_copy(Y[:, t, :], o).then_inc(sem("o1_read"), 1)
                st.settle("o1_read")

            cross_tiles(1, 8, None, keep_o)
            for b in range(B):
                st.do(ln(3, b, Y))
                gain(b, "ln_g", "ln_b").then_inc(sem("xh3"), 1)
                st.settle("xh3")
            dve.wait_ge(sem("xh3"), 2)
            for b in range(B):
                dve.wait_ge(sem("l1_wo_gelu"), b + 1)
                st.do(v.tensor_tensor(Y[:, half(b), :], ACC[:, half(b), :], XH[:, half(b), :], ALU.add))
                add_to_x(b, Y[:, half(b), :], 1)
            for b in range(B):
                ln(4, b, X).then_inc(sem("xh4"), 1)
                st.settle("xh4")
            st.do(v.memset(VS[:, :, :, :], 0.0))
            st.do(v.memset(VS[:, :, :, 8:9], 1.0))
            for b in range(B):
                dve.wait_ge(sem("qk_done"), b + 1)
                for which in range(2):
                    n = 2 * which
                    names = (("bq", "bqR"), ("bk", "bkR"))[which]
                    st.do(v.scalar_tensor_tensor(out=TMP[:, :], in0=PS[:, n, :], scalar=w(names[0]), in1=c("cos"),
                                                 op0=ALU.add, op1=ALU.mult))
                    st.do(v.scalar_tensor_tensor(out=TMP2[:, :], in0=PS[:, n + 1, :], scalar=w(names[1]), in1=c("sin"),
                                                 op0=ALU.add, op1=ALU.mult))
                    st.do(v.tensor_tensor(TMP[:, :], TMP[:, :], TMP2[:, :], ALU.add))
                    split3([PIE[3 * which + i][:, cols(b)] for i in range(3)], TMP[:, :], TMP2[:, :])\
                        .then_inc(sem("qk_pieces"), 1)
                    st.settle("qk_pieces")
                    dve.wait_ge(sem("qk_pieces"), 2 * b + which + 1)
                dve.wait_ge(sem("v_done"), b + 1)
                v.tensor_tensor(VS[:, half(b), :, 0:8], PS[:, 4 + b, :].rearrange("p (t h i) -> p t h i", t=HT, i=8),
                                bc(r("bv"), HT, 1).rearrange("p t (h i) -> p t h i", i=8), ALU.add).then_inc(sem("v_ready"), 1)
                st.settle("v_ready")

            def maxima(g):
                for j in range(4):
                    for u in range(2):
                        i = 8 * g + 2 * j + u
                        dve.wait_ge(sem("max_scores"), i + 1)
                        v.tensor_reduce(MX[:, 2 * u:2 * u + 2, j], PS[:, 2 * (i % 2):2 * (i % 2) + 2, :], AX.X, ALU.max,
                                        negate=True).then_inc(sem("max_done"), 1)
                        st.settle("max_done")
                dve.wait_ge(sem("max_done"), 8 * g + 8)
                left = SM[:, 0:16].rearrange("p (t h) -> p t h", t=HT)
                split3([MPB[:, :, i, :] for i in range(3)], MX[:, :, :], left).then_inc(sem("max_pieces"), 1)
                st.settle("max_pieces")

            def max_rows(g):
                dve.wait_ge(sem("max_turned"), g + 1)
                if g:
                    b = g - 1
                    dve.wait_ge(sem(f"max_stacked{b % 2}"), 16 * 12 * (b // 2 + 1))
                v.tensor_copy(MT, PS[0:12, 7, 0:256].bitcast(BF16)).then_inc(sem("max_rows"), 1)
                st.settle("max_rows")

            def heads_out(g):
                b, g4 = g // 4, g % 4
                dve.wait_ge(sem("pv_done"), 4 * g + 4)
                v.tensor_copy(TMP[:, :], PS[:, 6, :]).then_inc(sem("heads_copied"), 1)
                st.settle("heads_copied")
                dve.wait_ge(sem("heads_turned"), g + 1)
                o = PS[:, 7, :].rearrange("p (t j r) -> p t j r", t=HT, r=32)
                rec = SM[:, 16:32].rearrange("p (t h) -> p t h", t=HT)
                st.do(v.reciprocal(rec, o[:, :, :, 8]))
                v.tensor_tensor(Y[:, half(b), 32 * g4:32 * g4 + 32].rearrange("p t (j i) -> p t j i", i=8),
                                o[:, :, :, 0:8], bc(rec, 8, 3), ALU.mult).then_inc(sem("heads_ready"), 1)
                st.settle("heads_ready")

            maxima(0)
            max_rows(0)
            for g in range(8):
                if g == 0:
                    for b in range(B):
                        dve.wait_ge(sem(f"spilled{b}"), 16 * 6)
                if g < 7:
                    maxima(g + 1)
                    max_rows(g + 1)
                heads_out(g)
            for b in range(B):
                dve.wait_ge(sem("l1f_o"), b + 1)
                st.do(v.tensor_tensor(TMP[:, :].rearrange("p (t d) -> p t d", t=HT), tiles(b), bc(r("bo"), HT, 1), ALU.add))
                st.do(v.tensor_tensor(Y[:, half(b), :], TMP[:, :].rearrange("p (t d) -> p t d", t=HT), XH[:, half(b), :], ALU.add))
                st.do(ln(5, b, Y))
                gain(b, "g1", "be1").then_inc(sem("xh5"), 1)
                st.settle("xh5")
            dve.wait_ge(sem("xh5"), 2)
            moe(1, 0)
            for b in range(B):
                st.do(ln(6, b, ACC))
                st.do(gain(b, "g2", "be2"))
                add_to_x(b, XH[:, half(b), :], 5)
            for b in range(B):
                ln(7, b, X).then_inc(sem("xh7"), 1)
                st.settle("xh7")
            cross_setup(2, 16, 1)

            def tail2(t, o):
                v.tensor_tensor(TMP[:, 0:D], o, r("L2_bo"), ALU.add).then_inc(sem("o2_read"), 1)
                st.settle("o2_read")
                st.do(v.scalar_tensor_tensor(out=X[:, t, :], in0=TMP[:, 0:D], scalar=TG[:, 2:3], in1=X[:, t, :],
                                             op0=ALU.mult, op1=ALU.add))

            cross_tiles(2, 16, None, tail2)
            for b in range(B):
                ln(8, b, X).then_inc(sem("xh8"), 1)
                st.settle("xh8")
            dve.wait_ge(sem("xh8"), 2)
            moe(2, None)
            for b in range(B):
                add_to_x(b, ACC[:, half(b), :], 6)
                ln(9, b, X).then_inc(sem("xh9"), 1)
                st.settle("xh9")
            cross_setup(3, 16, 8)

            def tail3(t, o):
                v.tensor_tensor(TMP[:, 0:D], o, r("b_out"), ALU.add).then_inc(sem("o3_read"), 1)
                st.settle("o3_read")
                st.do(v.tensor_scalar(TMP[:, 0:D], TMP[:, 0:D], TG[:, 8:9], None, ALU.mult))
                st.do(v.scalar_tensor_tensor(out=X[:, t, :], in0=TMP[:, 0:D], scalar=TG[:, 3:4], in1=X[:, t, :],
                                             op0=ALU.mult, op1=ALU.add))

            cross_tiles(3, 16, None, tail3)
            for b in range(B):
                ln(10, b, X).then_inc(sem("xh10"), 1)
                st.settle("xh10")
            moe(3, 1)
            for b in range(B):
                v.scalar_tensor_tensor(out=X[:, half(b), :], in0=ACC[:, half(b), :], scalar=TG[:, 7:8],
                                       in1=X[:, half(b), :], op0=ALU.mult, op1=ALU.add).then_inc(sem("x_final"), 1)
                st.settle("x_final")

        @block.tensor
        def _(pe):
            mm, tp = nc.tensor.matmul, nc.tensor.transpose
            inputs_ready(pe)

            def turn(m, b, src, ready, value):
                pe.wait_ge(sem(ready), value)
                for j in range(HT):
                    ins = tp(PS[:, 6 + b, j * P:(j + 1) * P], src[:, HT * b + j, :], ident)
                ins.then_inc(sem("tp_done"), 1)

            def turned(m, b):
                pe.wait_ge(sem("tr_ready"), 2 * m + b + 1)

            def tile_of(a, b, j):
                return a[:, (HT * b + j) * P:(HT * b + j + 1) * P]

            for b in range(B):
                ct = w("ctxT")[:, b * C:(b + 1) * C]
                mm(PS[0:C, b, 0:D], ct, w("L0_WkT"), start=True, stop=True)
                mm(PS[0:C, b, D:2 * D], ct, w("L0_WvT"), start=True, stop=True).then_inc(sem("l0_kv"), 1)
            for b in range(B):
                turn(0, b, XH, "xh0", b + 1)
            for b in range(B):
                turned(0, b)
                for j in range(HT):
                    ins = mm(PS[:, 4 + b, j * P:(j + 1) * P], tile_of(HTR, b, j), w("L0_WqT"), start=True, stop=True)
                ins.then_inc(sem("l0_q"), 1)
            for b in range(B):
                pe.wait_ge(sem("l0_k_ready"), b + 1)
                mm(PS[:, 2 + b, 0:D + 1], KF[:, b, :], VA[:, b, 0:D + 1], start=True, stop=True).then_inc(sem("l0_sums"), 1)
            for b in range(B):
                turn(1, b, QF, "qf_ready", b + 1)
            for b in range(B):
                turned(1, b)
                pe.wait_ge(sem("l0_state_ready"), 2)
                for j in range(HT):
                    ins = mm(PS[:, 2 * b + j // 2, (j % 2) * 256:(j % 2) * 256 + D + 16], tile_of(QT, b, j), KVM[:, b, :],
                             start=True, stop=True)
                ins.then_inc(sem("l0_y"), 1)
            for b in range(B):
                turn(2, b, Y, "y_ready", b + 1)
            for b in range(B):
                turned(2, b)
                for j in range(HT):
                    ins = mm(PS[:, 4 + b, j * P:(j + 1) * P], tile_of(YT, b, j), w("L0_WpT"), start=True, stop=True)
                ins.then_inc(sem("l0_o"), 1)
            for b in range(B):
                turn(3, b, XH, "xn_ready", b + 1)
            for b in range(B):
                turned(3, b)
                mm(PS[0:E0, b, :], w("L0_routerT"), HTR[:, cols(b)], start=True, stop=True).then_inc(sem("l0_logits"), 1)
            pe.wait_ge(sem("l0_logits_ready"), 2)
            for t in range(NT):
                ins = tp(PS[:, 2, t * E0:(t + 1) * E0], LG[:, t * P:(t + 1) * P], ident[0:E0, 0:E0])
            ins.then_inc(sem("l0_logits_turned"), 1)
            pe.wait_ge(sem("places_ready"), 1)
            for t in range(NT):
                ins = tp(PS[:, 3, t * E0:(t + 1) * E0], CUM[:, t * P:(t + 1) * P], ident[0:E0, 0:E0])
            ins.then_inc(sem("places_turned"), 1)
            pe.wait_ge(sem("xp_ready"), 1)
            for n in range(2):
                for t in range(NT):
                    pe.wait_ge(sem("slots_ready"), t + 1)
                    for i in range(3):
                        ins = mm(PS[:, 4 + n, :], XP[:, t, i, :], S0[:, t, cols(n)], start=(t == 0 and i == 0),
                                 stop=(t == NT - 1 and i == 2))
                ins.then_inc(sem("gathered"), 1)
            pe.wait_ge(sem("shares_ready"), 1)
            for n in range(2):
                for t in range(NT):
                    ins = mm(PS[0:48, n, :], WP[:, t, :, :].rearrange("p i e -> p (i e)"), S0[:, t, cols(n)],
                             start=(t == 0), stop=(t == NT - 1))
                ins.then_inc(sem("shares_gathered"), 1)
            pe.wait_ge(sem("idb_ready"), 1)
            for q in range(PAIRS):
                if q >= 2:
                    pe.wait_ge(sem("slots_turned_ready"), q - 1)
                for t in range(NT):
                    ins = tp(PS[:, 2 + q % 2, :].bitcast(BF16)[:, t * P:(t + 1) * P], S0[:, t, q * P:(q + 1) * P], IDB[:, :])
                ins.then_inc(sem("slots_turned"), 1)
            pe.wait_ge(sem("shares_own"), 2)
            for q in range(PAIRS):
                ins = mm(PS[:, 7, q:q + 1], GM48[:, q * P:(q + 1) * P], c("iota", 48)[:, 0:1], start=True, stop=True)
            ins.then_inc(sem("shares_turned"), 1)
            pe.wait_ge(sem("slots_turned_ready"), PAIRS)
            pe.wait_ge(sem("gathered_ready"), 2)

            def hidden0(q):
                sel = c("pairsel", E0)[:, q * P:(q + 1) * P]
                for j in range(2):
                    mm(PS[64 * j:64 * j + 64, q % 2, :], sel[:, 64 * j:64 * j + 64], B0[:, 0:F], start=True, stop=False)
                for j in range(2):
                    n = 2 * q + j
                    expert_ready(pe, n)
                    ins = mm(PS[64 * j:64 * j + 64, q % 2, :], XET[:, n * SLOTS:(n + 1) * SLOTS],
                             RINGW[:, n % RING, 0:F], start=False, stop=True)
                ins.then_inc(sem("l0_hidden"), 1)

            hidden0(0)
            for q in range(PAIRS):
                pe.wait_ge(sem("l0_gelu"), q + 1)
                for ch in range(FC):
                    ins = tp(PS[:, 2, ch * P:(ch + 1) * P], HS[:, ch * P:(ch + 1) * P], ident)
                ins.then_inc(sem("l0_hidden_turned"), 1)
                if q + 1 < PAIRS:
                    hidden0(q + 1)
                pe.wait_ge(sem("l0_hidden_ready"), q + 1)
                if q:
                    pe.wait_ge(sem("yp_ready"), q)
                sel = c("pairsel", E0)[:, q * P:(q + 1) * P]
                for j in range(2):
                    mm(PS[64 * j:64 * j + 64, 3, 0:D], sel[:, 64 * j:64 * j + 64], B0[:, F:F + D], start=True, stop=False)
                for ch in range(FC):
                    for j in range(2):
                        n = 2 * q + j
                        ins = mm(PS[64 * j:64 * j + 64, 3, 0:D], HST[:, ch * P + 64 * j:ch * P + 64 * j + 64],
                                 RINGW[:, n % RING, F + ch * D:F + (ch + 1) * D], start=False, stop=(ch == FC - 1))
                ins.then_inc(sem("expert_used"), 2)
            pe.wait_ge(sem("yp_ready"), PAIRS)
            for t in range(NT):
                for q in range(PAIRS):
                    for i in range(3):
                        ins = mm(PS[:, 4 + t // HT, (t % HT) * D:(t % HT + 1) * D], S0T[:, q, t * P:(t + 1) * P],
                                 YP[:, q, i, :], start=(q == 0 and i == 0), stop=(q == PAIRS - 1 and i == 2))
                if t % HT == HT - 1:
                    ins.then_inc(sem("scattered"), 1)

            def cross_setup(k, chunks, wk, wv, wo, keys):
                values = w("ctxT")
                for ch in range(chunks):
                    i = 2 * ch
                    if ch >= 1:
                        pe.wait_ge(sem(f"kv{k}_ready"), i - 1)
                    mm(PS[:, 4, 0:B * C], wk[:, ch * D:(ch + 1) * D], keys, start=True, stop=True).then_inc(sem(f"kv{k}_done"), 1)
                    if k > 1:
                        if ch >= 1:
                            pe.wait_ge(sem(f"kv{k}_ready"), i)
                        mm(PS[:, 5, 0:B * C], wv[:, ch * D:(ch + 1) * D], values, start=True, stop=True)\
                            .then_inc(sem(f"kv{k}_done"), 1)
                pe.wait_ge(sem(f"kv{k}_ready"), chunks if k == 1 else 2 * chunks)
                if k > 1:
                    for n in range(8):
                        b = n // 4
                        if n >= 4:
                            pe.wait_ge(sem("vw_ready"), 8 * (k - 2) + n - 3)
                        for h in range(4 * (n % 4), 4 * (n % 4) + 4):
                            ch = h // 2 if chunks > 1 else 0
                            ins = mm(PS[0:C, n % 4, (h % 4) * D:(h % 4 + 1) * D], VTM[:, b, h, :],
                                     wo[:, ch * D:(ch + 1) * D], start=True, stop=True)
                        ins.then_inc(sem("vw_done"), 1)
                    pe.wait_ge(sem("vw_ready"), 8 * (k - 1))

            def cross_tiles(k, heads, chunks, wq):
                turns, rounds = heads // 4, (chunks + 3) // 4
                for t in range(NT + 1):
                    if t < NT:
                        b = t // HT
                        for n in range(rounds):
                            if t or n:
                                pe.wait_ge(sem(f"q{k}_ready"), t * rounds + n)
                            for ch in range(4 * n, min(4 * n + 4, chunks)):
                                ins = mm(PS[:, 6, (ch % 4) * P:(ch % 4 + 1) * P], wq[:, ch * D:(ch + 1) * D],
                                         HTR[:, t * P:(t + 1) * P], start=True, stop=True)
                            ins.then_inc(sem(f"q{k}_done"), 1)
                        pe.wait_ge(sem(f"q{k}_ready"), (t + 1) * rounds)
                        if t:
                            pe.wait_ge(sem(f"s{k}_shifted"), t)
                        for n in range(turns):
                            if chunks == 1:
                                ins = mm(PS[:, n, 0:4 * C], QC[:, 0, :],
                                         KTM[:, b, 4 * n:4 * n + 4, :].rearrange("p h k -> p (h k)"), start=True, stop=True)
                            else:
                                for ch in (2 * n, 2 * n + 1):
                                    ins = mm(PS[:, n, (ch % 2) * 2 * C:(ch % 2 + 1) * 2 * C], QC[:, ch, :],
                                             KTM[:, b, 2 * ch:2 * ch + 2, :].rearrange("p h k -> p (h k)"),
                                             start=True, stop=True)
                        ins.then_inc(sem(f"s{k}_done"), 1)
                    if t >= 1:
                        u = t - 1
                        pe.wait_ge(sem(f"p{k}_normed"), u + 1)
                        for n in range(turns):
                            i = u * turns + n
                            if i >= 2:
                                pe.wait_ge(sem(f"p{k}_ready"), i - 1)
                            for h in range(4 * n, 4 * n + 4):
                                ins = tp(PS[0:C, 4 + i % 2, (h % 4) * P:(h % 4 + 1) * P], SC[u % 2][:, h, :], ident)
                            ins.then_inc(sem(f"p{k}_turned"), 1)
                        pe.wait_ge(sem(f"p{k}_ready"), (u + 1) * turns)
                        if u:
                            pe.wait_ge(sem(f"o{k}_read"), u)
                        for h in range(heads):
                            ins = mm(PS[:, 7, (u % 2) * D:(u % 2) * D + D], PT[:, h, :], VW[:, u // HT, h, :],
                                     start=(h == 0), stop=(h == heads - 1))
                        ins.then_inc(sem(f"o{k}_done"), 1)

            def moe(k, router_w, n, second):
                m = {1: 8, 2: 10, 3: 12}[k]
                turned(m, 1)
                for t in range(NT):
                    ins = mm(PS[:, 4, t * 16:t * 16 + n], HTR[:, t * P:(t + 1) * P], router_w, start=True, stop=True)
                ins.then_inc(sem("router_done"), 1)

                def hidden(i):
                    g, slot = 16 * (k - 1) + i, (E0 + E * (k - 1) + i // 2) % RING
                    if i % 2 == 0:
                        expert_ready(pe, E0 + E * (k - 1) + i // 2)
                    for ch in range(FC):
                        if g >= 1:
                            pe.wait_ge(sem("moe_gelu"), 4 * (g - 1) + ch + 1)
                        mm(PS[:, ch, :], RINGW[:, slot, ch * P:(ch + 1) * P], HTR[:, cols(i % 2)], start=True, stop=True)\
                            .then_inc(sem("moe_hidden"), 1)

                hidden(0)
                for i in range(2 * E):
                    g, slot = 16 * (k - 1) + i, (E0 + E * (k - 1) + i // 2) % RING
                    if i + 1 < 2 * E:
                        hidden(i + 1)
                    pe.wait_ge(sem("moe_gelu"), 4 * g + 4)
                    pe.wait_ge(sem("comb_ready"), k)
                    if i >= 2:
                        pe.wait_ge(sem("moe_summed"), g - 1)
                    for j in range(HT):
                        for ch in range(FC):
                            ins = mm(PS[:, 4 + g % 2, j * D:(j + 1) * D], HB[g % 2][:, ch, j * P:(j + 1) * P],
                                     RINGW[:, slot, F + ch * D:F + (ch + 1) * D], start=(ch == 0), stop=(ch == FC - 1))
                    ins.then_inc(sem("moe_out"), 1)
                    if i % 2:
                        pe.wait_ge(sem("moe_out"), g + 1)
                        nc.tensor.nop().then_inc(sem("expert_used"), 1)
                    if i == 7 and second is not None:
                        for b in range(B):
                            for j in range(HT):
                                ins = tp(PS[0:E, 6 + b, j * P:(j + 1) * P], GC[:, HT * b + j, 0:E], ident)
                            ins.then_inc(sem("comb_turned"), 1)
                        for b in range(B):
                            pe.wait_ge(sem("combt_ready"), 2 * second + b + 1)
                            for j in range(HT):
                                ins = mm(PS[:, 6 + b, j * D:(j + 1) * D], COMBT[0:E, (HT * b + j) * P:(HT * b + j + 1) * P],
                                         B2[:, second, :], start=True, stop=True)
                            ins.then_inc(sem("moe_bias"), 1)

            pe.wait_ge(sem("ctx_normed"), 1)
            for b in range(B):
                ins = tp(PS[:, 5, b * C:(b + 1) * C], TMP[0:C, b * D:(b + 1) * D], ident[0:C, 0:C])
            ins.then_inc(sem("ctx_turned"), 1)
            for b in range(B):
                mm(PS[0:C, b, 0:D], w("ctxT")[:, b * C:(b + 1) * C], w("L1x_Wv"), start=True, stop=True).then_inc(sem("v1_done"), 1)
            for b in range(B):
                turn(4, b, XH, "xh2", b + 1)
            pe.wait_ge(sem("v1_ready"), 2)
            pe.wait_ge(sem("ctxn_ready"), 1)
            cross_setup(1, 1, w("L1x_Wk"), None, None, CTXN)
            turned(4, 1)
            cross_tiles(1, 8, 1, w("L1x_Wq"))
            for b in range(B):
                turn(5, b, XH, "xh3", b + 1)
            for b in range(B):
                turned(5, b)
                for j in range(HT):
                    ins = mm(PS[:, b, j * D:(j + 1) * D], tile_of(YT, b, j), w("L1x_Wo"), start=True, stop=True)
                ins.then_inc(sem("l1_wo"), 1)
            for b in range(B):
                turn(6, b, XH, "xh4", b + 1)
            for b in range(B):
                turned(6, b)
                if b:
                    pe.wait_ge(sem("qk_pieces"), 2)
                for n, name in enumerate(("L1f_Wq", "L1f_WqR", "L1f_Wk", "L1f_WkR")):
                    ins = mm(PS[:, n, :], w(name), HTR[:, cols(b)], start=True, stop=True)
                ins.then_inc(sem("qk_done"), 1)
                for j in range(HT):
                    ins = mm(PS[:, 4 + b, j * D:(j + 1) * D], tile_of(HTR, b, j), w("L1f_Wv"), start=True, stop=True)
                ins.then_inc(sem("v_done"), 1)

            def max_scores(g, units):
                b = g // 4
                for un in units:
                    i = 8 * g + un
                    h = 4 * (g % 4) + un // 2
                    if un == 0 and g % 4 == 0:
                        pe.wait_ge(sem(f"stacked{b}"), 16 * 18)
                        pe.wait_ge(sem("qk_pieces"), 4)
                    if i >= 2:
                        pe.wait_ge(sem("max_done"), i - 1)
                    for x in range(2):
                        q0 = N * b + (2 * (un % 2) + x) * P
                        ins = mm(PS[:, 2 * (i % 2) + x, :], QS[0:72, h, q0:q0 + P], KS[0:72, h, cols(b)], start=True, stop=True)
                    ins.then_inc(sem("max_scores"), 1)

            def turn_max(g):
                pe.wait_ge(sem("max_pieces"), g + 1)
                if g >= 2:
                    pe.wait_ge(sem("heads_ready"), g - 1)
                for t in range(HT):
                    ins = tp(PS[0:12, 7, 0:256].bitcast(BF16)[:, t * P:(t + 1) * P],
                             MPB[:, t, :, :].rearrange("p i h -> p (i h)"), IDB[:, :])
                ins.then_inc(sem("max_turned"), 1)

            def attend(g, kt):
                b = g // 4
                if g % 4 == 0 and kt == 0:
                    pe.wait_ge(sem("v_ready"), 2)
                    pe.wait_ge(sem("ones_stacked"), 16)
                if kt == 0:
                    pe.wait_ge(sem(f"max_stacked{g % 2}"), 16 * 12 * (g // 2 + 1))
                for j in range(4):
                    idx = 16 * g + 4 * kt + j
                    h = 4 * (g % 4) + j
                    if idx >= 2:
                        pe.wait_ge(sem("probs"), idx - 1)
                    k0 = N * b + kt * P
                    mm(PS[:, 4 + idx % 2, :], KS[0:75, h, k0:k0 + P], QS[0:75, h, cols(b)], start=True, stop=True)\
                        .then_inc(sem("scores"), 1)

            def values(g, kt):
                b = g // 4
                pe.wait_ge(sem("probs"), 16 * g + 4 * kt + 4)
                if g and kt == 0:
                    pe.wait_ge(sem("heads_copied"), g)
                for j in range(4):
                    idx = 16 * g + 4 * kt + j
                    ins = mm(PS[32 * j:32 * j + 32, 6, :], VS[:, HT * b + kt, 4 * (g % 4) + j, :], PR[idx % 8],
                             start=(kt == 0), stop=(kt == 3))
                ins.then_inc(sem("pv_done"), 1)

            def turn_heads(g):
                pe.wait_ge(sem("heads_copied"), g + 1)
                if g < 7:
                    pe.wait_ge(sem("max_rows"), g + 2)
                for t in range(HT):
                    ins = tp(PS[:, 7, t * P:(t + 1) * P], TMP[:, t * P:(t + 1) * P], ident)
                ins.then_inc(sem("heads_turned"), 1)

            max_scores(0, range(8))
            turn_max(0)
            for g in range(8):
                for kt in range(4):
                    if g < 7 and kt < 3:
                        max_scores(g + 1, ((0, 1, 2), (3, 4, 5), (6, 7))[kt])
                    attend(g, kt)
                    if kt:
                        values(g, kt - 1)
                if g < 7:
                    turn_max(g + 1)
                values(g, 3)
                turn_heads(g)
            for b in range(B):
                turn(7, b, Y, "heads_ready", 4 * b + 4)
            for b in range(B):
                turned(7, b)
                for j in range(HT):
                    ins = mm(PS[:, b, j * D:(j + 1) * D], tile_of(YT, b, j), w("L1f_Wo"), start=True, stop=True)
                ins.then_inc(sem("l1f_o"), 1)
            for b in range(B):
                turn(8, b, XH, "xh5", b + 1)
            moe(1, w("L1f_Wg"), E, 0)
            pe.wait_ge(sem("xh7"), 1)
            cross_setup(2, 1, w("L2x_Wk"), w("L2x_Wv"), w("L2x_Wo"), w("ctxT"))
            for b in range(B):
                turn(9, b, XH, "xh7", b + 1)
            turned(9, 1)
            cross_tiles(2, 16, 1, w("L2x_Wq"))
            for b in range(B):
                turn(10, b, XH, "xh8", b + 1)
            moe(2, w("L2f_router"), E + 1, None)
            pe.wait_ge(sem("xh9"), 1)
            cross_setup(3, 8, w("L3x_wk"), w("L3x_wv"), w("L3x_wout"), w("ctxT"))
            for b in range(B):
                turn(11, b, XH, "xh9", b + 1)
            turned(11, 1)
            cross_tiles(3, 16, 8, w("L3x_wq"))
            for b in range(B):
                turn(12, b, XH, "xh10", b + 1)
            moe(3, w("L3f_router"), E, 1)


def kernel(**inputs):
    import concourse.bacc as bacc
    from concourse.bass_utils import run_bass_kernel_spmd as run

    a = {n: np.asarray(x) for n, x in inputs.items()}
    turn = np.array([8 * (i // 8) + (i % 8 + 4) % 8 for i in range(D)])

    def chunked(m):
        return m.reshape(-1, P, m.shape[1]).transpose(1, 0, 2).reshape(P, -1)

    def col(vec):
        return vec.reshape(-1, 1)

    parts = {
        "L0_WqT": a["L0_xattn_Wq"].T, "L0_WkT": a["L0_xattn_Wk"].T, "L0_WvT": a["L0_xattn_Wv"].T,
        "L0_WpT": a["L0_xattn_Wp"].T, "L0_routerT": a["L0_ffn_router_weight"].T,
        "L1x_Wq": a["L1_xattn_Wq"], "L1x_Wk": a["L1_xattn_Wk"], "L1x_Wv": a["L1_xattn_Wv"], "L1x_Wo": a["L1_xattn_Wo"],
        "L1f_Wq": a["L1_ffn_Wq"], "L1f_WqR": a["L1_ffn_Wq"][:, turn], "L1f_Wk": a["L1_ffn_Wk"],
        "L1f_WkR": a["L1_ffn_Wk"][:, turn], "L1f_Wv": a["L1_ffn_Wv"], "L1f_Wo": a["L1_ffn_Wo"], "L1f_Wg": a["L1_ffn_Wg"],
        "L2x_Wq": a["L2_xattn_W_q"], "L2x_Wk": a["L2_xattn_W_k"], "L2x_Wv": a["L2_xattn_W_v"], "L2x_Wo": a["L2_xattn_W_o"],
        "L2f_router": a["L2_ffn_router_w"],
        "L3x_wq": a["L3_xattn_w_q"], "L3x_wk": a["L3_xattn_w_kv"][:, :1024], "L3x_wv": a["L3_xattn_w_kv"][:, 1024:],
        "L3x_wout": chunked(a["L3_xattn_w_out"]), "L3f_router": a["L3_ffn_w_router"],
        "pre_g": col(a["L1_xattn_pre_g"]), "pre_b": col(a["L1_xattn_pre_b"]),
        "L3_gamma": col(a["L3_xattn_ln_gamma"]), "L3_beta": col(a["L3_xattn_ln_beta"]),
        "bq": col(a["L1_ffn_bq"]), "bqR": col(a["L1_ffn_bq"][turn]), "bk": col(a["L1_ffn_bk"]), "bkR": col(a["L1_ffn_bk"][turn]),
        "L1_b1": a["L1_ffn_b1"].reshape(E * FC, P).T, "L3_b1": a["L3_ffn_b1"].reshape(E * FC, P).T,
        "ctxT": a["ctx_1024"].reshape(B * C, D).T,
    }
    rows = {
        "g_xattn": a["g_xattn"], "g_ffn": a["g_ffn"], "gate": a["L3_xattn_gate"], "focus": a["L0_xattn_focusing_factor"].reshape(1),
        "norm_weight": a["L0_ffn_norm_weight"], "ln_g": a["L1_xattn_ln_g"], "ln_b": a["L1_xattn_ln_b"],
        "bv": a["L1_ffn_bv"], "bo": a["L1_ffn_bo"], "g1": a["L1_ffn_g1"], "be1": a["L1_ffn_be1"],
        "g2": a["L1_ffn_g2"], "be2": a["L1_ffn_be2"], "bg": a["L1_ffn_bg"], "L2_bo": a["L2_xattn_b_o"],
        "L2_router_b": a["L2_ffn_router_b"], "b_out": a["L3_xattn_b_out"],
    }

    def experts(w1, w2):
        n = w1.shape[0]
        second = w2.reshape(n, FC, P, D).transpose(0, 2, 1, 3).reshape(n, P, FC * D)
        return np.concatenate([w1, second], 2)

    arrays = {
        "wpack": np.concatenate([parts[n] for n, _ in W_PARTS], 1),
        "rpack": np.concatenate([rows[n] for n, _ in R_PARTS])[None],
        "cpack": shape_constants(),
        "ones": np.full((3, 16 * T // 2), 0x3F803F80, np.uint32).view(np.float32),
        "ctx_rows": a["ctx_1024"].transpose(1, 0, 2),
        "x": a["x"].reshape(NT, P, D).transpose(1, 0, 2),
        "up0": experts(a["L0_ffn_fc1_weight"].transpose(0, 2, 1), a["L0_ffn_fc2_weight"].transpose(0, 2, 1)),
        "up": np.concatenate([experts(a["L1_ffn_W1"], a["L1_ffn_W2"]), experts(a["L2_ffn_w1"], a["L2_ffn_w2"]),
                              experts(a["L3_ffn_w1"], a["L3_ffn_w2"])]),
        "b_l0": np.concatenate([a["L0_ffn_fc1_bias"], a["L0_ffn_fc2_bias"], a["L0_ffn_router_bias"][:, None]], 1),
        "b2_l1": a["L1_ffn_b2"], "b2_l3": a["L3_ffn_b2"],
    }
    nc = bacc.Bacc("TRN2", target_bir_lowering=False, num_devices=1)
    arrays = {n: np.ascontiguousarray(x) for n, x in arrays.items()}
    t = {n: nc.dram_tensor(n, x.shape, F32, kind="ExternalInput").ap() for n, x in arrays.items()}
    out = nc.dram_tensor("out", (P, NT, D), F32, kind="ExternalOutput").ap()
    scratch = nc.dram_tensor("scratch", (6, P, T), BF16).ap()
    build(nc, t["wpack"], t["rpack"], t["cpack"], t["ones"], t["ctx_rows"], t["x"], t["up0"], t["up"], t["b_l0"],
          t["b2_l1"], t["b2_l3"], scratch, out)
    r = run(nc, [arrays], core_ids=[0])
    return r.results[0]["out"].transpose(1, 0, 2).reshape(B, N, D)
```

```python
from contextlib import ExitStack

import numpy as np
import concourse.bass as bass
from concourse import mybir

F32 = mybir.dt.float32
BF16 = mybir.dt.bfloat16
ALU = mybir.AluOpType
ACT = mybir.ActivationFunctionType
AX = mybir.AxisListType

P = 128
D = 128
B = 2
N = 512
T = B * N
NT = T // P
HT = NT // B
C = 77
F = 512
FC = F // P
SLOTS = 64
E0 = 16
E = 8
PAIRS = E0 // 2
KEEP = 5
EPS = 1e-5
RING = 4
UB = 5
UW = UB * P
UK = 8 * C
CROSS_KEPT = 12000
NEG = -3.0e38

W_PARTS = [("L0_WqT", D), ("L0_WkT", D), ("L0_WvT", D), ("L0_WpT", D), ("L0_routerT", E0),
           ("L1x_Wq", D), ("L1x_Wk", D), ("L1x_Wv", D), ("L1x_Wo", D),
           ("L1f_Wq", D), ("L1f_WqR", D), ("L1f_Wk", D), ("L1f_WkR", D), ("L1f_Wv", D), ("L1f_Wo", D),
           ("L1f_Wg", E), ("L2x_Wq", D), ("L2x_Wk", D), ("L2x_Wv", D), ("L2x_Wo", D), ("L2f_router", E + 1),
           ("L3x_wq", 1024), ("L3x_wk", 1024), ("L3x_wv", 1024), ("L3x_wout", 1024), ("L3f_router", E),
           ("pre_g", 1), ("pre_b", 1), ("L3_gamma", 1), ("L3_beta", 1),
           ("bq", 1), ("bqR", 1), ("bk", 1), ("bkR", 1),
           ("L1_b1", E * FC), ("L3_b1", E * FC), ("ctxT", B * C)]
R_PARTS = [("g_xattn", 4), ("g_ffn", 4), ("gate", 1), ("focus", 1), ("norm_weight", D), ("ln_g", D), ("ln_b", D),
           ("bv", D), ("bo", D), ("g1", D), ("be1", D), ("g2", D), ("be2", D), ("bg", E),
           ("L2_bo", D), ("L2_router_b", E + 1), ("b_out", D)]
C_PARTS = [("ident", P), ("mask16", 16), ("mask8", 8), ("mask2", 2), ("blocks", D), ("order8", 8), ("order9", 9),
           ("cos", N), ("sin", N), ("iota", SLOTS), ("diag", T), ("pairsel", PAIRS * P)]


def columns(parts):
    at, out = 0, {}
    for name, n in parts:
        out[name] = (at, n)
        at += n
    return out, at


W_AT, W_COLS = columns(W_PARTS)
R_AT, R_COLS = columns(R_PARTS)
C_AT, C_COLS = columns(C_PARTS)


def shape_constants():
    c = np.zeros((P, C_COLS), np.float32)

    def put(name, a):
        at, n = C_AT[name]
        c[0:a.shape[0], at:at + n] = a

    p = np.arange(P)
    put("ident", np.eye(P))
    put("mask16", p[:, None] // 8 == np.arange(16)[None])
    put("mask8", p[:, None] // 16 == np.arange(8)[None])
    put("mask2", p[:, None] // 64 == np.arange(2)[None])
    put("blocks", p[:, None] // 8 == p[None] // 8)
    put("order8", np.tile(7 - np.arange(8), (P, 1)))
    put("order9", np.tile(8 - np.arange(9), (P, 1)))
    inv = 1.0 / 10000.0 ** (np.arange(0, 8, 2, dtype=np.float32) / np.float32(8))
    freqs = np.arange(N, dtype=np.float32)[:, None] * inv.astype(np.float32)[None]
    emb = np.concatenate([freqs, freqs], -1).astype(np.float32)
    sign = np.where(np.arange(8) < 4, -1.0, 1.0)
    put("cos", np.tile(np.cos(emb).T, (16, 1)))
    put("sin", np.tile((np.sin(emb) * sign).T, (16, 1)))
    put("iota", np.tile(1 + np.arange(SLOTS), (P, 1)))
    slot_expert = np.arange(T) // SLOTS
    put("diag", np.tile(np.arange(E0)[:, None] == slot_expert[None], (3, 1)))
    sel = np.zeros((E0, PAIRS, P))
    for pair in range(PAIRS):
        for m in range(P):
            sel[2 * pair + m // SLOTS, pair, m] = 1
    put("pairsel", sel.reshape(E0, PAIRS * P))
    return c


def build(nc, wpack, rpack, cpack, ones_in, ctx_rows, x_in, up0, up, b_l0, b2_l1, b2_l3, scratch, out):
    with ExitStack() as ctx:
        def sb(name, shape, dt=F32):
            return ctx.enter_context(nc.sbuf_tensor(name, shape, dt))

        sems = {}

        def sem(name):
            if name not in sems:
                sems[name] = ctx.enter_context(nc.semaphore(name))
            return sems[name]

        Wt = sb("Wt", [P, W_COLS])
        Rt = sb("Rt", [P, R_COLS])
        Ct = sb("Ct", [P, C_COLS])
        CX = sb("CX", [C, B, D])
        B0 = sb("B0", [E0, F + D + 1])
        B2 = sb("B2", [E, 2, D])
        RINGW = sb("RINGW", [P, RING, 2 * F])

        X = sb("X", [P, NT, D])
        XH = sb("XH", [P, NT, D])
        HTR = sb("HTR", [P, T])
        Y = sb("Y", [P, NT, D])
        YT = sb("YT", [P, T])
        ACC = sb("ACC", [P, NT, D])
        TG = sb("TG", [P, 9])
        ST6 = sb("ST6", [P, NT, 6])
        MV = sb("MV", [P, NT, 2])
        RS = sb("RS", [P, NT, 4])
        HALFNEG = sb("HALFNEG", [P, HT])
        REC = sb("REC", [P, 2, 8])
        CTXH = sb("CTXH", [C, B, D])
        CTXN = sb("CTXN", [P, B * C])
        OT = sb("OT", [P, N])
        GL = sb("GL", [P, NT, 16])
        GM = sb("GM", [P, NT, 16])
        GR = sb("GR", [P, NT, 16])
        GC = sb("GC", [P, NT, 16])
        GS = sb("GS", [P, NT, 16])
        G1 = sb("G1", [P, NT])
        G2 = sb("G2", [P, NT])
        COMBT = sb("COMBT", [16, T])
        TMP = sb("TMP", [P, N])
        TMP2 = sb("TMP2", [P, N])
        RK = sb("RK", [P, N])
        RG = sb("RG", [P, N])
        SM = sb("SM", [P, 64])
        BIG = sb("BIG", [P, 22528])
        PS = ctx.enter_context(nc.psum_tensor("PS", [P, 8, 512], F32))

        def w(name, a=0, b=None):
            at, n = W_AT[name]
            return Wt[:, at + a:at + (n if b is None else b)]

        def r(name, rows=P):
            at, n = R_AT[name]
            return Rt[0:rows, at:at + n]

        def c(name, rows=P):
            at, n = C_AT[name]
            return Ct[0:rows, at:at + n]

        ident = c("ident")
        big_at = [0]

        def big(rows, cols, dt=F32):
            n = cols if dt == F32 else (cols + 1) // 2
            a = BIG[0:rows, big_at[0]:big_at[0] + n]
            big_at[0] += n
            assert big_at[0] <= 22528, big_at[0]
            return a if dt == F32 else a.bitcast(dt)

        big_at[0] = 0
        KF = big(C, B * D).rearrange("p (b d) -> p b d", b=B)
        KZ = big(C, B * D).rearrange("p (b d) -> p b d", b=B)
        VA = big(C, B * (D + 2)).rearrange("p (b d) -> p b d", b=B)
        KVM = big(P, B * (D + 16)).rearrange("p (b d) -> p b d", b=B)
        QF = big(P, T).rearrange("p (t d) -> p t d", t=NT)
        QT = big(P, T)
        big_at[0] = 0
        LG = big(E0, T)
        LW = big(E0, T)
        CUM = big(E0, T)
        ONESR = big(E0, T)
        M8 = big(E0, 8)
        S0 = big(P, NT * T, BF16).rearrange("p (t s) -> p t s", t=NT)
        S0T = big(P, PAIRS * T, BF16).rearrange("p (q t) -> p q t", q=PAIRS)
        XP = big(P, NT * 3 * D, BF16).rearrange("p (t i d) -> p t i d", t=NT, i=3)
        WP = big(P, NT * 48, BF16).rearrange("p (t i e) -> p t i e", t=NT, i=3)
        XET = YT
        GM48 = big(48, T)
        GSL = big(P, PAIRS)
        HS = XH[:, 0:HT, :].rearrange("p t d -> p (t d)")
        HST = XH[:, HT:NT, :].rearrange("p t d -> p (t d)")
        YP = big(P, PAIRS * 3 * D, BF16).rearrange("p (q i d) -> p q i d", q=PAIRS, i=3)

        def cross_buffers(at, tiles_at, k, heads, chunks):
            units = heads // 8
            big_at[0] = at
            vt = [big(P, B * units * UW).rearrange("p (b u w) -> p b u w", b=B, u=units) for _ in range(2 if k == 3 else 1)]
            raw = [big(P, chunks * B * C).rearrange("p (c b k) -> p c b k", c=chunks, b=B) for _ in range(2)]
            end = big_at[0]
            if k > 1:
                big_at[0] = CROSS_KEPT
            kt = big(P, B * heads * C).rearrange("p (b h k) -> p b h k", b=B, h=heads)
            vw = big(P, B * units * UW).rearrange("p (b u i d) -> p b u i d", b=B, u=units, i=UB)
            if k == 1:
                big_at[0] = 0
            sc = [big(P, UW) for _ in range(3)]
            pt = [big(P, UW) for _ in range(2)]
            if k > 1:
                assert end <= CROSS_KEPT
                big_at[0] = 0
            qc = big(P, chunks * T).rearrange("p (b c n) -> p b c n", b=B, c=chunks)
            return dict(vt=vt, raw=raw, kt=kt, vw=vw, sc=sc, pt=pt, qc=qc)

        CROSS = {1: cross_buffers(16592, 0, 1, 8, 1), 2: cross_buffers(FC * N * 2, 0, 2, 16, 1),
                 3: cross_buffers(FC * N * 2, 0, 3, 16, 8)}
        big_at[0] = 0
        QS = big(75, 16 * T, BF16).rearrange("p (h t) -> p h t", h=16)
        KS = big(75, 16 * T, BF16).rearrange("p (h t) -> p h t", h=16)
        VS = big(P, NT * 16 * 32).rearrange("p (t h d) -> p t h d", t=NT, h=16)
        flat_y = Y[:, :, :].rearrange("p t d -> p (t d)")
        flat_acc = ACC[:, :, :].rearrange("p t d -> p (t d)")
        PIE = [a[:, n * 512:(n + 1) * 512].bitcast(BF16) for a in (flat_y, YT[:, :], flat_acc) for n in (0, 1)]
        PR = [a[:, n * N:(n + 1) * N] for a in (YT[:, :], flat_acc) for n in (0, 1)] + [big(P, N) for _ in range(4)]
        big_at[0] = 0
        HB = [big(P, FC * N).rearrange("p (c n) -> p c n", c=FC) for _ in range(2)]

        IDB = sb("IDB", [P, P], BF16)
        MX = sb("MX", [P, HT, 4])
        MPB = sb("MPB", [P, HT, 3, 4], BF16)
        MT = [a[0:12, 0:256].bitcast(BF16) for a in (TMP, TMP2)]

        def bc(ap, n, axis):
            a = ap.unsqueeze(axis)
            shape = list(a.shape)
            shape[axis] = n
            return a.to_broadcast(shape)

        def half(b):
            return slice(HT * b, HT * b + HT)

        def cols(b):
            return slice(N * b, N * b + N)

        def tiles(bank):
            return PS[:, bank, :].rearrange("p (t d) -> p t d", t=HT)

        def expert_ready(eng, n):
            eng.wait_ge(sem(f"expert_loaded{n % RING}"), 16 * (n // RING + 1))

        def inputs_ready(eng):
            for name in ("x_loaded", "consts_loaded", "weights_loaded"):
                eng.wait_ge(sem(name), 16)
            eng.wait_ge(sem("rows_loaded"), 16 * 5)

        class Steps:
            def __init__(self, eng, s):
                self.eng, self.s, self.n, self.told = eng, s, 0, {}

            def do(self, ins):
                ins.then_inc(self.s, 1)
                self.n += 1
                self.eng.wait_ge(self.s, self.n)

            def settle(self, name):
                self.told[name] = self.told.get(name, 0) + 1
                self.eng.wait_ge(sem(name), self.told[name])

        block = ctx.enter_context(nc.Block())

        @block.sync
        def _(sp):
            sp.dma_start(X[:, :, :], x_in).then_inc(sem("x_loaded"), 16)
            sp.dma_start(Ct[:, :], cpack).then_inc(sem("consts_loaded"), 16)
            sp.dma_start(Wt[:, :], wpack).then_inc(sem("weights_loaded"), 16)
            sp.dma_start(Rt[:, :], rpack.to_broadcast([P, R_COLS])).then_inc(sem("rows_loaded"), 16)
            sp.dma_start(CX[:, :, :], ctx_rows).then_inc(sem("rows_loaded"), 16)
            sp.dma_start(B0[:, :], b_l0).then_inc(sem("rows_loaded"), 16)
            sp.dma_start(B2[:, 0, :], b2_l1).then_inc(sem("rows_loaded"), 16)
            sp.dma_start(B2[:, 1, :], b2_l3).then_inc(sem("rows_loaded"), 16)

            def load_experts(lo, hi):
                for n in range(lo, hi):
                    if n >= RING:
                        sp.wait_ge(sem("expert_used"), n - RING + 1)
                    src = up0[n] if n < E0 else up[n - E0]
                    sp.dma_start(RINGW[:, n % RING, :], src).then_inc(sem(f"expert_loaded{n % RING}"), 16)

            load_experts(0, E0 + RING)
            sp.wait_ge(sem("qk_pieces"), 1)
            sp.dma_start(KS[72:75, :, :].rearrange("p h t -> p (h t)").bitcast(F32), ones_in).then_inc(sem("ones_stacked"), 16)
            for b in range(B):
                sp.wait_ge(sem("qk_pieces"), 2 * b + 2)
                for j in range(6):
                    sp.dma_start(scratch[j, :, cols(b)], PIE[j][:, cols(b)]).then_inc(sem(f"spilled{b}"), 16)
                sp.wait_ge(sem(f"spilled{b}"), 16 * 6)
                for i in range(3):
                    for j in range(3):
                        row = 8 * (3 * i + j)
                        for S, piece in ((QS, j), (KS, 3 + i)):
                            src = scratch[piece, :, cols(b)].rearrange("(h d) t -> d h t", d=8)
                            sp.dma_start(S[row:row + 8, :, cols(b)], src).then_inc(sem(f"stacked{b}"), 16)
            for g in range(8):
                sp.wait_ge(sem("max_rows"), g + 1)
                b, h0 = g // 4, 4 * (g % 4)
                sp.dma_start(QS[72:75, h0:h0 + 4, cols(b)], MT[g % 2]).then_inc(sem(f"max_stacked{g % 2}"), 16)
            load_experts(E0 + RING, E0 + 3 * E)
            for b in range(B):
                sp.wait_ge(sem("x_final"), b + 1)
                sp.dma_start(out[:, half(b), :], X[:, half(b), :]).then_inc(sem("stored"), 16)
            sp.wait_ge(sem("stored"), 16 * B)

        @block.gpsimd
        def _(pool):
            st = Steps(pool, sem("pool_step"))
            st.do(nc.gpsimd.memset(HALFNEG[:, :], -0.5))

            def inv_root(dst, var, rows=P, n=HT):
                st.do(nc.gpsimd.tensor_scalar(dst, var, EPS, None, ALU.add))
                return nc.gpsimd.tensor_tensor(dst, dst, HALFNEG[0:rows, 0:n], ALU.pow)

            def ln(n, b, double=False):
                pool.wait_ge(sem("ln_var"), 2 * n + b + 1)
                h = half(b)
                if not double:
                    inv_root(RS[:, h, 0], MV[:, h, 1]).then_inc(sem("ln_rstd"), 1)
                    return
                st.do(inv_root(RS[:, h, 1], MV[:, h, 1]))
                st.do(nc.gpsimd.tensor_tensor(RS[:, h, 2], RS[:, h, 1], RS[:, h, 1], ALU.mult))
                st.do(nc.gpsimd.tensor_tensor(RS[:, h, 2], RS[:, h, 2], MV[:, h, 1], ALU.mult))
                st.do(inv_root(RS[:, h, 3], RS[:, h, 2]))
                nc.gpsimd.tensor_tensor(RS[:, h, 0], RS[:, h, 1], RS[:, h, 3], ALU.mult).then_inc(sem("ln_rstd"), 1)

            for b in range(B):
                ln(0, b)
            pool.wait_ge(sem("ctx_var"), 1)
            inv_root(SM[0:C, 40:42], SM[0:C, 32:36].rearrange("p (b v) -> p b v", v=2)[:, :, 1], C, B)\
                .then_inc(sem("ctx_rstd"), 1)
            for b in range(B):
                ln(1, b, double=True)
            pool.wait_ge(sem("xn_ready"), 2)
            st.do(nc.gpsimd.tensor_copy(XP[:, :, 0, :], XH[:, :, :]))
            st.do(nc.gpsimd.tensor_tensor(ACC[:, :, :], XH[:, :, :], XP[:, :, 0, :], ALU.subtract))
            st.do(nc.gpsimd.tensor_copy(XP[:, :, 1, :], ACC[:, :, :]))
            st.do(nc.gpsimd.tensor_tensor(ACC[:, :, :], ACC[:, :, :], XP[:, :, 1, :], ALU.subtract))
            nc.gpsimd.tensor_copy(XP[:, :, 2, :], ACC[:, :, :]).then_inc(sem("xp_ready"), 1)
            def cross_setup(k, heads, chunks):
                x = CROSS[k]
                for vt in x["vt"]:
                    st.do(nc.gpsimd.memset(vt, 0.0))
                for ch in range(chunks):
                    hs = slice(2 * ch, 2 * ch + 2) if chunks > 1 else slice(0, heads)
                    n = hs.stop - hs.start
                    mask = c({2: "mask2", 8: "mask8", 16: "mask16"}[n])
                    pool.wait_ge(sem(f"kv{k}_raw"), ch // 3 + 1)
                    for b in range(B):
                        ins = nc.gpsimd.tensor_tensor(x["kt"][:, b, hs, :], bc(x["raw"][0][:, ch, b, :], n, 1), bc(mask, C, 2), ALU.mult)
                        units = [(hs.start // 8, hs)] if n == 2 else [(u, slice(8 * u, 8 * u + 8)) for u in range(heads // 8)]
                        for u, part in units:
                            m = part.stop - part.start
                            at = (part.start - 8 * u) * C
                            dst = x["vt"][ch % len(x["vt"])][:, b, u, at:at + m * C].rearrange("p (h k) -> p h k", h=m)
                            ins = nc.gpsimd.tensor_tensor(dst, bc(x["raw"][1][:, ch, b, :], m, 1),
                                                          bc(mask[:, part.start - hs.start:part.stop - hs.start], C, 2), ALU.mult)
                ins.then_inc(sem(f"kv{k}_masked"), 1)

            def cross_units(k, heads):
                x = CROSS[k]
                for u in range(NT * heads // 8):
                    pool.wait_ge(sem(f"sum{k}_ready"), u + 1)
                    s = x["sc"][u % 3][:, 0:UK].rearrange("p (h k) -> p h k", h=8)
                    nc.gpsimd.tensor_tensor(s, s, bc(REC[:, u % 2, :], C, 2), ALU.mult).then_inc(sem(f"p{k}_normed"), 1)

            def pads(k):
                for n, s in enumerate(CROSS[k]["sc"]):
                    ins = nc.gpsimd.memset(s[:, UK:UW], 0.0)
                ins.then_inc(sem("pads_ready"), 1)

            cross_setup(1, 8, 1)
            for b in range(B):
                ln(2, b, True)
            pads(1)
            cross_units(1, 8)
            for n in (3, 4, 5):
                for b in range(B):
                    ln(n, b)
            cross_setup(2, 16, 1)
            for n in (6, 7):
                for b in range(B):
                    ln(n, b)
            pads(2)
            cross_units(2, 16)
            for b in range(B):
                ln(8, b)
            cross_setup(3, 16, 8)
            for b in range(B):
                ln(9, b, True)
            pads(3)
            cross_units(3, 16)
            for b in range(B):
                ln(10, b)

        @block.scalar
        def _(act):
            st = Steps(act, sem("act_step"))
            inputs_ready(act)
            nc.scalar.activation(IDB[:, :], ident, ACT.Copy).then_inc(sem("idb_ready"), 1)
            at = R_AT["g_xattn"][0]
            nc.scalar.activation(TG[:, :], Rt[:, at:at + 9], ACT.Tanh).then_inc(sem("tg_ready"), 1)

            def transposed(m, b, dst, scale=None, bias=None):
                act.wait_ge(sem("tp_done"), 2 * m + b + 1)
                if scale is None:
                    ins = nc.scalar.activation(dst[:, cols(b)], PS[:, 6 + b, :], ACT.Copy)
                else:
                    ins = nc.scalar.activation(dst[:, cols(b)], PS[:, 6 + b, :], ACT.Identity, bias=bias, scale=scale)
                ins.then_inc(sem("tr_ready"), 1)

            def cross_raw(k, r, chunks):
                x = CROSS[k]
                lo, hi = 3 * r, min(3 * r + 3, chunks)
                act.wait_ge(sem(f"kv{k}_done"), r + 1)
                for i in range(2):
                    src = PS[:, 6 + i, 0:(hi - lo) * B * C].rearrange("p (c b k) -> p c b k", c=hi - lo, b=B)
                    ins = nc.scalar.activation(x["raw"][i][:, lo:hi, :, :], src, ACT.Copy)
                ins.then_inc(sem(f"kv{k}_raw"), 1)

            def cross_vw(k, n, units):
                x = CROSS[k]
                b, u = n // units, n % units
                act.wait_ge(sem(f"vw{k}_done"), n + 1)
                nc.scalar.activation(x["vw"][:, b, u, 0:3, :], PS[:, 6, 0:3 * D].rearrange("p (i d) -> p i d", i=3), ACT.Copy)
                nc.scalar.activation(x["vw"][:, b, u, 3:5, :], PS[:, 7, 0:2 * D].rearrange("p (i d) -> p i d", i=2),
                                     ACT.Copy).then_inc(sem(f"vw{k}_ready"), 1)

            def cross_tiles(k, heads, chunks, scale):
                x = CROSS[k]
                units = NT * heads // 8
                first = B if chunks == 1 else chunks

                def q_out(j, bank):
                    act.wait_ge(sem(f"q{k}_done"), j + 1)
                    nc.scalar.activation(x["qc"][:, j // chunks, j % chunks, :], PS[:, bank, :], ACT.Copy)\
                        .then_inc(sem(f"q{k}_ready"), 1)

                for j in range(first):
                    q_out(j, j)
                for s in range(units + 2):
                    if s < units:
                        act.wait_ge(sem(f"s{k}_shifted"), s + 1)
                        a = x["sc"][s % 3][:, 0:UK]
                        nc.scalar.activation(a, a, ACT.Exp, scale=scale).then_inc(sem(f"s{k}_exp"), 1)
                    if chunks > 1 and s < chunks:
                        q_out(chunks + s, 6)
                    if s >= 2:
                        u = s - 2
                        if u >= 2:
                            act.wait_ge(sem(f"pv{k}_done"), u - 1)
                        for n, (lo, hi) in enumerate(((0, 3), (3, 5))):
                            act.wait_ge(sem(f"p{k}_turned"), 2 * u + n + 1)
                            nc.scalar.activation(x["pt"][u % 2][:, lo * P:hi * P], PS[:, 4 + n, 0:(hi - lo) * P], ACT.Copy)\
                                .then_inc(sem(f"pt{k}_ready"), 1)

            def focus(fi, rows, groups):
                act.wait_ge(sem("focus_abs"), fi + 1)
                nc.scalar.activation(TMP[0:rows, 0:groups * D], TMP2[0:rows, 0:groups * D], ACT.Ln,
                                     bias=SM[0:rows, 63:64]).then_inc(sem("focus_ln"), 1)
                act.wait_ge(sem("focus_max"), fi + 1)
                for g in range(groups):
                    ins = nc.scalar.activation(TMP2[0:rows, g * D:(g + 1) * D], TMP[0:rows, g * D:(g + 1) * D], ACT.Exp,
                                               bias=SM[0:rows, 8 + g:9 + g], accum_out=SM[0:rows, 16 + g:17 + g])
                ins.then_inc(sem("focus_exp"), 1)

            for b in range(B):
                transposed(0, b, HTR)
            for b in range(B):
                focus(b, C, 1)
            for b in range(B):
                focus(2 + b, P, HT)
                if b:
                    transposed(1, 0, QT)
            transposed(1, 1, QT)
            for b in range(B):
                transposed(2, b, YT)
            for b in range(B):
                transposed(3, b, HTR)
                act.wait_ge(sem("l0_logits"), b + 1)
                nc.scalar.activation(LG[:, cols(b)], PS[0:E0, b, :], ACT.Identity, bias=B0[:, F + D:F + D + 1])\
                    .then_inc(sem("l0_logits_ready"), 1)

            def router_exp(k, n):
                act.wait_ge(sem("router_shifted"), k + 1)
                nc.scalar.activation(GM[:, :, 0:n], GL[:, :, 0:n], ACT.Exp).then_inc(sem("router_exp"), 1)

            act.wait_ge(sem("ctx_turned"), 1)
            nc.scalar.activation(CTXN[:, :], PS[:, 5, 0:B * C], ACT.Identity, bias=w("pre_b"), scale=w("pre_g"))\
                .then_inc(sem("ctxn_ready"), 1)
            router_exp(0, E0)
            cross_raw(1, 0, 1)
            for q in range(PAIRS):
                act.wait_ge(sem("slots_turned"), q + 1)
                nc.scalar.activation(S0T[:, q, :], PS[:, 2 + q % 2, :].bitcast(BF16), ACT.Copy)\
                    .then_inc(sem("slots_turned_ready"), 1)
            for n in range(2):
                act.wait_ge(sem("gathered"), n + 1)
                nc.scalar.activation(XET[:, cols(n)], PS[:, 4 + n, :], ACT.Copy).then_inc(sem("gathered_ready"), 1)
            for n in range(B):
                cross_vw(1, n, 1)
            for q in range(PAIRS):
                act.wait_ge(sem("l0_hidden"), q + 1)
                nc.scalar.activation(HS, PS[:, q % 2, :], ACT.Gelu).then_inc(sem("l0_gelu"), 1)
                act.wait_ge(sem("l0_hidden_turned"), q + 1)
                nc.scalar.activation(HST, PS[:, 2, :], ACT.Copy).then_inc(sem("l0_hidden_ready"), 1)

            def moe(k, func, b1, second):
                router_exp(k, E + 1 if k == 2 else E)
                for i in range(2 * E):
                    g = 16 * (k - 1) + i
                    for ch in range(FC):
                        act.wait_ge(sem("moe_hidden"), 4 * g + ch + 1)
                        if g >= 2:
                            act.wait_ge(sem("moe_out"), g - 1)
                        col = b1[:, i // 2 * FC + ch:i // 2 * FC + ch + 1] if b1 is not None else 0.0
                        nc.scalar.activation(HB[g % 2][:, ch, :], PS[:, ch, :], func, bias=col)\
                            .then_inc(sem("moe_gelu"), 1)
                    if i == 7 and second is not None:
                        for b in range(B):
                            act.wait_ge(sem("comb_turned"), 2 * second + b + 1)
                            nc.scalar.activation(COMBT[0:E, cols(b)], PS[0:E, 6 + b, :], ACT.Copy)\
                                .then_inc(sem("combt_ready"), 1)
                    if k < 3:
                        chunks = 1 if k == 1 else 8
                        if 0 <= i - 8 < (chunks + 2) // 3:
                            cross_raw(k + 1, i - 8, chunks)
                        if i >= 12:
                            cross_vw(k + 1, i - 12, 2)

            for b in range(B):
                transposed(4, b, HTR, w("pre_g"), w("pre_b"))
            cross_tiles(1, 8, 1, 1.0 / np.sqrt(128.0))
            for b in range(B):
                transposed(5, b, YT)
            for b in range(B):
                act.wait_ge(sem("l1_wo"), b + 1)
                nc.scalar.activation(ACC[:, half(b), :], tiles(b), ACT.Gelu).then_inc(sem("l1_wo_gelu"), 1)
            for b in range(B):
                transposed(6, b, HTR)
            for idx in range(8 * 16):
                act.wait_ge(sem("scores"), idx + 1)
                if idx >= 8:
                    act.wait_ge(sem("pv_done"), (idx - 8) // 4 + 1)
                nc.scalar.activation(PR[idx % 8], PS[:, 4 + idx % 2, :], ACT.Exp, scale=1.0 / np.sqrt(8.0))\
                    .then_inc(sem("probs"), 1)
            for b in range(B):
                transposed(7, b, YT)
            for b in range(B):
                transposed(8, b, HTR)
            moe(1, ACT.Gelu, w("L1_b1"), 0)
            for b in range(B):
                transposed(9, b, HTR)
            cross_tiles(2, 16, 1, 1.0 / np.sqrt(8.0))
            for b in range(B):
                transposed(10, b, HTR)
            moe(2, ACT.Gelu, None, None)
            for b in range(B):
                transposed(11, b, HTR, w("L3_gamma"), w("L3_beta"))
            cross_tiles(3, 16, 8, 64.0 ** -0.5)
            for b in range(B):
                transposed(12, b, HTR)
            moe(3, ACT.Gelu_apprx_tanh, w("L3_b1"), 1)

        @block.vector
        def _(dve):
            v = nc.vector
            st = Steps(dve, sem("dve_step"))
            inputs_ready(dve)
            st.do(v.memset(SM[:, 63:64], 1e-6))
            for b in range(B):
                st.do(v.bn_stats(ST6[0:C, b, :], CX[:, b, :]))
                ins = v.bn_aggr(SM[0:C, 32 + 2 * b:34 + 2 * b], ST6[0:C, b, :])
            ins.then_inc(sem("ctx_var"), 1)
            st.settle("ctx_var")

            def ln(n, b, src):
                h = range(HT * b, HT * b + HT)
                for t in h:
                    ins = v.bn_stats(ST6[:, t, :], src[:, t, :])
                st.do(ins)
                for t in h:
                    ins = v.bn_aggr(MV[:, t, :], ST6[:, t, :])
                ins.then_inc(sem("ln_var"), 1)
                st.settle("ln_var")
                dve.wait_ge(sem("ln_rstd"), 2 * n + b + 1)
                dve.wait_ge(sem("ln_var"), 2 * n + b + 1)
                for t in h:
                    ins = v.tensor_scalar(XH[:, t, :], src[:, t, :], MV[:, t, 0:1], RS[:, t, 0:1],
                                          ALU.subtract, ALU.mult)
                return ins

            def gain(b, name, name2):
                st.do(v.tensor_tensor(XH[:, half(b), :], XH[:, half(b), :], bc(r(name), HT, 1), ALU.mult))
                return v.tensor_tensor(XH[:, half(b), :], XH[:, half(b), :], bc(r(name2), HT, 1), ALU.add)

            def keep_largest(dst, val, rows, groups, n, order, keep):
                R = RK[0:rows, 0:groups * n].rearrange("p (g i) -> p g i", i=n)
                G = RG[0:rows, 0:groups * n].rearrange("p (g i) -> p g i", i=n)
                st.do(v.tensor_copy(R, bc(order, groups, 1)))
                for s in range(1, n):
                    st.do(v.tensor_tensor(G[:, :, 0:n - s], val[:, :, 0:n - s], val[:, :, s:n], ALU.is_ge))
                    st.do(v.tensor_tensor(R[:, :, s:n], R[:, :, s:n], G[:, :, 0:n - s], ALU.add))
                    st.do(v.tensor_tensor(R[:, :, 0:n - s], R[:, :, 0:n - s], G[:, :, 0:n - s], ALU.subtract))
                return v.scalar_tensor_tensor(out=dst, in0=R, scalar=keep - 0.5, in1=val, op0=ALU.is_lt, op1=ALU.mult)

            def split3(dsts, src, left):
                st.do(v.tensor_copy(dsts[0], src))
                st.do(v.tensor_tensor(left, src, dsts[0], ALU.subtract))
                st.do(v.tensor_copy(dsts[1], left))
                st.do(v.tensor_tensor(left, left, dsts[1], ALU.subtract))
                return v.tensor_copy(dsts[2], left)

            def add_to_x(b, src, gate):
                st.do(v.scalar_tensor_tensor(out=X[:, half(b), :], in0=src, scalar=TG[:, gate:gate + 1],
                                             in1=X[:, half(b), :], op0=ALU.mult, op1=ALU.add))

            for b in range(B):
                ln(0, b, X).then_inc(sem("xh0"), 1)
                st.settle("xh0")

            dve.wait_ge(sem("ctx_rstd"), 1)
            for b in range(B):
                ins = v.tensor_scalar(CTXH[:, b, :], CX[:, b, :], SM[0:C, 32 + 2 * b:33 + 2 * b],
                                      SM[0:C, 40 + b:41 + b], ALU.subtract, ALU.mult)
            ins.then_inc(sem("ctx_normed"), 1)
            st.settle("ctx_normed")

            def focus(fi, src, dst, rows, groups):
                n = groups * D
                t1 = TMP[0:rows, 0:n].rearrange("p (g d) -> p g d", d=D)
                t2 = TMP2[0:rows, 0:n].rearrange("p (g d) -> p g d", d=D)
                sm = SM[0:rows, :]
                st.do(v.tensor_scalar(t1, src, -0.01, None, ALU.mult))
                v.tensor_tensor(t2, src, t1, ALU.max).then_inc(sem("focus_abs"), 1)
                st.settle("focus_abs")
                dve.wait_ge(sem("focus_abs"), fi + 1)
                st.do(v.tensor_reduce(sm[:, 0:groups], t2, AX.X, ALU.add))
                dve.wait_ge(sem("focus_ln"), fi + 1)
                st.do(v.tensor_scalar(t1, t1, r("focus", rows), None, ALU.mult))
                v.tensor_reduce(sm[:, 8:8 + groups], t1, AX.X, ALU.max, negate=True).then_inc(sem("focus_max"), 1)
                st.settle("focus_max")
                dve.wait_ge(sem("focus_exp"), fi + 1)
                st.do(v.reciprocal(sm[:, 16:16 + groups], sm[:, 16:16 + groups]))
                st.do(v.tensor_scalar(sm[:, 0:groups], sm[:, 0:groups], 1.0 / D, 1e-6, ALU.mult, ALU.add))
                st.do(v.tensor_tensor(sm[:, 0:groups], sm[:, 0:groups], sm[:, 16:16 + groups], ALU.mult))
                for g in range(groups):
                    ins = v.tensor_scalar(t2[:, g, :], t2[:, g, :], sm[:, g:g + 1], None, ALU.mult)
                st.do(ins)
                flat = t2.rearrange("p g (h i) -> p (g h) i", i=8)
                return keep_largest(dst, flat, rows, groups * 16, 8, c("order8", rows), KEEP)

            for b in range(B):
                dve.wait_ge(sem("l0_kv"), b + 1)
                st.do(v.tensor_copy(VA[:, b, 0:D], PS[0:C, b, D:2 * D]))
                st.do(v.memset(VA[:, b, D:D + 1], 1.0))
                focus(b, PS[0:C, b, 0:D].rearrange("p (g d) -> p g d", g=1), 
                      KF[:, b, :].rearrange("p (h i) -> p h i", i=8), C, 1).then_inc(sem("l0_k_ready"), 1)
                st.settle("l0_k_ready")
            for b in range(B):
                dve.wait_ge(sem("l0_sums"), b + 1)
                st.do(v.scalar_tensor_tensor(out=KVM[:, b, 0:D], in0=PS[:, 2 + b, 0:D], scalar=1.0 / N,
                                             in1=c("blocks"), op0=ALU.mult, op1=ALU.mult))
                st.do(v.tensor_scalar(SM[:, 24:25], PS[:, 2 + b, D:D + 1], 1.0 / C, None, ALU.mult))
                v.tensor_scalar(KVM[:, b, D:D + 16], c("mask16"), SM[:, 24:25], None, ALU.mult)\
                    .then_inc(sem("l0_state_ready"), 1)
                st.settle("l0_state_ready")
            for b in range(B):
                dve.wait_ge(sem("l0_q"), b + 1)
                focus(2 + b, tiles(4 + b), QF[:, half(b), :].rearrange("p t (h i) -> p (t h) i", i=8), P, HT)\
                    .then_inc(sem("qf_ready"), 1)
                st.settle("qf_ready")
            for b in range(B):
                dve.wait_ge(sem("l0_y"), b + 1)
                y = PS[:, 2 * b:2 * b + 2, :].rearrange("p k (j n) -> p (k j) n", n=256)
                z = RG[:, 0:64].rearrange("p (t h) -> p t h", t=HT)
                st.do(v.tensor_scalar(z, y[:, :, D:D + 16], 1e-6, None, ALU.add))
                st.do(v.reciprocal(z, z))
                v.tensor_tensor(Y[:, half(b), :].rearrange("p t (h i) -> p t h i", i=8),
                                y[:, :, 0:D].rearrange("p t (h i) -> p t h i", i=8), bc(z, 8, 3), ALU.mult)\
                    .then_inc(sem("y_ready"), 1)
                st.settle("y_ready")
            dve.wait_ge(sem("tg_ready"), 1)
            for b in range(B):
                dve.wait_ge(sem("l0_o"), b + 1)
                add_to_x(b, tiles(4 + b), 0)
                st.do(ln(1, b, X))
                v.tensor_tensor(XH[:, half(b), :], XH[:, half(b), :], bc(r("norm_weight"), HT, 1), ALU.mult)\
                    .then_inc(sem("xn_ready"), 1)
                st.settle("xn_ready")

            def router(k, n, src, bias):
                gl = GL[:, :, 0:n]
                if bias is None:
                    st.do(v.tensor_copy(gl, src))
                else:
                    st.do(v.tensor_tensor(gl, src, bc(bias, NT, 1), ALU.add))
                st.do(v.tensor_reduce(G1[:, :], gl, AX.X, ALU.max))
                v.tensor_tensor(gl, gl, bc(G1[:, :], n, 2), ALU.subtract).then_inc(sem("router_shifted"), 1)
                st.settle("router_shifted")
                dve.wait_ge(sem("router_exp"), k + 1)
                st.do(v.tensor_reduce(G1[:, :], GM[:, :, 0:n], AX.X, ALU.add))
                st.do(v.reciprocal(G1[:, :], G1[:, :]))
                st.do(v.tensor_tensor(GR[:, :, 0:n], GM[:, :, 0:n], bc(G1[:, :], n, 2), ALU.mult))

            st.do(v.memset(ONESR[:, :], 1.0))
            dve.wait_ge(sem("l0_logits_ready"), 2)
            src = LG
            for n in range(SLOTS // 8):
                st.do(v.max(M8[:, :], src))
                st.do(v.match_replace(LW, M8[:, :], src, NEG))
                src = LW
            st.do(v.tensor_tensor(LW, LW, LG, ALU.not_equal))
            st.do(v.tensor_tensor_scan(CUM, ONESR, LW, 0.0, ALU.mult, ALU.add))
            v.tensor_tensor(CUM, CUM, LW, ALU.mult).then_inc(sem("places_ready"), 1)
            st.settle("places_ready")
            dve.wait_ge(sem("l0_logits_turned"), 1)
            router(0, E0, PS[:, 2, 0:NT * E0].rearrange("p (t e) -> p t e", t=NT), None)
            dve.wait_ge(sem("places_turned"), 1)
            places = PS[:, 3, 0:NT * E0].rearrange("p (t e) -> p t e", t=NT)
            st.do(v.tensor_copy(GC[:, :, :], places))
            for t in range(NT):
                v.tensor_tensor(S0[:, t, :].rearrange("p (e s) -> p e s", e=E0), bc(c("iota"), E0, 1),
                                bc(GC[:, t, :], SLOTS, 2), ALU.is_equal).then_inc(sem("slots_ready"), 1)
                st.settle("slots_ready")
            st.do(v.scalar_tensor_tensor(out=GS[:, :, :], in0=GC[:, :, :], scalar=0.0, in1=GR[:, :, :], op0=ALU.is_gt, op1=ALU.mult))
            st.do(v.tensor_reduce(G2[:, :], GS[:, :, :], AX.X, ALU.add))
            st.do(v.tensor_scalar(G2[:, :], G2[:, :], 1e-37, None, ALU.max))
            st.do(v.reciprocal(G2[:, :], G2[:, :]))
            st.do(v.tensor_tensor(GS[:, :, :], GS[:, :, :], bc(G2[:, :], E0, 2), ALU.mult))
            split3([WP[:, :, i, :] for i in range(3)], GS[:, :, :], GM[:, :, :]).then_inc(sem("shares_ready"), 1)
            st.settle("shares_ready")
            for n in range(2):
                dve.wait_ge(sem("shares_gathered"), n + 1)
                v.tensor_tensor(GM48[:, cols(n)], PS[0:48, n, :], c("diag", 48)[:, cols(n)], ALU.mult)\
                    .then_inc(sem("shares_own"), 1)
                st.settle("shares_own")
            dve.wait_ge(sem("shares_turned"), 1)
            st.do(v.tensor_copy(GSL[:, :], PS[:, 7, 0:PAIRS]))
            for q in range(PAIRS):
                dve.wait_ge(sem("expert_used"), 2 * q + 2)
                st.do(v.tensor_scalar(TMP[:, 0:D], PS[:, 3, 0:D], GSL[:, q:q + 1], None, ALU.mult))
                split3([YP[:, q, i, :] for i in range(3)], TMP[:, 0:D], TMP2[:, 0:D]).then_inc(sem("yp_ready"), 1)
                st.settle("yp_ready")
            for b in range(B):
                dve.wait_ge(sem("scattered"), b + 1)
                add_to_x(b, tiles(4 + b), 4)
                ln(2, b, X).then_inc(sem("xh2"), 1)
                st.settle("xh2")

            def cross_tiles(k, heads, tail):
                x = CROSS[k]
                per = heads // 8
                units = NT * per
                for s in range(units + 4):
                    if s < units:
                        a = x["sc"][s % 3][:, 0:UK].rearrange("p (n h k) -> p n h k", n=2, k=C)
                        raw = PS[:, 2 * (s % 2):2 * (s % 2) + 2, 0:4 * C].rearrange("p n (h k) -> p n h k", k=C)
                        top = SM[:, 0:8].rearrange("p (n h) -> p n h", h=4)
                        dve.wait_ge(sem(f"s{k}_done"), s + 1)
                        if s >= 3:
                            dve.wait_ge(sem(f"p{k}_turned"), 2 * (s - 2))
                        if k == 1:
                            lim = 10000.0 * float(np.sqrt(128.0))
                            st.do(v.tensor_scalar(a, raw, lim, -lim, ALU.min, ALU.max))
                            raw = a
                        st.do(v.tensor_reduce(top, raw, AX.X, ALU.max))
                        v.tensor_tensor(a, raw, bc(top, C, 3), ALU.subtract).then_inc(sem(f"s{k}_shifted"), 1)
                        st.settle(f"s{k}_shifted")
                    if 1 <= s <= units:
                        u = s - 1
                        a = x["sc"][u % 3][:, 0:UK].rearrange("p (h k) -> p h k", k=C)
                        dve.wait_ge(sem(f"s{k}_exp"), u + 1)
                        if u >= 2:
                            dve.wait_ge(sem(f"p{k}_normed"), u - 1)
                        st.do(v.tensor_reduce(REC[:, u % 2, :], a, AX.X, ALU.add))
                        v.reciprocal(REC[:, u % 2, :], REC[:, u % 2, :]).then_inc(sem(f"sum{k}_ready"), 1)
                        st.settle(f"sum{k}_ready")
                    if s >= 4 and (s - 3) % per == 0:
                        t = (s - 3) // per - 1
                        dve.wait_ge(sem(f"pv{k}_done"), per * (t + 1))
                        tail(t, PS[:, 7, 0:D])

            def top2(k, n):
                sem_in = sem("router_done")
                dve.wait_ge(sem_in, k)
                src = PS[:, 4, 0:NT * 16].rearrange("p (t e) -> p t e", t=NT)[:, :, 0:n]
                router(k, n, src, {1: r("bg"), 2: r("L2_router_b"), 3: None}[k])
                st.do(keep_largest(GC[:, :, 0:n], GR[:, :, 0:n], P, NT, n, c("order9" if n == 9 else "order8"), 2))
                if k == 1:
                    st.do(v.tensor_reduce(G1[:, :], GC[:, :, 0:n], AX.X, ALU.add))
                    st.do(v.reciprocal(G1[:, :], G1[:, :]))
                    st.do(v.tensor_tensor(GC[:, :, 0:n], GC[:, :, 0:n], bc(G1[:, :], n, 2), ALU.mult))
                if k == 1:
                    ins = v.tensor_copy(ACC[:, :, :], XH[:, :, :])
                elif k == 2:
                    ins = v.tensor_tensor(ACC[:, :, :], XH[:, :, :], bc(GC[:, :, E], D, 2), ALU.mult)
                else:
                    ins = v.memset(ACC[:, :, :], 0.0)
                ins.then_inc(sem("comb_ready"), 1)
                st.settle("comb_ready")
                dve.wait_ge(sem("comb_ready"), k)

            def moe(k, second):
                top2(k, E + 1 if k == 2 else E)
                for i in range(2 * E):
                    g = 16 * (k - 1) + i
                    e, b = i // 2, i % 2
                    dve.wait_ge(sem("moe_out"), g + 1)
                    if i >= 2:
                        dve.wait_ge(sem("moe_summed"), g - 1)
                    for j in range(HT):
                        t = HT * b + j
                        ins = v.scalar_tensor_tensor(out=ACC[:, t, :], in0=PS[:, 4 + g % 2, j * D:(j + 1) * D],
                                                     scalar=GC[:, t, e:e + 1], in1=ACC[:, t, :], op0=ALU.mult, op1=ALU.add)
                    ins.then_inc(sem("moe_summed"), 1)
                    st.settle("moe_summed")
                    if i == 7 and second is not None:
                        for b2 in range(B):
                            dve.wait_ge(sem("moe_bias"), 2 * second + b2 + 1)
                            dve.wait_ge(sem("moe_summed"), g + 1)
                            v.tensor_tensor(ACC[:, half(b2), :], tiles(6 + b2), ACC[:, half(b2), :], ALU.add)\
                                .then_inc(sem("bias_added"), 1)
                            st.settle("bias_added")
                dve.wait_ge(sem("moe_summed"), 16 * k)

            def keep_o(t, o):
                v.tensor_copy(Y[:, t, :], o).then_inc(sem("o1_read"), 1)
                st.settle("o1_read")

            cross_tiles(1, 8, keep_o)
            for b in range(B):
                st.do(ln(3, b, Y))
                gain(b, "ln_g", "ln_b").then_inc(sem("xh3"), 1)
                st.settle("xh3")
            dve.wait_ge(sem("xh3"), 2)
            for b in range(B):
                dve.wait_ge(sem("l1_wo_gelu"), b + 1)
                st.do(v.tensor_tensor(Y[:, half(b), :], ACC[:, half(b), :], XH[:, half(b), :], ALU.add))
                add_to_x(b, Y[:, half(b), :], 1)
            for b in range(B):
                ln(4, b, X).then_inc(sem("xh4"), 1)
                st.settle("xh4")
            st.do(v.memset(VS[:, :, :, :], 0.0))
            st.do(v.memset(VS[:, :, :, 8:9], 1.0))
            for b in range(B):
                dve.wait_ge(sem("qk_done"), b + 1)
                for which in range(2):
                    n = 2 * which
                    names = (("bq", "bqR"), ("bk", "bkR"))[which]
                    st.do(v.scalar_tensor_tensor(out=TMP[:, :], in0=PS[:, n, :], scalar=w(names[0]), in1=c("cos"),
                                                 op0=ALU.add, op1=ALU.mult))
                    st.do(v.scalar_tensor_tensor(out=TMP2[:, :], in0=PS[:, n + 1, :], scalar=w(names[1]), in1=c("sin"),
                                                 op0=ALU.add, op1=ALU.mult))
                    st.do(v.tensor_tensor(TMP[:, :], TMP[:, :], TMP2[:, :], ALU.add))
                    split3([PIE[3 * which + i][:, cols(b)] for i in range(3)], TMP[:, :], TMP2[:, :])\
                        .then_inc(sem("qk_pieces"), 1)
                    st.settle("qk_pieces")
                    dve.wait_ge(sem("qk_pieces"), 2 * b + which + 1)
                dve.wait_ge(sem("v_done"), b + 1)
                v.tensor_tensor(VS[:, half(b), :, 0:8], PS[:, 4 + b, :].rearrange("p (t h i) -> p t h i", t=HT, i=8),
                                bc(r("bv"), HT, 1).rearrange("p t (h i) -> p t h i", i=8), ALU.add).then_inc(sem("v_ready"), 1)
                st.settle("v_ready")

            def maxima(g, part):
                for un in range(4 * part, 4 * part + 4):
                    i = 8 * g + un
                    dve.wait_ge(sem("max_scores"), i + 1)
                    if un == 0 and g:
                        dve.wait_ge(sem("max_pieces"), g)
                    v.tensor_reduce(MX[:, 2 * (un % 2):2 * (un % 2) + 2, un // 2], PS[:, 2 * (i % 2):2 * (i % 2) + 2, :], AX.X,
                                    ALU.max, negate=True).then_inc(sem("max_done"), 1)
                    st.settle("max_done")

            def max_pieces(g):
                left = SM[:, 0:16].rearrange("p (t h) -> p t h", t=HT)
                if g:
                    dve.wait_ge(sem("max_turned"), g)
                split3([MPB[:, :, i, :] for i in range(3)], MX[:, :, :], left).then_inc(sem("max_pieces"), 1)
                st.settle("max_pieces")

            def max_rows(g):
                dve.wait_ge(sem("max_turned"), g + 1)
                if g >= 2:
                    dve.wait_ge(sem(f"max_stacked{g % 2}"), 16 * (g // 2))
                v.tensor_copy(MT[g % 2], PS[0:12, 7, 0:256].bitcast(BF16)).then_inc(sem("max_rows"), 1)
                st.settle("max_rows")

            def heads_copy(g):
                dve.wait_ge(sem("pv_done"), 4 * g + 4)
                v.tensor_copy(OT[:, :], PS[:, 6, :]).then_inc(sem("heads_copied"), 1)
                st.settle("heads_copied")

            def heads_out(g):
                b, g4 = g // 4, g % 4
                dve.wait_ge(sem("heads_turned"), g + 1)
                o = PS[:, 7, :].rearrange("p (t j r) -> p t j r", t=HT, r=32)
                rec = SM[:, 16:32].rearrange("p (t h) -> p t h", t=HT)
                st.do(v.reciprocal(rec, o[:, :, :, 8]))
                v.tensor_tensor(Y[:, half(b), 32 * g4:32 * g4 + 32].rearrange("p t (j i) -> p t j i", i=8),
                                o[:, :, :, 0:8], bc(rec, 8, 3), ALU.mult).then_inc(sem("heads_ready"), 1)
                st.settle("heads_ready")

            for g in range(2):
                maxima(g, 0)
                maxima(g, 1)
                max_pieces(g)
                max_rows(g)
            for b in range(B):
                dve.wait_ge(sem(f"spilled{b}"), 16 * 6)
            for g in range(8):
                if g < 6:
                    maxima(g + 2, 0)
                if g:
                    heads_out(g - 1)
                if g < 6:
                    maxima(g + 2, 1)
                    max_pieces(g + 2)
                    max_rows(g + 2)
                heads_copy(g)
            heads_out(7)
            for b in range(B):
                dve.wait_ge(sem("l1f_o"), b + 1)
                st.do(v.tensor_tensor(TMP[:, :].rearrange("p (t d) -> p t d", t=HT), tiles(b), bc(r("bo"), HT, 1), ALU.add))
                st.do(v.tensor_tensor(Y[:, half(b), :], TMP[:, :].rearrange("p (t d) -> p t d", t=HT), XH[:, half(b), :], ALU.add))
                st.do(ln(5, b, Y))
                gain(b, "g1", "be1").then_inc(sem("xh5"), 1)
                st.settle("xh5")
            dve.wait_ge(sem("xh5"), 2)
            moe(1, 0)
            for b in range(B):
                st.do(ln(6, b, ACC))
                st.do(gain(b, "g2", "be2"))
                add_to_x(b, XH[:, half(b), :], 5)
            for b in range(B):
                ln(7, b, X).then_inc(sem("xh7"), 1)
                st.settle("xh7")
            def tail2(t, o):
                v.tensor_tensor(TMP[:, 0:D], o, r("L2_bo"), ALU.add).then_inc(sem("o2_read"), 1)
                st.settle("o2_read")
                st.do(v.scalar_tensor_tensor(out=X[:, t, :], in0=TMP[:, 0:D], scalar=TG[:, 2:3], in1=X[:, t, :],
                                             op0=ALU.mult, op1=ALU.add))

            cross_tiles(2, 16, tail2)
            for b in range(B):
                ln(8, b, X).then_inc(sem("xh8"), 1)
                st.settle("xh8")
            dve.wait_ge(sem("xh8"), 2)
            moe(2, None)
            for b in range(B):
                add_to_x(b, ACC[:, half(b), :], 6)
                ln(9, b, X).then_inc(sem("xh9"), 1)
                st.settle("xh9")
            def tail3(t, o):
                v.tensor_tensor(TMP[:, 0:D], o, r("b_out"), ALU.add).then_inc(sem("o3_read"), 1)
                st.settle("o3_read")
                st.do(v.tensor_scalar(TMP[:, 0:D], TMP[:, 0:D], TG[:, 8:9], None, ALU.mult))
                st.do(v.scalar_tensor_tensor(out=X[:, t, :], in0=TMP[:, 0:D], scalar=TG[:, 3:4], in1=X[:, t, :],
                                             op0=ALU.mult, op1=ALU.add))

            cross_tiles(3, 16, tail3)
            for b in range(B):
                ln(10, b, X).then_inc(sem("xh10"), 1)
                st.settle("xh10")
            moe(3, 1)
            for b in range(B):
                v.scalar_tensor_tensor(out=X[:, half(b), :], in0=ACC[:, half(b), :], scalar=TG[:, 7:8],
                                       in1=X[:, half(b), :], op0=ALU.mult, op1=ALU.add).then_inc(sem("x_final"), 1)
                st.settle("x_final")

        @block.tensor
        def _(pe):
            mm, tp = nc.tensor.matmul, nc.tensor.transpose
            inputs_ready(pe)

            def turn(m, b, src, ready, value):
                pe.wait_ge(sem(ready), value)
                for j in range(HT):
                    ins = tp(PS[:, 6 + b, j * P:(j + 1) * P], src[:, HT * b + j, :], ident)
                ins.then_inc(sem("tp_done"), 1)

            def turned(m, b):
                pe.wait_ge(sem("tr_ready"), 2 * m + b + 1)

            def tile_of(a, b, j):
                return a[:, (HT * b + j) * P:(HT * b + j + 1) * P]

            def cross_kv(k, r, chunks, wk, wv, keys):
                lo, hi = 3 * r, min(3 * r + 3, chunks)
                if r:
                    pe.wait_ge(sem(f"kv{k}_raw"), r)
                for ch in range(lo, hi):
                    at = (ch - lo) * B * C
                    mm(PS[:, 6, at:at + B * C], wk[:, ch * D:(ch + 1) * D], keys, start=True, stop=True)
                    ins = mm(PS[:, 7, at:at + B * C], wv[:, ch * D:(ch + 1) * D], w("ctxT"), start=True, stop=True)
                ins.then_inc(sem(f"kv{k}_done"), 1)

            def cross_vw(k, n, units, wo):
                x = CROSS[k]
                b, u = n // units, n % units
                if n == 0:
                    pe.wait_ge(sem(f"kv{k}_masked"), 1)
                    pe.wait_ge(sem(f"kv{k}_raw"), 1 if k < 3 else 3)
                else:
                    pe.wait_ge(sem(f"vw{k}_ready"), n)
                for i in range(UB):
                    out_i = PS[:, 6, i * D:(i + 1) * D] if i < 3 else PS[:, 7, (i - 3) * D:(i - 2) * D]
                    if k < 3:
                        ins = mm(out_i, x["vt"][0][:, b, u, i * P:(i + 1) * P], wo, start=True, stop=True)
                        continue
                    pairs = sorted({min(i * P // (2 * C), 3), min((i * P + P - 1) // (2 * C), 3)})
                    for pair in pairs:
                        ch = 4 * u + pair
                        ins = mm(out_i, x["vt"][ch % 2][:, b, u, i * P:(i + 1) * P], wo[:, ch * D:(ch + 1) * D],
                                 start=(pair == pairs[0]), stop=(pair == pairs[-1]))
                ins.then_inc(sem(f"vw{k}_done"), 1)

            def cross_tiles(k, heads, chunks, wq):
                x = CROSS[k]
                per = heads // 8
                units = NT * per
                first = B if chunks == 1 else chunks

                def query(j, bank):
                    mm(PS[:, bank, :], wq[:, (j % chunks) * D:(j % chunks + 1) * D], HTR[:, cols(j // chunks)],
                       start=True, stop=True).then_inc(sem(f"q{k}_done"), 1)

                for j in range(first):
                    query(j, j)
                pe.wait_ge(sem(f"q{k}_ready"), first)
                pe.wait_ge(sem(f"vw{k}_ready"), B * per)
                pe.wait_ge(sem("pads_ready"), k)
                for s in range(units + 3):
                    if s < units:
                        t, hh = s // per, s % per
                        b, j = t // HT, t % HT
                        if chunks > 1 and b:
                            pe.wait_ge(sem(f"q{k}_ready"), B * chunks)
                        if s >= 2:
                            pe.wait_ge(sem(f"s{k}_shifted"), s - 1)
                        for n in range(2):
                            h0 = 8 * hh + 4 * n
                            if chunks == 1:
                                ins = mm(PS[:, 2 * (s % 2) + n, 0:4 * C], x["qc"][:, b, 0, j * P:(j + 1) * P],
                                         x["kt"][:, b, h0:h0 + 4, :].rearrange("p h k -> p (h k)"), start=True, stop=True)
                                continue
                            for m in range(2):
                                ins = mm(PS[:, 2 * (s % 2) + n, m * 2 * C:(m + 1) * 2 * C],
                                         x["qc"][:, b, h0 // 2 + m, j * P:(j + 1) * P],
                                         x["kt"][:, b, h0 + 2 * m:h0 + 2 * m + 2, :].rearrange("p h k -> p (h k)"),
                                         start=True, stop=True)
                        ins.then_inc(sem(f"s{k}_done"), 1)
                    if chunks > 1 and s < chunks:
                        if s:
                            pe.wait_ge(sem(f"q{k}_ready"), chunks + s)
                        query(chunks + s, 6)
                    if 2 <= s < units + 2:
                        u = s - 2
                        pe.wait_ge(sem(f"p{k}_normed"), u + 1)
                        for i in range(UB):
                            n = i // 3
                            if u and i in (0, 3):
                                pe.wait_ge(sem(f"pt{k}_ready"), 2 * (u - 1) + n + 1)
                            ins = tp(PS[:, 4 + n, (i - 3 * n) * P:(i - 3 * n + 1) * P], x["sc"][u % 3][:, i * P:(i + 1) * P], ident)
                            if i in (2, 4):
                                ins.then_inc(sem(f"p{k}_turned"), 1)
                    if s >= 3:
                        u = s - 3
                        t, hh = u // per, u % per
                        pe.wait_ge(sem(f"pt{k}_ready"), 2 * u + 2)
                        if t and hh == 0:
                            pe.wait_ge(sem(f"o{k}_read"), t)
                        for i in range(UB):
                            ins = mm(PS[:, 7, 0:D], x["pt"][u % 2][:, i * P:(i + 1) * P], x["vw"][:, t // HT, hh, i, :],
                                     start=(hh == 0 and i == 0), stop=(hh == per - 1 and i == UB - 1))
                        ins.then_inc(sem(f"pv{k}_done"), 1)

            for b in range(B):
                ct = w("ctxT")[:, b * C:(b + 1) * C]
                mm(PS[0:C, b, 0:D], ct, w("L0_WkT"), start=True, stop=True)
                mm(PS[0:C, b, D:2 * D], ct, w("L0_WvT"), start=True, stop=True).then_inc(sem("l0_kv"), 1)
            for b in range(B):
                turn(0, b, XH, "xh0", b + 1)
            for b in range(B):
                turned(0, b)
                for j in range(HT):
                    ins = mm(PS[:, 4 + b, j * P:(j + 1) * P], tile_of(HTR, b, j), w("L0_WqT"), start=True, stop=True)
                ins.then_inc(sem("l0_q"), 1)
            for b in range(B):
                pe.wait_ge(sem("l0_k_ready"), b + 1)
                mm(PS[:, 2 + b, 0:D + 1], KF[:, b, :], VA[:, b, 0:D + 1], start=True, stop=True).then_inc(sem("l0_sums"), 1)
            for b in range(B):
                turn(1, b, QF, "qf_ready", b + 1)
            for b in range(B):
                turned(1, b)
                pe.wait_ge(sem("l0_state_ready"), 2)
                for j in range(HT):
                    ins = mm(PS[:, 2 * b + j // 2, (j % 2) * 256:(j % 2) * 256 + D + 16], tile_of(QT, b, j), KVM[:, b, :],
                             start=True, stop=True)
                ins.then_inc(sem("l0_y"), 1)
            for b in range(B):
                turn(2, b, Y, "y_ready", b + 1)
            for b in range(B):
                turned(2, b)
                for j in range(HT):
                    ins = mm(PS[:, 4 + b, j * P:(j + 1) * P], tile_of(YT, b, j), w("L0_WpT"), start=True, stop=True)
                ins.then_inc(sem("l0_o"), 1)
            for b in range(B):
                turn(3, b, XH, "xn_ready", b + 1)
            for b in range(B):
                turned(3, b)
                mm(PS[0:E0, b, :], w("L0_routerT"), HTR[:, cols(b)], start=True, stop=True).then_inc(sem("l0_logits"), 1)
            pe.wait_ge(sem("l0_logits_ready"), 2)
            for t in range(NT):
                ins = tp(PS[:, 2, t * E0:(t + 1) * E0], LG[:, t * P:(t + 1) * P], ident[0:E0, 0:E0])
            ins.then_inc(sem("l0_logits_turned"), 1)
            pe.wait_ge(sem("ctx_normed"), 1)
            for b in range(B):
                ins = tp(PS[:, 5, b * C:(b + 1) * C], CTXH[:, b, :], ident[0:C, 0:C])
            ins.then_inc(sem("ctx_turned"), 1)
            pe.wait_ge(sem("ctxn_ready"), 1)
            cross_kv(1, 0, 1, w("L1x_Wk"), w("L1x_Wv"), CTXN[:, :])
            pe.wait_ge(sem("places_ready"), 1)
            for t in range(NT):
                ins = tp(PS[:, 3, t * E0:(t + 1) * E0], CUM[:, t * P:(t + 1) * P], ident[0:E0, 0:E0])
            ins.then_inc(sem("places_turned"), 1)
            pe.wait_ge(sem("xp_ready"), 1)
            for n in range(2):
                for t in range(NT):
                    pe.wait_ge(sem("slots_ready"), t + 1)
                    for i in range(3):
                        ins = mm(PS[:, 4 + n, :], XP[:, t, i, :], S0[:, t, cols(n)], start=(t == 0 and i == 0),
                                 stop=(t == NT - 1 and i == 2))
                ins.then_inc(sem("gathered"), 1)
            pe.wait_ge(sem("shares_ready"), 1)
            for n in range(2):
                for t in range(NT):
                    ins = mm(PS[0:48, n, :], WP[:, t, :, :].rearrange("p i e -> p (i e)"), S0[:, t, cols(n)],
                             start=(t == 0), stop=(t == NT - 1))
                ins.then_inc(sem("shares_gathered"), 1)
            pe.wait_ge(sem("idb_ready"), 1)
            for q in range(PAIRS):
                if q >= 2:
                    pe.wait_ge(sem("slots_turned_ready"), q - 1)
                for t in range(NT):
                    ins = tp(PS[:, 2 + q % 2, :].bitcast(BF16)[:, t * P:(t + 1) * P], S0[:, t, q * P:(q + 1) * P], IDB[:, :])
                ins.then_inc(sem("slots_turned"), 1)
            for n in range(B):
                cross_vw(1, n, 1, ident)
            pe.wait_ge(sem("vw1_ready"), B)
            pe.wait_ge(sem("shares_own"), 2)
            for q in range(PAIRS):
                ins = mm(PS[:, 7, q:q + 1], GM48[:, q * P:(q + 1) * P], c("iota", 48)[:, 0:1], start=True, stop=True)
            ins.then_inc(sem("shares_turned"), 1)
            pe.wait_ge(sem("slots_turned_ready"), PAIRS)
            pe.wait_ge(sem("gathered_ready"), 2)

            def hidden0(q):
                sel = c("pairsel", E0)[:, q * P:(q + 1) * P]
                for j in range(2):
                    mm(PS[64 * j:64 * j + 64, q % 2, :], sel[:, 64 * j:64 * j + 64], B0[:, 0:F], start=True, stop=False)
                for j in range(2):
                    n = 2 * q + j
                    expert_ready(pe, n)
                    ins = mm(PS[64 * j:64 * j + 64, q % 2, :], XET[:, n * SLOTS:(n + 1) * SLOTS],
                             RINGW[:, n % RING, 0:F], start=False, stop=True)
                ins.then_inc(sem("l0_hidden"), 1)

            hidden0(0)
            for q in range(PAIRS):
                pe.wait_ge(sem("l0_gelu"), q + 1)
                for ch in range(FC):
                    ins = tp(PS[:, 2, ch * P:(ch + 1) * P], HS[:, ch * P:(ch + 1) * P], ident)
                ins.then_inc(sem("l0_hidden_turned"), 1)
                if q + 1 < PAIRS:
                    hidden0(q + 1)
                pe.wait_ge(sem("l0_hidden_ready"), q + 1)
                if q:
                    pe.wait_ge(sem("yp_ready"), q)
                sel = c("pairsel", E0)[:, q * P:(q + 1) * P]
                for j in range(2):
                    mm(PS[64 * j:64 * j + 64, 3, 0:D], sel[:, 64 * j:64 * j + 64], B0[:, F:F + D], start=True, stop=False)
                for ch in range(FC):
                    for j in range(2):
                        n = 2 * q + j
                        ins = mm(PS[64 * j:64 * j + 64, 3, 0:D], HST[:, ch * P + 64 * j:ch * P + 64 * j + 64],
                                 RINGW[:, n % RING, F + ch * D:F + (ch + 1) * D], start=False, stop=(ch == FC - 1))
                ins.then_inc(sem("expert_used"), 2)
            pe.wait_ge(sem("yp_ready"), PAIRS)
            for t in range(NT):
                for q in range(PAIRS):
                    for i in range(3):
                        ins = mm(PS[:, 4 + t // HT, (t % HT) * D:(t % HT + 1) * D], S0T[:, q, t * P:(t + 1) * P],
                                 YP[:, q, i, :], start=(q == 0 and i == 0), stop=(q == PAIRS - 1 and i == 2))
                if t % HT == HT - 1:
                    ins.then_inc(sem("scattered"), 1)

            def moe(k, router_w, n, second):
                m = {1: 8, 2: 10, 3: 12}[k]
                turned(m, 1)
                for t in range(NT):
                    ins = mm(PS[:, 4, t * 16:t * 16 + n], HTR[:, t * P:(t + 1) * P], router_w, start=True, stop=True)
                ins.then_inc(sem("router_done"), 1)

                def hidden(i):
                    g, slot = 16 * (k - 1) + i, (E0 + E * (k - 1) + i // 2) % RING
                    if i % 2 == 0:
                        expert_ready(pe, E0 + E * (k - 1) + i // 2)
                    for ch in range(FC):
                        if g >= 1:
                            pe.wait_ge(sem("moe_gelu"), 4 * (g - 1) + ch + 1)
                        mm(PS[:, ch, :], RINGW[:, slot, ch * P:(ch + 1) * P], HTR[:, cols(i % 2)], start=True, stop=True)\
                            .then_inc(sem("moe_hidden"), 1)

                hidden(0)
                for i in range(2 * E):
                    g, slot = 16 * (k - 1) + i, (E0 + E * (k - 1) + i // 2) % RING
                    if i + 1 < 2 * E:
                        hidden(i + 1)
                    pe.wait_ge(sem("moe_gelu"), 4 * g + 4)
                    pe.wait_ge(sem("comb_ready"), k)
                    if i >= 2:
                        pe.wait_ge(sem("moe_summed"), g - 1)
                    for j in range(HT):
                        for ch in range(FC):
                            ins = mm(PS[:, 4 + g % 2, j * D:(j + 1) * D], HB[g % 2][:, ch, j * P:(j + 1) * P],
                                     RINGW[:, slot, F + ch * D:F + (ch + 1) * D], start=(ch == 0), stop=(ch == FC - 1))
                    ins.then_inc(sem("moe_out"), 1)
                    if i % 2:
                        pe.wait_ge(sem("moe_out"), g + 1)
                        nc.tensor.nop().then_inc(sem("expert_used"), 1)
                    if i == 7 and second is not None:
                        for b in range(B):
                            for j in range(HT):
                                ins = tp(PS[0:E, 6 + b, j * P:(j + 1) * P], GC[:, HT * b + j, 0:E], ident)
                            ins.then_inc(sem("comb_turned"), 1)
                        for b in range(B):
                            pe.wait_ge(sem("combt_ready"), 2 * second + b + 1)
                            for j in range(HT):
                                ins = mm(PS[:, 6 + b, j * D:(j + 1) * D], COMBT[0:E, (HT * b + j) * P:(HT * b + j + 1) * P],
                                         B2[:, second, :], start=True, stop=True)
                            ins.then_inc(sem("moe_bias"), 1)
                    if k < 3:
                        chunks = 1 if k == 1 else 8
                        if i == 8 and second is not None:
                            pe.wait_ge(sem("bias_added"), 2)
                        if 0 <= i - 8 < (chunks + 2) // 3:
                            wk, wv = (("L2x_Wk", "L2x_Wv"), ("L3x_wk", "L3x_wv"))[k - 1]
                            cross_kv(k + 1, i - 8, chunks, w(wk), w(wv), w("ctxT"))
                        if i >= 12:
                            cross_vw(k + 1, i - 12, 2, w(("L2x_Wo", "L3x_wout")[k - 1]))
                if k < 3:
                    pe.wait_ge(sem(f"vw{k + 1}_ready"), 4)

            for b in range(B):
                turn(4, b, XH, "xh2", b + 1)
            turned(4, 1)
            cross_tiles(1, 8, 1, w("L1x_Wq"))
            for b in range(B):
                turn(5, b, XH, "xh3", b + 1)
            for b in range(B):
                turned(5, b)
                for j in range(HT):
                    ins = mm(PS[:, b, j * D:(j + 1) * D], tile_of(YT, b, j), w("L1x_Wo"), start=True, stop=True)
                ins.then_inc(sem("l1_wo"), 1)
            for b in range(B):
                turn(6, b, XH, "xh4", b + 1)
            for b in range(B):
                turned(6, b)
                if b:
                    pe.wait_ge(sem("qk_pieces"), 2)
                for n, name in enumerate(("L1f_Wq", "L1f_WqR", "L1f_Wk", "L1f_WkR")):
                    ins = mm(PS[:, n, :], w(name), HTR[:, cols(b)], start=True, stop=True)
                ins.then_inc(sem("qk_done"), 1)
                for j in range(HT):
                    ins = mm(PS[:, 4 + b, j * D:(j + 1) * D], tile_of(HTR, b, j), w("L1f_Wv"), start=True, stop=True)
                ins.then_inc(sem("v_done"), 1)

            def max_scores(g, units):
                b = g // 4
                for un in units:
                    i = 8 * g + un
                    h = 4 * (g % 4) + un // 2
                    if un == 0 and g % 4 == 0:
                        pe.wait_ge(sem(f"stacked{b}"), 16 * 18)
                        pe.wait_ge(sem("qk_pieces"), 4)
                    if i >= 2:
                        pe.wait_ge(sem("max_done"), i - 1)
                    for x in range(2):
                        q0 = N * b + (2 * (un % 2) + x) * P
                        ins = mm(PS[:, 2 * (i % 2) + x, :], QS[0:72, h, q0:q0 + P], KS[0:72, h, cols(b)], start=True, stop=True)
                    ins.then_inc(sem("max_scores"), 1)

            def turn_max(g):
                pe.wait_ge(sem("max_pieces"), g + 1)
                if g == 1:
                    pe.wait_ge(sem("max_rows"), 1)
                if g >= 3:
                    pe.wait_ge(sem("heads_ready"), g - 2)
                for t in range(HT):
                    ins = tp(PS[0:12, 7, 0:256].bitcast(BF16)[:, t * P:(t + 1) * P],
                             MPB[:, t, :, :].rearrange("p i h -> p (i h)"), IDB[:, :])
                ins.then_inc(sem("max_turned"), 1)

            def attend(g, kt):
                b = g // 4
                if g % 4 == 0 and kt == 0:
                    pe.wait_ge(sem("v_ready"), 2)
                    pe.wait_ge(sem("ones_stacked"), 16)
                if kt == 0:
                    pe.wait_ge(sem(f"max_stacked{g % 2}"), 16 * (g // 2 + 1))
                for j in range(4):
                    idx = 16 * g + 4 * kt + j
                    h = 4 * (g % 4) + j
                    if idx >= 2:
                        pe.wait_ge(sem("probs"), idx - 1)
                    k0 = N * b + kt * P
                    mm(PS[:, 4 + idx % 2, :], KS[0:75, h, k0:k0 + P], QS[0:75, h, cols(b)], start=True, stop=True)\
                        .then_inc(sem("scores"), 1)

            def values(g, kt):
                b = g // 4
                pe.wait_ge(sem("probs"), 16 * g + 4 * kt + 4)
                if g and kt == 0:
                    pe.wait_ge(sem("heads_copied"), g)
                for j in range(4):
                    idx = 16 * g + 4 * kt + j
                    ins = mm(PS[32 * j:32 * j + 32, 6, :], VS[:, HT * b + kt, 4 * (g % 4) + j, :], PR[idx % 8],
                             start=(kt == 0), stop=(kt == 3))
                ins.then_inc(sem("pv_done"), 1)

            def turn_heads(g):
                pe.wait_ge(sem("heads_copied"), g + 1)
                pe.wait_ge(sem("max_rows"), min(g + 3, 8))
                for t in range(HT):
                    ins = tp(PS[:, 7, t * P:(t + 1) * P], OT[:, t * P:(t + 1) * P], ident)
                ins.then_inc(sem("heads_turned"), 1)

            for g in range(2):
                max_scores(g, range(8))
                turn_max(g)
            for g in range(8):
                for kt in range(4):
                    if g < 6:
                        max_scores(g + 2, ((0, 1, 2), (3, 4, 5), (6, 7), ())[kt])
                    attend(g, kt)
                    if kt:
                        values(g, kt - 1)
                    if g and kt == 1:
                        turn_heads(g - 1)
                if g < 6:
                    turn_max(g + 2)
                values(g, 3)
            turn_heads(7)
            for b in range(B):
                turn(7, b, Y, "heads_ready", 4 * b + 4)
            for b in range(B):
                turned(7, b)
                for j in range(HT):
                    ins = mm(PS[:, b, j * D:(j + 1) * D], tile_of(YT, b, j), w("L1f_Wo"), start=True, stop=True)
                ins.then_inc(sem("l1f_o"), 1)
            for b in range(B):
                turn(8, b, XH, "xh5", b + 1)
            moe(1, w("L1f_Wg"), E, 0)
            for b in range(B):
                turn(9, b, XH, "xh7", b + 1)
            turned(9, 1)
            cross_tiles(2, 16, 1, w("L2x_Wq"))
            for b in range(B):
                turn(10, b, XH, "xh8", b + 1)
            moe(2, w("L2f_router"), E + 1, None)
            for b in range(B):
                turn(11, b, XH, "xh9", b + 1)
            turned(11, 1)
            cross_tiles(3, 16, 8, w("L3x_wq"))
            for b in range(B):
                turn(12, b, XH, "xh10", b + 1)
            moe(3, w("L3f_router"), E, 1)


def kernel(**inputs):
    import concourse.bacc as bacc
    from concourse.bass_utils import run_bass_kernel_spmd as run

    a = {n: np.asarray(x) for n, x in inputs.items()}
    turn = np.array([8 * (i // 8) + (i % 8 + 4) % 8 for i in range(D)])

    def chunked(m):
        return m.reshape(-1, P, m.shape[1]).transpose(1, 0, 2).reshape(P, -1)

    def col(vec):
        return vec.reshape(-1, 1)

    parts = {
        "L0_WqT": a["L0_xattn_Wq"].T, "L0_WkT": a["L0_xattn_Wk"].T, "L0_WvT": a["L0_xattn_Wv"].T,
        "L0_WpT": a["L0_xattn_Wp"].T, "L0_routerT": a["L0_ffn_router_weight"].T,
        "L1x_Wq": a["L1_xattn_Wq"], "L1x_Wk": a["L1_xattn_Wk"], "L1x_Wv": a["L1_xattn_Wv"], "L1x_Wo": a["L1_xattn_Wo"],
        "L1f_Wq": a["L1_ffn_Wq"], "L1f_WqR": a["L1_ffn_Wq"][:, turn], "L1f_Wk": a["L1_ffn_Wk"],
        "L1f_WkR": a["L1_ffn_Wk"][:, turn], "L1f_Wv": a["L1_ffn_Wv"], "L1f_Wo": a["L1_ffn_Wo"], "L1f_Wg": a["L1_ffn_Wg"],
        "L2x_Wq": a["L2_xattn_W_q"], "L2x_Wk": a["L2_xattn_W_k"], "L2x_Wv": a["L2_xattn_W_v"], "L2x_Wo": a["L2_xattn_W_o"],
        "L2f_router": a["L2_ffn_router_w"],
        "L3x_wq": a["L3_xattn_w_q"], "L3x_wk": a["L3_xattn_w_kv"][:, :1024], "L3x_wv": a["L3_xattn_w_kv"][:, 1024:],
        "L3x_wout": chunked(a["L3_xattn_w_out"]), "L3f_router": a["L3_ffn_w_router"],
        "pre_g": col(a["L1_xattn_pre_g"]), "pre_b": col(a["L1_xattn_pre_b"]),
        "L3_gamma": col(a["L3_xattn_ln_gamma"]), "L3_beta": col(a["L3_xattn_ln_beta"]),
        "bq": col(a["L1_ffn_bq"]), "bqR": col(a["L1_ffn_bq"][turn]), "bk": col(a["L1_ffn_bk"]), "bkR": col(a["L1_ffn_bk"][turn]),
        "L1_b1": a["L1_ffn_b1"].reshape(E * FC, P).T, "L3_b1": a["L3_ffn_b1"].reshape(E * FC, P).T,
        "ctxT": a["ctx_1024"].reshape(B * C, D).T,
    }
    rows = {
        "g_xattn": a["g_xattn"], "g_ffn": a["g_ffn"], "gate": a["L3_xattn_gate"], "focus": a["L0_xattn_focusing_factor"].reshape(1),
        "norm_weight": a["L0_ffn_norm_weight"], "ln_g": a["L1_xattn_ln_g"], "ln_b": a["L1_xattn_ln_b"],
        "bv": a["L1_ffn_bv"], "bo": a["L1_ffn_bo"], "g1": a["L1_ffn_g1"], "be1": a["L1_ffn_be1"],
        "g2": a["L1_ffn_g2"], "be2": a["L1_ffn_be2"], "bg": a["L1_ffn_bg"], "L2_bo": a["L2_xattn_b_o"],
        "L2_router_b": a["L2_ffn_router_b"], "b_out": a["L3_xattn_b_out"],
    }

    def experts(w1, w2):
        n = w1.shape[0]
        second = w2.reshape(n, FC, P, D).transpose(0, 2, 1, 3).reshape(n, P, FC * D)
        return np.concatenate([w1, second], 2)

    arrays = {
        "wpack": np.concatenate([parts[n] for n, _ in W_PARTS], 1),
        "rpack": np.concatenate([rows[n] for n, _ in R_PARTS])[None],
        "cpack": shape_constants(),
        "ones": np.full((3, 16 * T // 2), 0x3F803F80, np.uint32).view(np.float32),
        "ctx_rows": a["ctx_1024"].transpose(1, 0, 2),
        "x": a["x"].reshape(NT, P, D).transpose(1, 0, 2),
        "up0": experts(a["L0_ffn_fc1_weight"].transpose(0, 2, 1), a["L0_ffn_fc2_weight"].transpose(0, 2, 1)),
        "up": np.concatenate([experts(a["L1_ffn_W1"], a["L1_ffn_W2"]), experts(a["L2_ffn_w1"], a["L2_ffn_w2"]),
                              experts(a["L3_ffn_w1"], a["L3_ffn_w2"])]),
        "b_l0": np.concatenate([a["L0_ffn_fc1_bias"], a["L0_ffn_fc2_bias"], a["L0_ffn_router_bias"][:, None]], 1),
        "b2_l1": a["L1_ffn_b2"], "b2_l3": a["L3_ffn_b2"],
    }
    nc = bacc.Bacc("TRN2", target_bir_lowering=False, num_devices=1)
    arrays = {n: np.ascontiguousarray(x) for n, x in arrays.items()}
    t = {n: nc.dram_tensor(n, x.shape, F32, kind="ExternalInput").ap() for n, x in arrays.items()}
    out = nc.dram_tensor("out", (P, NT, D), F32, kind="ExternalOutput").ap()
    scratch = nc.dram_tensor("scratch", (6, P, T), BF16).ap()
    build(nc, t["wpack"], t["rpack"], t["cpack"], t["ones"], t["ctx_rows"], t["x"], t["up0"], t["up"], t["b_l0"],
          t["b2_l1"], t["b2_l3"], scratch, out)
    r = run(nc, [arrays], core_ids=[0])
    return r.results[0]["out"].transpose(1, 0, 2).reshape(B, N, D)
```

```python
from contextlib import ExitStack

import numpy as np
import concourse.bass as bass
from concourse import mybir

F32 = mybir.dt.float32
BF16 = mybir.dt.bfloat16
ALU = mybir.AluOpType
ACT = mybir.ActivationFunctionType
AX = mybir.AxisListType

P = 128
D = 128
B = 2
N = 512
T = B * N
NT = T // P
HT = NT // B
C = 77
F = 512
FC = F // P
SLOTS = 64
E0 = 16
E = 8
PAIRS = E0 // 2
KEEP = 5
EPS = 1e-5
RING = 6
UB = 5
UW = UB * P
UK = 8 * C
CROSS_KEPT = 12000
NEG = -3.0e38

W_PARTS = [("ctxT", B * C), ("L0_WqT", D), ("L0_WkT", D), ("L0_WvT", D), ("L0_WpT", D), ("L0_routerT", E0),
           ("L1x_Wq", D), ("L1x_Wk", D), ("L1x_Wv", D), ("L1x_Wo", D),
           ("L1f_Wq", D), ("L1f_WqR", D), ("L1f_Wk", D), ("L1f_WkR", D), ("L1f_Wv", D), ("L1f_Wo", D),
           ("L1f_Wg", E), ("L2x_Wq", D), ("L2x_Wk", D), ("L2x_Wv", D), ("L2x_Wo", D), ("L2f_router", E + 1),
           ("L3x_wq", 1024), ("L3x_wk", 1024), ("L3x_wv", 1024), ("L3x_wout", 1024), ("L3f_router", E),
           ("pre_g", 1), ("pre_b", 1), ("L3_gamma", 1), ("L3_beta", 1),
           ("bq", 1), ("bqR", 1), ("bk", 1), ("bkR", 1),
           ("L1_b1", E * FC), ("L3_b1", E * FC)]
R_PARTS = [("g_xattn", 4), ("g_ffn", 4), ("gate", 1), ("focus", 1), ("norm_weight", D), ("ln_g", D), ("ln_b", D),
           ("bv", D), ("bo", D), ("g1", D), ("be1", D), ("g2", D), ("be2", D), ("bg", E),
           ("L2_bo", D), ("L2_router_b", E + 1), ("b_out", D)]
C_PARTS = [("ident", P), ("mask16", 16), ("mask8", 8), ("mask2", 2), ("blocks", D), ("order8", 8), ("order9", 9),
           ("cos", N), ("sin", N), ("iota", SLOTS), ("diag", T), ("pairsel", PAIRS * P)]


def columns(parts):
    at, out = 0, {}
    for name, n in parts:
        out[name] = (at, n)
        at += n
    return out, at


W_AT, W_COLS = columns(W_PARTS)
W_FIRST = W_AT["L1x_Wq"][0]
R_AT, R_COLS = columns(R_PARTS)
C_AT, C_COLS = columns(C_PARTS)
C_FIRST = C_AT["cos"][0]


def shape_constants():
    c = np.zeros((P, C_COLS), np.float32)

    def put(name, a):
        at, n = C_AT[name]
        c[0:a.shape[0], at:at + n] = a

    p = np.arange(P)
    put("ident", np.eye(P))
    put("mask16", p[:, None] // 8 == np.arange(16)[None])
    put("mask8", p[:, None] // 16 == np.arange(8)[None])
    put("mask2", p[:, None] // 64 == np.arange(2)[None])
    put("blocks", p[:, None] // 8 == p[None] // 8)
    put("order8", np.tile(7 - np.arange(8), (P, 1)))
    put("order9", np.tile(8 - np.arange(9), (P, 1)))
    inv = 1.0 / 10000.0 ** (np.arange(0, 8, 2, dtype=np.float32) / np.float32(8))
    freqs = np.arange(N, dtype=np.float32)[:, None] * inv.astype(np.float32)[None]
    emb = np.concatenate([freqs, freqs], -1).astype(np.float32)
    sign = np.where(np.arange(8) < 4, -1.0, 1.0)
    put("cos", np.repeat(np.cos(emb).T, 16, 0))
    put("sin", np.repeat((np.sin(emb) * sign).T, 16, 0))
    put("iota", np.tile(1 + np.arange(SLOTS), (P, 1)))
    slot_expert = np.arange(T) // SLOTS
    put("diag", np.tile(np.arange(E0)[:, None] == slot_expert[None], (3, 1)))
    sel = np.zeros((E0, PAIRS, P))
    for pair in range(PAIRS):
        for m in range(P):
            sel[2 * pair + m // SLOTS, pair, m] = 1
    put("pairsel", sel.reshape(E0, PAIRS * P))
    return c


def build(nc, wpack, rpack, cpack, ones_in, ctx_rows, x_in, up0, up, b_l0, b2_l1, b2_l3, scratch, out):
    with ExitStack() as ctx:
        def sb(name, shape, dt=F32):
            return ctx.enter_context(nc.sbuf_tensor(name, shape, dt))

        sems = {}

        def sem(name):
            if name not in sems:
                sems[name] = ctx.enter_context(nc.semaphore(name))
            return sems[name]

        Wt = sb("Wt", [P, W_COLS])
        Rt = sb("Rt", [P, R_COLS])
        Ct = sb("Ct", [P, C_COLS])
        CX = sb("CX", [C, B, D])
        B0 = sb("B0", [E0, F + D + 1])
        B2 = sb("B2", [E, 2, D])
        RINGW = sb("RINGW", [P, RING, 2 * F])

        X = sb("X", [P, NT, D])
        XH = sb("XH", [P, NT, D])
        HTR = sb("HTR", [P, T])
        Y = sb("Y", [P, NT, D])
        YT = sb("YT", [P, T])
        ACC = sb("ACC", [P, NT, D])
        TG = sb("TG", [P, 9])
        ST6 = sb("ST6", [P, NT, 6])
        MV = sb("MV", [P, NT, 2])
        RS = sb("RS", [P, NT, 1])
        HALFNEG = sb("HALFNEG", [P, HT])
        REC = sb("REC", [P, 4, 8])
        NTOP = sb("NTOP", [P, 2, 8])
        CTXH = sb("CTXH", [C, B, D])
        CTXN = sb("CTXN", [P, B * C])
        OT = sb("OT", [P, N])
        GL = sb("GL", [P, NT, 16])
        GM = sb("GM", [P, NT, 16])
        GR = sb("GR", [P, NT, 16])
        GC = sb("GC", [P, NT, 16])
        GS = sb("GS", [P, NT, 16])
        G1 = sb("G1", [P, NT])
        G2 = sb("G2", [P, NT])
        COMBT = sb("COMBT", [16, T])
        TMP = sb("TMP", [P, N])
        TMP2 = sb("TMP2", [P, N])
        RK = sb("RK", [P, N])
        RG = sb("RG", [P, N])
        SM = sb("SM", [P, 64])
        BIG = sb("BIG", [P, 22528])
        PS = ctx.enter_context(nc.psum_tensor("PS", [P, 8, 512], F32))

        def w(name, a=0, b=None):
            at, n = W_AT[name]
            return Wt[:, at + a:at + (n if b is None else b)]

        def r(name, rows=P):
            at, n = R_AT[name]
            return Rt[0:rows, at:at + n]

        def c(name, rows=P):
            at, n = C_AT[name]
            return Ct[0:rows, at:at + n]

        ident = c("ident")
        big_at = [0]

        def big(rows, cols, dt=F32):
            n = cols if dt == F32 else (cols + 1) // 2
            a = BIG[0:rows, big_at[0]:big_at[0] + n]
            big_at[0] += n
            assert big_at[0] <= 22528, big_at[0]
            return a if dt == F32 else a.bitcast(dt)

        big_at[0] = 0
        KF = big(C, B * D).rearrange("p (b d) -> p b d", b=B)
        FT = [[big(rows, n) for _ in range(2)] for rows, n in ((C, B * D), (P, N), (P, N))]
        VA = big(C, B * (D + 2)).rearrange("p (b d) -> p b d", b=B)
        KVM = big(P, B * (D + 16)).rearrange("p (b d) -> p b d", b=B)
        QF = big(P, T).rearrange("p (t d) -> p t d", t=NT)
        QT = big(P, T)
        big_at[0] = 0
        LG = big(E0, T)
        LW = big(E0, T)
        CUM = big(E0, T)
        ONESR = big(E0, T)
        M8 = big(E0, 8)
        S0 = big(P, NT * T, BF16).rearrange("p (t s) -> p t s", t=NT)
        S0T = big(P, PAIRS * T, BF16).rearrange("p (q t) -> p q t", q=PAIRS)
        XP = big(P, NT * 3 * D, BF16).rearrange("p (t i d) -> p t i d", t=NT, i=3)
        WP = big(P, NT * 48, BF16).rearrange("p (t i e) -> p t i e", t=NT, i=3)
        XET = YT
        GM48 = big(48, T)
        GSL = big(P, PAIRS)
        HS = XH[:, 0:HT, :].rearrange("p t d -> p (t d)")
        HST = XH[:, HT:NT, :].rearrange("p t d -> p (t d)")
        YP = big(P, PAIRS * 3 * D, BF16).rearrange("p (q i d) -> p q i d", q=PAIRS, i=3)

        def cross_buffers(at, tiles_at, k, heads, chunks):
            units = heads // 8
            big_at[0] = at
            vt = [big(P, B * units * UW).rearrange("p (b u w) -> p b u w", b=B, u=units) for _ in range(2 if k == 3 else 1)]
            raw = [big(P, chunks * B * C).rearrange("p (c b k) -> p c b k", c=chunks, b=B) for _ in range(2)]
            end = big_at[0]
            if k > 1:
                big_at[0] = CROSS_KEPT
            kt = big(P, B * heads * C).rearrange("p (b h k) -> p b h k", b=B, h=heads)
            vw = big(P, B * units * UW).rearrange("p (b u i d) -> p b u i d", b=B, u=units, i=UB)
            if k == 1:
                big_at[0] = 0
            sc = [big(P, UW) for _ in range(4)]
            pt = [big(P, UW) for _ in range(3)]
            if k > 1:
                assert end <= CROSS_KEPT
                big_at[0] = 0
            qc = big(P, chunks * T).rearrange("p (b c n) -> p b c n", b=B, c=chunks)
            return dict(vt=vt, raw=raw, kt=kt, vw=vw, sc=sc, pt=pt, qc=qc)

        CROSS = {1: cross_buffers(16592, 0, 1, 8, 1), 2: cross_buffers(FC * N * 2, 0, 2, 16, 1),
                 3: cross_buffers(FC * N * 2, 0, 3, 16, 8)}
        big_at[0] = 0
        QS = big(75, 16 * T, BF16).rearrange("p (h t) -> p h t", h=16)
        KS = big(75, 16 * T, BF16).rearrange("p (h t) -> p h t", h=16)
        VS = big(P, NT * 16 * 32).rearrange("p (t h d) -> p t h d", t=NT, h=16)
        flat_y = Y[:, :, :].rearrange("p t d -> p (t d)")
        flat_acc = ACC[:, :, :].rearrange("p t d -> p (t d)")
        PIE = [a[:, n * 512:(n + 1) * 512].bitcast(BF16) for a in (flat_y, YT[:, :], flat_acc) for n in (0, 1)]
        PR = [a[:, n * N:(n + 1) * N] for a in (YT[:, :], flat_acc) for n in (0, 1)] + [big(P, N) for _ in range(4)]
        KR = RK[:, :]
        big_at[0] = 0
        HB = [big(P, FC * N).rearrange("p (c n) -> p c n", c=FC) for _ in range(2)]

        IDB = sb("IDB", [P, P], BF16)
        MX = [sb(f"MX{i}", [P, HT, 4]) for i in range(2)]
        MLEFT = sb("MLEFT", [P, HT, 4])
        MTS = sb("MTS", [12, 2, N], BF16)
        MT = [MTS[:, i, :] for i in range(2)]
        FS = sb("FS", [P, 3, 12])
        MPB = sb("MPB", [P, HT, 3, 4], BF16)

        def bc(ap, n, axis):
            a = ap.unsqueeze(axis)
            shape = list(a.shape)
            shape[axis] = n
            return a.to_broadcast(shape)

        def half(b):
            return slice(HT * b, HT * b + HT)

        def cols(b):
            return slice(N * b, N * b + N)

        def tiles(bank):
            return PS[:, bank, :].rearrange("p (t d) -> p t d", t=HT)

        def expert_ready(eng, n):
            eng.wait_ge(sem(f"expert_loaded{n % RING}"), 16 * (n // RING + 1))

        def inputs_ready(eng):
            for name in ("x_loaded", "consts_loaded", "weights_loaded"):
                eng.wait_ge(sem(name), 16)
            eng.wait_ge(sem("rows_loaded"), 16 * 2)

        def rest_ready(eng):
            eng.wait_ge(sem("rest_loaded"), 16 * 5)

        MOE_ORDER = [(e, 0) for e in range(6)] + [(0, 1), (1, 1), (2, 1), (6, 0), (7, 0)] + [(e, 1) for e in range(3, E)]
        BIAS_AT, PREPARE_AT, VW_AT, NEXT_AT = 4, 5, 9, 14
        HALF_DONE = MOE_ORDER.index((E - 1, 0))

        VALUES_AT = 4
        QK_BANKS = ((0, 2), (6, 0))

        def MAX_AHEAD(g, p):
            if g == 0:
                return [(1 + p // 4, (2 * p + n) % 8) for n in range(2)]
            return [(g + 2, p)] if g < 6 else []

        TURN_STEP = {1: 2, 2: 5, 3: 2}
        HALF_STEP = 13

        def second_queries(k, s, chunks):
            n = s - TURN_STEP[k] - 1
            return range(max(2 * n, 0), min(2 * n + 2, chunks)) if n < 3 else range(min(n + 3, chunks), min(n + 4, chunks))

        def query_bank(s, n):
            return 6 + n if s < 5 else 6

        class Steps:
            def __init__(self, eng, s):
                self.eng, self.s, self.n, self.told = eng, s, 0, {}

            def do(self, ins):
                ins.then_inc(self.s, 1)
                self.n += 1
                self.eng.wait_ge(self.s, self.n)

            def settle(self, name):
                self.told[name] = self.told.get(name, 0) + 1
                self.eng.wait_ge(sem(name), self.told[name])

            def mark(self, ins):
                ins.then_inc(self.s, 1)
                self.n += 1
                return self.n

            def until(self, count):
                self.eng.wait_ge(self.s, count)

        block = ctx.enter_context(nc.Block())

        @block.sync
        def _(sp):
            sp.dma_start(X[:, :, :], x_in).then_inc(sem("x_loaded"), 16)
            sp.dma_start(Ct[:, 0:C_FIRST], cpack[:, 0:C_FIRST]).then_inc(sem("consts_loaded"), 16)
            sp.dma_start(Wt[:, 0:W_FIRST], wpack[:, 0:W_FIRST]).then_inc(sem("weights_loaded"), 16)
            sp.dma_start(CX[:, :, :], ctx_rows).then_inc(sem("rows_loaded"), 16)
            sp.dma_start(Rt[:, :], rpack.to_broadcast([P, R_COLS])).then_inc(sem("rows_loaded"), 16)
            sp.dma_start(B0[:, :], b_l0).then_inc(sem("rest_loaded"), 16)
            sp.dma_start(B2[:, 0, :], b2_l1).then_inc(sem("rest_loaded"), 16)
            sp.dma_start(B2[:, 1, :], b2_l3).then_inc(sem("rest_loaded"), 16)
            sp.dma_start(Ct[:, C_FIRST:], cpack[:, C_FIRST:]).then_inc(sem("rest_loaded"), 16)
            sp.dma_start(Wt[:, W_FIRST:], wpack[:, W_FIRST:]).then_inc(sem("rest_loaded"), 16)

            def load_experts(lo, hi):
                for n in range(lo, hi):
                    if n >= RING:
                        sp.wait_ge(sem("expert_used"), n - RING + 1)
                    src = up0[n] if n < E0 else up[n - E0]
                    sp.dma_start(RINGW[:, n % RING, :], src).then_inc(sem(f"expert_loaded{n % RING}"), 16)

            load_experts(0, E0 + RING)
            sp.wait_ge(sem("qk_pieces"), 1)
            sp.dma_start(KS[72:75, :, :].rearrange("p h t -> p (h t)").bitcast(F32), ones_in).then_inc(sem("ones_stacked"), 16)
            for b in range(B):
                for which in range(2):
                    sp.wait_ge(sem("k_pieces" if b and which else "qk_pieces"), 1 if b and which else 2 * b + which + 1)
                    for j in range(3 * which, 3 * which + 3):
                        sp.dma_start(scratch[j, :, cols(b)], PIE[j][:, cols(b)]).then_inc(sem(f"spilled{b}"), 16)
                    sp.wait_ge(sem(f"spilled{b}"), 48 * (which + 1))
                    for i in range(3):
                        if which == 0:
                            src = scratch[0:3, :, cols(b)].rearrange("j (d h) t -> (j d) h t", h=16)
                            sp.dma_start(QS[24 * i:24 * i + 24, :, cols(b)], src).then_inc(sem(f"stacked{b}"), 16)
                        else:
                            src = scratch[3 + i, :, cols(b)].rearrange("(d h) t -> d h t", h=16)
                            sp.dma_start(KS[24 * i:24 * i + 24, :, cols(b)], src.unsqueeze(0).to_broadcast([3, 8, 16, N]))\
                                .then_inc(sem(f"stacked{b}"), 16)
            for g in range(8):
                sp.wait_ge(sem("max_rows"), g + 1)
                b, h0 = g // 4, 4 * (g % 4)
                sp.dma_start(QS[72:75, h0:h0 + 4, cols(b)], MT[g % 2]).then_inc(sem(f"max_stacked{g % 2}"), 16)
            load_experts(E0 + RING, E0 + 3 * E)
            for b in range(B):
                sp.wait_ge(sem("x_final"), b + 1)
                sp.dma_start(out[:, half(b), :], X[:, half(b), :]).then_inc(sem("stored"), 16)
            sp.wait_ge(sem("stored"), 16 * B)

        @block.gpsimd
        def _(pool):
            st = Steps(pool, sem("pool_step"))
            st.do(nc.gpsimd.memset(HALFNEG[:, :], -0.5))

            def inv_root(dst, var, rows=P, n=HT):
                st.do(nc.gpsimd.tensor_scalar(dst, var, EPS, None, ALU.add))
                return nc.gpsimd.tensor_tensor(dst, dst, HALFNEG[0:rows, 0:n], ALU.pow)

            norms = [0]

            def ln(b, double=False):
                norms[0] += 1
                pool.wait_ge(sem("ln_var"), norms[0])
                f, var = RS[:, half(b), 0], MV[:, half(b), 1]
                if double:
                    st.do(nc.gpsimd.tensor_scalar(f, var, 1.0 + EPS, EPS * EPS, ALU.mult, ALU.add))
                    nc.gpsimd.tensor_tensor(f, f, HALFNEG[:, 0:HT], ALU.pow).then_inc(sem("ln_rstd"), 1)
                else:
                    inv_root(f, var).then_inc(sem("ln_rstd"), 1)

            for b in range(B):
                ln(b)
            inputs_ready(pool)
            pool.wait_ge(sem("ctx_var"), 1)
            inv_root(SM[0:C, 40:42], SM[0:C, 32:36].rearrange("p (b v) -> p b v", v=2)[:, :, 1], C, B)\
                .then_inc(sem("ctx_rstd"), 1)
            for b in range(B):
                ln(b, True)
            pool.wait_ge(sem("xn_ready"), 2)
            st.do(nc.gpsimd.tensor_copy(XP[:, :, 0, :], XH[:, :, :]))
            st.do(nc.gpsimd.tensor_tensor(ACC[:, :, :], XH[:, :, :], XP[:, :, 0, :], ALU.subtract))
            st.do(nc.gpsimd.tensor_copy(XP[:, :, 1, :], ACC[:, :, :]))
            st.do(nc.gpsimd.tensor_tensor(ACC[:, :, :], ACC[:, :, :], XP[:, :, 1, :], ALU.subtract))
            nc.gpsimd.tensor_copy(XP[:, :, 2, :], ACC[:, :, :]).then_inc(sem("xp_ready"), 1)
            def cross_setup(k, heads, chunks):
                x = CROSS[k]
                for vt in x["vt"]:
                    st.do(nc.gpsimd.memset(vt, 0.0))
                for ch in range(chunks):
                    hs = slice(2 * ch, 2 * ch + 2) if chunks > 1 else slice(0, heads)
                    n = hs.stop - hs.start
                    mask = c({2: "mask2", 8: "mask8", 16: "mask16"}[n])
                    pool.wait_ge(sem(f"kv{k}_raw"), ch // 3 + 1)
                    for b in range(B):
                        ins = nc.gpsimd.tensor_tensor(x["kt"][:, b, hs, :], bc(x["raw"][0][:, ch, b, :], n, 1), bc(mask, C, 2), ALU.mult)
                        units = [(hs.start // 8, hs)] if n == 2 else [(u, slice(8 * u, 8 * u + 8)) for u in range(heads // 8)]
                        for u, part in units:
                            m = part.stop - part.start
                            at = (part.start - 8 * u) * C
                            dst = x["vt"][ch % len(x["vt"])][:, b, u, at:at + m * C].rearrange("p (h k) -> p h k", h=m)
                            ins = nc.gpsimd.tensor_tensor(dst, bc(x["raw"][1][:, ch, b, :], m, 1),
                                                          bc(mask[:, part.start - hs.start:part.stop - hs.start], C, 2), ALU.mult)
                ins.then_inc(sem(f"kv{k}_masked"), 1)

            def cross_units(k, heads):
                x = CROSS[k]
                ln(1, k != 2)
                for u in range(NT * heads // 8):
                    pool.wait_ge(sem(f"sum{k}_ready"), u + 1)
                    s = x["sc"][u % 4][:, 0:UK].rearrange("p (h k) -> p h k", h=8)
                    nc.gpsimd.tensor_tensor(s, s, bc(REC[:, u % 4, :], C, 2), ALU.mult).then_inc(sem(f"p{k}_normed"), 1)
                    if k == 2 and u == 1:
                        ln(1)
                    if k > 1 and u == HALF_STEP - 1:
                        ln(0)

            def pads(k):
                for n, s in enumerate(CROSS[k]["sc"]):
                    ins = nc.gpsimd.memset(s[:, UK:UW], 0.0)
                ins.then_inc(sem("pads_ready"), 1)

            cross_setup(1, 8, 1)
            ln(0, True)
            pads(1)
            cross_units(1, 8)
            for n in (3, 4):
                for b in range(B):
                    ln(b)
            pool.wait_ge(sem("k_turned"), 1)
            for i in range(3):
                ins = nc.gpsimd.tensor_copy(PIE[3 + i][:, cols(1)], KR)
                if i < 2:
                    st.do(ins)
                    st.do(nc.gpsimd.tensor_tensor(KR, KR, PIE[3 + i][:, cols(1)], ALU.subtract))
            ins.then_inc(sem("k_pieces"), 1)
            for g in range(8):
                pool.wait_ge(sem("max_done"), 8 * g + 8)
                if g:
                    pool.wait_ge(sem("max_turned"), g)
                m = MX[g % 2]
                st.do(nc.gpsimd.tensor_copy(MPB[:, :, 0, :], m[:, :, :]))
                st.do(nc.gpsimd.tensor_tensor(MLEFT[:, :, :], m[:, :, :], MPB[:, :, 0, :], ALU.subtract))
                st.do(nc.gpsimd.tensor_copy(MPB[:, :, 1, :], MLEFT[:, :, :]))
                st.do(nc.gpsimd.tensor_tensor(MLEFT[:, :, :], MLEFT[:, :, :], MPB[:, :, 1, :], ALU.subtract))
                nc.gpsimd.tensor_copy(MPB[:, :, 2, :], MLEFT[:, :, :]).then_inc(sem("max_pieces"), 1)
            for b in range(B):
                ln(b)
            cross_setup(2, 16, 1)
            pads(2)
            for n in range(2):
                ln(0)
            cross_units(2, 16)
            ln(1)
            cross_setup(3, 16, 8)
            pads(3)
            ln(0, True)
            cross_units(3, 16)
            ln(1)

        @block.scalar
        def _(act):
            st = Steps(act, sem("act_step"))
            inputs_ready(act)
            nc.scalar.activation(IDB[:, :], ident, ACT.Copy).then_inc(sem("idb_ready"), 1)
            at = R_AT["g_xattn"][0]
            nc.scalar.activation(TG[:, :], Rt[:, at:at + 9], ACT.Tanh).then_inc(sem("tg_ready"), 1)

            turns = [0]

            def transposed(b, dst, scale=None, bias=None, bank=None):
                turns[0] += 1
                act.wait_ge(sem("tp_done"), turns[0])
                src = PS[:, 6 + b if bank is None else bank, :]
                if scale is None:
                    ins = nc.scalar.activation(dst[:, cols(b)], src, ACT.Copy)
                else:
                    ins = nc.scalar.activation(dst[:, cols(b)], src, ACT.Identity, bias=bias, scale=scale)
                ins.then_inc(sem("tr_ready"), 1)

            def cross_raw(k, r, chunks):
                x = CROSS[k]
                lo, hi = 3 * r, min(3 * r + 3, chunks)
                act.wait_ge(sem(f"kv{k}_done"), r + 1)
                for i in range(2):
                    src = PS[:, 6 + i, 0:(hi - lo) * B * C].rearrange("p (c b k) -> p c b k", c=hi - lo, b=B)
                    ins = nc.scalar.activation(x["raw"][i][:, lo:hi, :, :], src, ACT.Copy)
                ins.then_inc(sem(f"kv{k}_raw"), 1)

            def cross_vw(k, n, units):
                x = CROSS[k]
                b, u = n // units, n % units
                act.wait_ge(sem(f"vw{k}_done"), n + 1)
                nc.scalar.activation(x["vw"][:, b, u, 0:3, :], PS[:, 6, 0:3 * D].rearrange("p (i d) -> p i d", i=3), ACT.Copy)
                nc.scalar.activation(x["vw"][:, b, u, 3:5, :], PS[:, 7, 0:2 * D].rearrange("p (i d) -> p i d", i=2),
                                     ACT.Copy).then_inc(sem(f"vw{k}_ready"), 1)

            def cross_tiles(k, heads, chunks, scale, turn_in):
                x = CROSS[k]
                units = NT * heads // 8

                def q_out(j, bank):
                    act.wait_ge(sem(f"q{k}_done"), j + 1)
                    nc.scalar.activation(x["qc"][:, j // chunks, j % chunks, :], PS[:, bank, :], ACT.Copy, scale=scale)\
                        .then_inc(sem(f"q{k}_ready"), 1)

                turn_in(0)
                for j in range(chunks):
                    q_out(j, j)
                for s in range(units + 3):
                    if s < units:
                        act.wait_ge(sem(f"s{k}_shifted"), s + 1)
                        a = x["sc"][s % 4]
                        nc.scalar.activation(a[:, 0:4 * C], a[:, 0:4 * C], ACT.Exp)
                        if s >= 4:
                            act.wait_ge(sem(f"p{k}_normed"), s - 3)
                        for h in range(4, 8):
                            e = a[:, h * C:(h + 1) * C]
                            raw = e if k == 1 else PS[:, 2 * (s % 2) + 1, (h - 4) * C:(h - 3) * C]
                            ins = nc.scalar.activation(e, raw, ACT.Exp, bias=NTOP[:, s % 2, h:h + 1],
                                                       accum_out=REC[:, s % 4, h:h + 1])
                        ins.then_inc(sem(f"s{k}_exp"), 1)
                    if s >= 3:
                        u = s - 3
                        if u >= 3:
                            act.wait_ge(sem(f"pv{k}_done"), u - 2)
                        for n, (lo, hi) in enumerate(((0, 3), (3, 5))):
                            act.wait_ge(sem(f"p{k}_turned"), 2 * u + n + 1)
                            nc.scalar.activation(x["pt"][u % 3][:, lo * P:hi * P], PS[:, 4 + n, 0:(hi - lo) * P], ACT.Copy)\
                                .then_inc(sem(f"pt{k}_ready"), 1)
                    if s == TURN_STEP[k]:
                        turn_in(1)
                    for n, j in enumerate(second_queries(k, s, chunks)):
                        q_out(chunks + j, query_bank(s, n))
                    if k > 1 and s == HALF_STEP + 2:
                        transposed(0, HTR)

            def focus_ln(fi, rows, groups):
                t1, t2 = FT[fi]
                act.wait_ge(sem("focus_abs"), fi + 1)
                nc.scalar.activation(t1, t2, ACT.Ln, bias=SM[0:rows, 63:64]).then_inc(sem("focus_ln"), 1)

            def focus_exp(fi, rows, groups):
                t1, t2 = FT[fi]
                act.wait_ge(sem("focus_max"), fi + 1)
                for g in range(groups):
                    ins = nc.scalar.activation(t2[:, g * D:(g + 1) * D], t1[:, g * D:(g + 1) * D], ACT.Exp,
                                               bias=FS[0:rows, fi, 4 + g:5 + g], accum_out=FS[0:rows, fi, 8 + g:9 + g])
                ins.then_inc(sem("focus_exp"), 1)

            for b in range(B):
                transposed(b, HTR)
            for f in (focus_ln, focus_exp):
                f(0, C, B)
                for b in range(B):
                    f(1 + b, P, HT)
            for b in range(B):
                transposed(b, QT)
            for b in range(B):
                transposed(b, YT)
            rest_ready(act)
            for b in range(B):
                transposed(b, HTR)
                act.wait_ge(sem("l0_logits"), b + 1)
                nc.scalar.activation(LG[:, cols(b)], PS[0:E0, b, :], ACT.Identity, bias=B0[:, F + D:F + D + 1])\
                    .then_inc(sem("l0_logits_ready"), 1)

            def router_exp(k, n):
                act.wait_ge(sem("router_shifted"), k + 1)
                nc.scalar.activation(GM[:, :, 0:n], GL[:, :, 0:n], ACT.Exp).then_inc(sem("router_exp"), 1)

            act.wait_ge(sem("ctx_turned"), 1)
            nc.scalar.activation(CTXN[:, :], PS[:, 5, 0:B * C], ACT.Identity, bias=w("pre_b"), scale=w("pre_g"))\
                .then_inc(sem("ctxn_ready"), 1)
            router_exp(0, E0)
            cross_raw(1, 0, 1)
            for n in range(2):
                act.wait_ge(sem("gathered"), n + 1)
                nc.scalar.activation(XET[:, cols(n)], PS[:, 4 + n, :], ACT.Copy).then_inc(sem("gathered_ready"), 1)

            def slots_out(q):
                act.wait_ge(sem("slots_turned"), q + 1)
                nc.scalar.activation(S0T[:, q, :], PS[:, 4 + q % 2, :].bitcast(BF16), ACT.Copy)\
                    .then_inc(sem("slots_turned_ready"), 1)

            for q in range(PAIRS):
                act.wait_ge(sem("l0_hidden"), q + 1)
                nc.scalar.activation(HS, PS[:, q % 2, :], ACT.Gelu).then_inc(sem("l0_gelu"), 1)
                act.wait_ge(sem("l0_hidden_turned"), q + 1)
                nc.scalar.activation(HST, PS[:, 2, :], ACT.Copy).then_inc(sem("l0_hidden_ready"), 1)
                if q:
                    slots_out(q - 1)
                if 0 <= q - VALUES_AT - 1 < B:
                    cross_vw(1, q - VALUES_AT - 1, 1)
            slots_out(PAIRS - 1)

            def moe(k, func, b1, second):
                for i in range(2 * E):
                    g = 16 * (k - 1) + i
                    for ch in range(FC):
                        act.wait_ge(sem("moe_hidden"), 4 * g + ch + 1)
                        if g >= 2:
                            act.wait_ge(sem("moe_out"), g - 1)
                        e = MOE_ORDER[i][0]
                        col = b1[:, e * FC + ch:e * FC + ch + 1] if b1 is not None else 0.0
                        nc.scalar.activation(HB[g % 2][:, ch, :], PS[:, ch, :], func, bias=col)\
                            .then_inc(sem("moe_gelu"), 1)
                    if i == BIAS_AT and second is not None:
                        for b in range(B):
                            act.wait_ge(sem("comb_turned"), 2 * second + b + 1)
                            nc.scalar.activation(COMBT[0:E, cols(b)], PS[0:E, 6 + b, :], ACT.Copy)\
                                .then_inc(sem("combt_ready"), 1)
                    if i == 1:
                        transposed(1, HTR)
                        router_exp(k, E + 1 if k == 2 else E)
                    if k < 3:
                        chunks = 1 if k == 1 else 8
                        if 0 <= i - PREPARE_AT - 1 < (chunks + 2) // 3:
                            cross_raw(k + 1, i - PREPARE_AT - 1, chunks)
                        if 0 <= i - VW_AT - 1 < 4:
                            cross_vw(k + 1, i - VW_AT - 1, 2)

            cross_tiles(1, 8, 1, 1.0 / np.sqrt(128.0), lambda b: transposed(b, HTR, w("pre_g"), w("pre_b"), bank=6))
            for b in range(B):
                transposed(b, YT)
                act.wait_ge(sem("l1_wo"), b + 1)
                nc.scalar.activation(ACC[:, half(b), :], tiles(b), ACT.Gelu).then_inc(sem("l1_wo_gelu"), 1)
            for b in range(B):
                transposed(b, HTR)
            def max_rows(g):
                act.wait_ge(sem("max_turned"), g + 1)
                if g >= 2:
                    act.wait_ge(sem(f"max_stacked{g % 2}"), 16 * (g // 2))
                nc.scalar.activation(MT[g % 2], PS[0:12, 7, 0:256].bitcast(BF16), ACT.Copy).then_inc(sem("max_rows"), 1)

            def heads_copy(g):
                act.wait_ge(sem("pv_done"), 4 * g + 4)
                if g:
                    act.wait_ge(sem("heads_turned"), g)
                nc.scalar.activation(OT[:, :], PS[:, 6, :], ACT.Copy).then_inc(sem("heads_copied"), 1)

            max_rows(0)
            for g in range(8):
                for i in range(16):
                    idx = 16 * g + i
                    act.wait_ge(sem("scores"), idx + 1)
                    if idx >= 8:
                        act.wait_ge(sem("pv_done"), (idx - 8) // 4 + 1)
                    nc.scalar.activation(PR[idx % 8], PS[:, 4 + idx % 2, :], ACT.Exp, scale=1.0 / np.sqrt(8.0))\
                        .then_inc(sem("probs"), 1)
                    if i == 3 and g:
                        heads_copy(g - 1)
                    if (g, i) == (6, 4):
                        transposed(0, HTR, bank=2)
                    if (g, i) == (7, 8):
                        transposed(0, HTR, bank=3)
                    if i == (7 if g else 12) and g <= 6:
                        max_rows(g + 1)
            heads_copy(7)
            transposed(1, HTR)
            moe(1, ACT.Gelu, w("L1_b1"), 0)
            cross_tiles(2, 16, 1, 1.0 / np.sqrt(8.0), lambda b: transposed(b, HTR, bank=6))
            moe(2, ACT.Gelu, None, None)
            cross_tiles(3, 16, 8, 64.0 ** -0.5, lambda b: transposed(b, HTR, w("L3_gamma"), w("L3_beta"), bank=6))
            moe(3, ACT.Gelu_apprx_tanh, w("L3_b1"), 1)

        @block.vector
        def _(dve):
            v = nc.vector
            st = Steps(dve, sem("dve_step"))
            st.do(v.memset(SM[:, 63:64], 1e-6))
            dve.wait_ge(sem("x_loaded"), 16)
            norms = [0]

            def ln_stats(b, src):
                h = range(HT * b, HT * b + HT)
                norms[0] += 1
                for t in h:
                    ins = v.bn_stats(ST6[:, t, :], src[:, t, :])
                st.do(ins)
                for t in h:
                    ins = v.bn_aggr(MV[:, t, :], ST6[:, t, :])
                ins.then_inc(sem("ln_var"), 1)
                st.settle("ln_var")

            def ln_apply(b, src, earlier=0):
                dve.wait_ge(sem("ln_rstd"), norms[0] - earlier)
                for t in range(HT * b, HT * b + HT):
                    ins = v.tensor_scalar(XH[:, t, :], src[:, t, :], MV[:, t, 0:1], RS[:, t, 0:1],
                                          ALU.subtract, ALU.mult)
                return ins

            def ln(b, src):
                ln_stats(b, src)
                return ln_apply(b, src)

            def gain(b, name, name2):
                st.do(v.tensor_tensor(XH[:, half(b), :], XH[:, half(b), :], bc(r(name), HT, 1), ALU.mult))
                return v.tensor_tensor(XH[:, half(b), :], XH[:, half(b), :], bc(r(name2), HT, 1), ALU.add)

            def keep_largest(dst, val, rows, groups, n, order, keep):
                flat = groups * n
                R, S, even, odd = (a[0:rows, :].bitcast(BF16)[:, k * N:k * N + flat].rearrange("p (i g) -> p i g", i=n)
                                 for a in (RK, RG) for k in range(2))
                vt = val.rearrange("p g i -> p i g")
                added = st.mark(v.tensor_copy(R, bc(order, groups, 2)))
                taken = st.mark(v.memset(S, 0.0))
                compared = {}
                for s in range(1, n + 1):
                    if s < n:
                        G = (even, odd)[s % 2]
                        if s > 2:
                            st.until(taken)
                        compared[s] = st.mark(v.tensor_tensor(G[:, 0:n - s, :], vt[:, 0:n - s, :], vt[:, s:n, :], ALU.is_ge))
                    if s > 1:
                        d, G = s - 1, (even, odd)[(s - 1) % 2]
                        st.until(max(compared[d], added))
                        added = st.mark(v.tensor_tensor(R[:, d:n, :], R[:, d:n, :], G[:, 0:n - d, :], ALU.add))
                        st.until(taken)
                        taken = st.mark(v.tensor_tensor(S[:, 0:n - d, :], S[:, 0:n - d, :], G[:, 0:n - d, :], ALU.subtract))
                st.until(taken)
                st.do(v.tensor_tensor(R, R, S, ALU.add))
                return v.scalar_tensor_tensor(out=dst, in0=R.rearrange("p i g -> p g i"), scalar=keep - 0.5, in1=val,
                                              op0=ALU.is_lt, op1=ALU.mult)

            def split3(dsts, src, left):
                st.do(v.tensor_copy(dsts[0], src))
                st.do(v.tensor_tensor(left, src, dsts[0], ALU.subtract))
                st.do(v.tensor_copy(dsts[1], left))
                st.do(v.tensor_tensor(left, left, dsts[1], ALU.subtract))
                return v.tensor_copy(dsts[2], left)

            def add_to_x(b, src, gate):
                st.do(v.scalar_tensor_tensor(out=X[:, half(b), :], in0=src, scalar=TG[:, gate:gate + 1],
                                             in1=X[:, half(b), :], op0=ALU.mult, op1=ALU.add))

            for b in range(B):
                ln_stats(b, X)
            for b in range(B):
                ln_apply(b, X, B - 1 - b).then_inc(sem("xh_ready"), 1)
                st.settle("xh_ready")
            inputs_ready(dve)
            for b in range(B):
                st.do(v.bn_stats(ST6[0:C, b, :], CX[:, b, :]))
                ins = v.bn_aggr(SM[0:C, 32 + 2 * b:34 + 2 * b], ST6[0:C, b, :])
            ins.then_inc(sem("ctx_var"), 1)
            st.settle("ctx_var")

            dve.wait_ge(sem("ctx_rstd"), 1)
            for b in range(B):
                ins = v.tensor_scalar(CTXH[:, b, :], CX[:, b, :], SM[0:C, 32 + 2 * b:33 + 2 * b],
                                      SM[0:C, 40 + b:41 + b], ALU.subtract, ALU.mult)
            ins.then_inc(sem("ctx_normed"), 1)
            st.settle("ctx_normed")

            def focus_abs(fi, src, rows, groups):
                t1, t2 = (a.rearrange("p (g d) -> p g d", g=groups) for a in FT[fi])
                st.do(v.tensor_scalar(t1, src, -0.01, None, ALU.mult))
                v.tensor_tensor(t2, src, t1, ALU.max).then_inc(sem("focus_abs"), 1)
                st.settle("focus_abs")
                dve.wait_ge(sem("focus_abs"), fi + 1)
                v.tensor_reduce(FS[0:rows, fi, 0:groups], t2, AX.X, ALU.add).then_inc(sem("focus_sum"), 1)
                st.settle("focus_sum")

            def focus_max(fi, rows, groups):
                t1 = FT[fi][0]
                dve.wait_ge(sem("focus_ln"), fi + 1)
                st.do(v.tensor_scalar(t1, t1, r("focus", rows), None, ALU.mult))
                v.tensor_reduce(FS[0:rows, fi, 4:4 + groups], t1.rearrange("p (g d) -> p g d", g=groups), AX.X, ALU.max,
                                negate=True).then_inc(sem("focus_max"), 1)
                st.settle("focus_max")

            def focus_keep(fi, dst, rows, groups):
                t2 = FT[fi][1].rearrange("p (g d) -> p g d", g=groups)
                fs = FS[0:rows, fi, :]
                dve.wait_ge(sem("focus_exp"), fi + 1)
                st.do(v.reciprocal(fs[:, 8:8 + groups], fs[:, 8:8 + groups]))
                st.do(v.tensor_scalar(fs[:, 0:groups], fs[:, 0:groups], 1.0 / D, 1e-6, ALU.mult, ALU.add))
                st.do(v.tensor_tensor(fs[:, 0:groups], fs[:, 0:groups], fs[:, 8:8 + groups], ALU.mult))
                for g in range(groups):
                    ins = v.tensor_scalar(t2[:, g, :], t2[:, g, :], fs[:, g:g + 1], None, ALU.mult)
                st.do(ins)
                flat = t2.rearrange("p g (h i) -> p (g h) i", i=8)
                return keep_largest(dst, flat, rows, groups * 16, 8, c("order8", rows), KEEP)

            dve.wait_ge(sem("l0_kv"), 1)
            for b in range(B):
                st.do(v.tensor_copy(VA[:, b, 0:D], PS[0:C, 1, b * D:(b + 1) * D]))
                st.do(v.memset(VA[:, b, D:D + 1], 1.0))
            focus_abs(0, PS[0:C, 0, 0:B * D].rearrange("p (b d) -> p b d", b=B), C, B)
            for b in range(B):
                dve.wait_ge(sem("l0_q"), b + 1)
                focus_abs(1 + b, tiles(4 + b), P, HT)
            focus_max(0, C, B)
            for b in range(B):
                focus_max(1 + b, P, HT)
            focus_keep(0, KF[:, :, :].rearrange("p b (h i) -> p (b h) i", i=8), C, B).then_inc(sem("l0_k_ready"), 1)
            st.settle("l0_k_ready")
            for b in range(B):
                focus_keep(1 + b, QF[:, half(b), :].rearrange("p t (h i) -> p (t h) i", i=8), P, HT)\
                    .then_inc(sem("qf_ready"), 1)
                st.settle("qf_ready")
                dve.wait_ge(sem("l0_sums"), b + 1)
                st.do(v.scalar_tensor_tensor(out=KVM[:, b, 0:D], in0=PS[:, 2 + b, 0:D], scalar=1.0 / N,
                                             in1=c("blocks"), op0=ALU.mult, op1=ALU.mult))
                st.do(v.tensor_scalar(SM[:, 24:25], PS[:, 2 + b, D:D + 1], 1.0 / C, None, ALU.mult))
                v.tensor_scalar(KVM[:, b, D:D + 16], c("mask16"), SM[:, 24:25], None, ALU.mult)\
                    .then_inc(sem("l0_state_ready"), 1)
                st.settle("l0_state_ready")
            for b in range(B):
                dve.wait_ge(sem("l0_y"), b + 1)
                y = PS[:, 2 * b:2 * b + 2, :].rearrange("p k (j n) -> p (k j) n", n=256)
                z = RG[:, 0:64].rearrange("p (t h) -> p t h", t=HT)
                st.do(v.tensor_scalar(z, y[:, :, D:D + 16], 1e-6, None, ALU.add))
                st.do(v.reciprocal(z, z))
                v.tensor_tensor(Y[:, half(b), :].rearrange("p t (h i) -> p t h i", i=8),
                                y[:, :, 0:D].rearrange("p t (h i) -> p t h i", i=8), bc(z, 8, 3), ALU.mult)\
                    .then_inc(sem("y_ready"), 1)
                st.settle("y_ready")
            dve.wait_ge(sem("tg_ready"), 1)
            for b in range(B):
                dve.wait_ge(sem("l0_o"), b + 1)
                add_to_x(b, tiles(4 + b), 0)
                ln_stats(b, X)
            for b in range(B):
                st.do(ln_apply(b, X, B - 1 - b))
                v.tensor_tensor(XH[:, half(b), :], XH[:, half(b), :], bc(r("norm_weight"), HT, 1), ALU.mult)\
                    .then_inc(sem("xn_ready"), 1)
                st.settle("xn_ready")

            def router(k, n, src, bias):
                gl = GL[:, :, 0:n]
                if bias is None:
                    st.do(v.tensor_copy(gl, src))
                else:
                    st.do(v.tensor_tensor(gl, src, bc(bias, NT, 1), ALU.add))
                st.do(v.tensor_reduce(G1[:, :], gl, AX.X, ALU.max))
                v.tensor_tensor(gl, gl, bc(G1[:, :], n, 2), ALU.subtract).then_inc(sem("router_shifted"), 1)
                st.settle("router_shifted")
                dve.wait_ge(sem("router_exp"), k + 1)
                st.do(v.tensor_reduce(G1[:, :], GM[:, :, 0:n], AX.X, ALU.add))
                st.do(v.reciprocal(G1[:, :], G1[:, :]))
                st.do(v.tensor_tensor(GR[:, :, 0:n], GM[:, :, 0:n], bc(G1[:, :], n, 2), ALU.mult))

            rest_ready(dve)
            st.do(v.memset(ONESR[:, :], 1.0))
            dve.wait_ge(sem("l0_logits_ready"), 2)
            src = LG
            for n in range(SLOTS // 8):
                st.do(v.max(M8[:, :], src))
                st.do(v.match_replace(LW, M8[:, :], src, NEG))
                src = LW
            st.do(v.tensor_tensor(LW, LW, LG, ALU.not_equal))
            st.do(v.tensor_tensor_scan(CUM, ONESR, LW, 0.0, ALU.mult, ALU.add))
            v.tensor_tensor(CUM, CUM, LW, ALU.mult).then_inc(sem("places_ready"), 1)
            st.settle("places_ready")
            dve.wait_ge(sem("places_turned"), 1)
            places = PS[:, 3, 0:NT * E0].rearrange("p (t e) -> p t e", t=NT)
            st.do(v.tensor_copy(GC[:, :, :], places))
            for t in range(NT):
                v.tensor_tensor(S0[:, t, :].rearrange("p (e s) -> p e s", e=E0), bc(c("iota"), E0, 1),
                                bc(GC[:, t, :], SLOTS, 2), ALU.is_equal).then_inc(sem("slots_ready"), 1)
                st.settle("slots_ready")
            dve.wait_ge(sem("l0_logits_turned"), 1)
            router(0, E0, PS[:, 2, 0:NT * E0].rearrange("p (t e) -> p t e", t=NT), None)
            st.do(v.scalar_tensor_tensor(out=GS[:, :, :], in0=GC[:, :, :], scalar=0.0, in1=GR[:, :, :], op0=ALU.is_gt, op1=ALU.mult))
            st.do(v.tensor_reduce(G2[:, :], GS[:, :, :], AX.X, ALU.add))
            st.do(v.tensor_scalar(G2[:, :], G2[:, :], 1e-37, None, ALU.max))
            st.do(v.reciprocal(G2[:, :], G2[:, :]))
            st.do(v.tensor_tensor(GS[:, :, :], GS[:, :, :], bc(G2[:, :], E0, 2), ALU.mult))
            split3([WP[:, :, i, :] for i in range(3)], GS[:, :, :], GM[:, :, :]).then_inc(sem("shares_ready"), 1)
            st.settle("shares_ready")
            for n in range(2):
                dve.wait_ge(sem("shares_gathered"), n + 1)
                v.tensor_tensor(GM48[:, cols(n)], PS[0:48, 6 + n, :], c("diag", 48)[:, cols(n)], ALU.mult)\
                    .then_inc(sem("shares_own"), 1)
                st.settle("shares_own")
            dve.wait_ge(sem("shares_turned"), 1)
            st.do(v.tensor_copy(GSL[:, :], PS[:, 7, 0:PAIRS]))
            for q in range(PAIRS):
                dve.wait_ge(sem("expert_used"), 2 * q + 2)
                st.do(v.tensor_scalar(TMP[:, 0:D], PS[:, 3, 0:D], GSL[:, q:q + 1], None, ALU.mult))
                split3([YP[:, q, i, :] for i in range(3)], TMP[:, 0:D], TMP2[:, 0:D]).then_inc(sem("yp_ready"), 1)
                st.settle("yp_ready")
            def next_apply(b):
                ln_apply(b, X).then_inc(sem("xh_ready"), 1)
                st.settle("xh_ready")

            def level0_out(b):
                dve.wait_ge(sem("scattered"), b + 1)
                add_to_x(b, tiles(4 + b), 4)
                ln_stats(b, X)

            level0_out(0)
            next_apply(0)

            def cross_tiles(k, heads, tail, before):
                x = CROSS[k]
                per = heads // 8
                units = NT * per
                for s in range(units + 6):
                    if s >= 6 and (s - 5) % per == 0:
                        t = (s - 5) // per - 1
                        dve.wait_ge(sem(f"pv{k}_done"), per * (t + 1))
                        tail(t, PS[:, 7, 0:D])
                    if s < units:
                        a = x["sc"][s % 4][:, 0:UK].rearrange("p (n h k) -> p n h k", n=2, k=C)
                        raw = PS[:, 2 * (s % 2):2 * (s % 2) + 2, 0:4 * C].rearrange("p n (h k) -> p n h k", k=C)
                        ntop = NTOP[:, s % 2, :].rearrange("p (n h) -> p n h", h=4)
                        dve.wait_ge(sem(f"s{k}_done"), s + 1)
                        if s >= 4:
                            dve.wait_ge(sem(f"p{k}_turned"), 2 * (s - 3))
                        if k == 1:
                            st.do(v.tensor_scalar(a, raw, 1e4, -1e4, ALU.min, ALU.max))
                            raw = a
                        st.do(v.tensor_reduce(ntop, raw, AX.X, ALU.max, negate=True))
                        v.tensor_tensor(a[:, 0], raw[:, 0], bc(ntop[:, 0], C, 2), ALU.add).then_inc(sem(f"s{k}_shifted"), 1)
                        st.settle(f"s{k}_shifted")
                    if 1 <= s <= units:
                        u = s - 1
                        a = x["sc"][u % 4][:, 0:UK].rearrange("p (h k) -> p h k", k=C)
                        dve.wait_ge(sem(f"s{k}_exp"), u + 1)
                        if u >= 4:
                            dve.wait_ge(sem(f"p{k}_normed"), u - 3)
                        st.do(v.tensor_reduce(REC[:, u % 4, 0:4], a[:, 0:4, :], AX.X, ALU.add))
                        v.reciprocal(REC[:, u % 4, :], REC[:, u % 4, :]).then_inc(sem(f"sum{k}_ready"), 1)
                        st.settle(f"sum{k}_ready")
                    if s < len(before):
                        before[s](1)
                    if k == 1 and s == units + 1:
                        ln_stats(0, Y)
                    if k == 1 and s == units + 3:
                        st.do(ln_apply(0, Y))
                    if k == 1 and s == units + 4:
                        gain(0, "ln_g", "ln_b").then_inc(sem("xh_ready"), 1)
                        st.settle("xh_ready")
                    if k > 1 and s == HALF_STEP:
                        ln_stats(0, X)
                    if k > 1 and s == HALF_STEP + 1:
                        next_apply(0)

            def top2(k, n):
                sem_in = sem("router_done")
                dve.wait_ge(sem_in, k)
                src = PS[:, 6, 0:NT * 16].rearrange("p (t e) -> p t e", t=NT)[:, :, 0:n]
                router(k, n, src, {1: r("bg"), 2: r("L2_router_b"), 3: None}[k])
                st.do(keep_largest(GC[:, :, 0:n], GR[:, :, 0:n], P, NT, n, c("order9" if n == 9 else "order8"), 2))
                if k == 1:
                    st.do(v.tensor_reduce(G1[:, :], GC[:, :, 0:n], AX.X, ALU.add))
                    st.do(v.reciprocal(G1[:, :], G1[:, :]))
                    st.do(v.tensor_tensor(GC[:, :, 0:n], GC[:, :, 0:n], bc(G1[:, :], n, 2), ALU.mult))
                if k == 1:
                    ins = v.tensor_copy(ACC[:, :, :], XH[:, :, :])
                elif k == 2:
                    ins = v.tensor_tensor(ACC[:, :, :], XH[:, :, :], bc(GC[:, :, E], D, 2), ALU.mult)
                else:
                    ins = v.memset(ACC[:, :, :], 0.0)
                ins.then_inc(sem("comb_ready"), 1)
                st.settle("comb_ready")
                dve.wait_ge(sem("comb_ready"), k)

            def moe(k, second, after):
                top2(k, E + 1 if k == 2 else E)
                for i in range(2 * E):
                    g = 16 * (k - 1) + i
                    e, b = MOE_ORDER[i]
                    dve.wait_ge(sem("moe_out"), g + 1)
                    if i >= 1:
                        dve.wait_ge(sem("moe_summed"), g)
                    for j in range(HT):
                        t = HT * b + j
                        ins = v.scalar_tensor_tensor(out=ACC[:, t, :], in0=PS[:, 4 + g % 2, j * D:(j + 1) * D],
                                                     scalar=GC[:, t, e:e + 1], in1=ACC[:, t, :], op0=ALU.mult, op1=ALU.add)
                    ins.then_inc(sem("moe_summed"), 1)
                    st.settle("moe_summed")
                    if i == BIAS_AT and second is not None:
                        for b2 in range(B):
                            dve.wait_ge(sem("moe_bias"), 2 * second + b2 + 1)
                            dve.wait_ge(sem("moe_summed"), g + 1)
                            v.tensor_tensor(ACC[:, half(b2), :], tiles(6 + b2), ACC[:, half(b2), :], ALU.add)\
                                .then_inc(sem("bias_added"), 1)
                            st.settle("bias_added")
                    if HALF_DONE <= i < HALF_DONE + len(after):
                        after[i - HALF_DONE](0)

            def keep_o(t, o):
                v.tensor_copy(Y[:, t, :], o).then_inc(sem("o_read"), 1)
                st.settle("o_read")

            cross_tiles(1, 8, keep_o, [level0_out, next_apply])
            def level1_residual(b):
                dve.wait_ge(sem("l1_wo_gelu"), b + 1)
                st.do(v.tensor_tensor(Y[:, half(b), :], ACC[:, half(b), :], XH[:, half(b), :], ALU.add))
                add_to_x(b, Y[:, half(b), :], 1)

            ln_stats(1, Y)
            level1_residual(0)
            st.do(ln_apply(1, Y))
            gain(1, "ln_g", "ln_b").then_inc(sem("xh_ready"), 1)
            st.settle("xh_ready")
            ln_stats(0, X)
            st.do(v.memset(VS[:, half(0), :, :], 0.0))
            ln_apply(0, X).then_inc(sem("xh_ready"), 1)
            st.settle("xh_ready")
            dve.wait_ge(sem("xh_ready"), 6)
            level1_residual(1)
            ln_stats(1, X)
            st.do(v.memset(VS[:, half(1), :, :], 0.0))
            ln_apply(1, X).then_inc(sem("xh_ready"), 1)
            st.settle("xh_ready")
            st.do(v.memset(VS[:, :, :, 8:9], 1.0))
            for b in range(B):
                dve.wait_ge(sem("qk_done"), 2 * b + 1)
                for which in range(2):
                    n = QK_BANKS[b][which]
                    names = (("bq", "bqR"), ("bk", "bkR"))[which]
                    dve.wait_ge(sem("qk_done"), 2 * b + which + 1)
                    st.do(v.scalar_tensor_tensor(out=TMP[:, :], in0=PS[:, n, :], scalar=w(names[0]), in1=c("cos"),
                                                 op0=ALU.add, op1=ALU.mult))
                    st.do(v.scalar_tensor_tensor(out=TMP2[:, :], in0=PS[:, n + 1, :], scalar=w(names[1]), in1=c("sin"),
                                                 op0=ALU.add, op1=ALU.mult))
                    if b and which:
                        v.tensor_tensor(KR, TMP[:, :], TMP2[:, :], ALU.add).then_inc(sem("k_turned"), 1)
                        st.settle("k_turned")
                        continue
                    st.do(v.tensor_tensor(TMP[:, :], TMP[:, :], TMP2[:, :], ALU.add))
                    split3([PIE[3 * which + i][:, cols(b)] for i in range(3)], TMP[:, :], TMP2[:, :])\
                        .then_inc(sem("qk_pieces"), 1)
                    st.settle("qk_pieces")
                dve.wait_ge(sem("v_done"), b + 1)
                v.tensor_tensor(VS[:, half(b), :, 0:8], PS[:, 4 + b, :].rearrange("p (t h i) -> p t h i", t=HT, i=8),
                                bc(r("bv"), HT, 1).rearrange("p t (h i) -> p t h i", i=8), ALU.add).then_inc(sem("v_ready"), 1)
                st.settle("v_ready")

            def maximum(g, un):
                i = 8 * g + un
                dve.wait_ge(sem("max_scores"), i + 1)
                if un == 0 and g >= 2:
                    dve.wait_ge(sem("max_pieces"), g - 1)
                v.tensor_reduce(MX[g % 2][:, 2 * (un % 2):2 * (un % 2) + 2, un // 2], PS[:, 2 * (i % 2):2 * (i % 2) + 2, :], AX.X,
                                ALU.max, negate=True).then_inc(sem("max_done"), 1)
                st.settle("max_done")

            def heads_out(g):
                b, g4 = g // 4, g % 4
                dve.wait_ge(sem("heads_turned"), g + 1)
                o = PS[:, 7, :].rearrange("p (t j r) -> p t j r", t=HT, r=32)
                rec = SM[:, 16:32].rearrange("p (t h) -> p t h", t=HT)
                st.do(v.reciprocal(rec, o[:, :, :, 8]))
                v.tensor_tensor(Y[:, half(b), 32 * g4:32 * g4 + 32].rearrange("p t (j i) -> p t j i", i=8),
                                o[:, :, :, 0:8], bc(rec, 8, 3), ALU.mult).then_inc(sem("heads_ready"), 1)
                st.settle("heads_ready")

            def attention_residual(b):
                dve.wait_ge(sem("l1f_o"), b + 1)
                st.do(v.tensor_tensor(TMP[:, :].rearrange("p (t d) -> p t d", t=HT), tiles(5 * b), bc(r("bo"), HT, 1), ALU.add))
                st.do(v.tensor_tensor(Y[:, half(b), :], TMP[:, :].rearrange("p (t d) -> p t d", t=HT), XH[:, half(b), :], ALU.add))
                st.do(ln(b, Y))
                gain(b, "g1", "be1").then_inc(sem("xh_ready"), 1)
                st.settle("xh_ready")

            for un in range(8):
                maximum(0, un)
            for b in range(B):
                dve.wait_ge(sem(f"spilled{b}"), 16 * 6)
            for g in range(8):
                for p in range(8):
                    for g2, un in MAX_AHEAD(g, p):
                        maximum(g2, un)
                    if g and p == 5:
                        heads_out(g - 1)
                    if (g, p) == (6, 6):
                        attention_residual(0)
            heads_out(7)
            attention_residual(1)

            def out_stats(b):
                ln_stats(b, ACC)

            def out_norm(b):
                st.do(ln_apply(b, ACC))
                st.do(gain(b, "g2", "be2"))

            def out_add(b):
                add_to_x(b, XH[:, half(b), :], 5)
                ln_stats(b, X)

            moe(1, 0, [out_stats, out_norm, out_add, next_apply])
            def tail2(t, o):
                v.tensor_tensor(TMP[:, 0:D], o, r("L2_bo"), ALU.add).then_inc(sem("o_read"), 1)
                st.settle("o_read")
                st.do(v.scalar_tensor_tensor(out=X[:, t, :], in0=TMP[:, 0:D], scalar=TG[:, 2:3], in1=X[:, t, :],
                                             op0=ALU.mult, op1=ALU.add))

            cross_tiles(2, 16, tail2, [out_stats, out_norm, out_add, next_apply])
            ln_stats(1, X)
            next_apply(1)
            dve.wait_ge(sem("xh_ready"), 14)

            def level2_out(b):
                add_to_x(b, ACC[:, half(b), :], 6)
                ln_stats(b, X)

            moe(2, None, [level2_out, next_apply])
            def tail3(t, o):
                v.tensor_tensor(TMP[:, 0:D], o, r("b_out"), ALU.add).then_inc(sem("o_read"), 1)
                st.settle("o_read")
                st.do(v.tensor_scalar(TMP[:, 0:D], TMP[:, 0:D], TG[:, 8:9], None, ALU.mult))
                st.do(v.scalar_tensor_tensor(out=X[:, t, :], in0=TMP[:, 0:D], scalar=TG[:, 3:4], in1=X[:, t, :],
                                             op0=ALU.mult, op1=ALU.add))

            cross_tiles(3, 16, tail3, [level2_out, next_apply])
            ln_stats(1, X)
            next_apply(1)

            def finish(b):
                v.scalar_tensor_tensor(out=X[:, half(b), :], in0=ACC[:, half(b), :], scalar=TG[:, 7:8],
                                       in1=X[:, half(b), :], op0=ALU.mult, op1=ALU.add).then_inc(sem("x_final"), 1)
                st.settle("x_final")

            moe(3, 1, [finish])
            finish(1)

        @block.tensor
        def _(pe):
            mm, tp = nc.tensor.matmul, nc.tensor.transpose
            inputs_ready(pe)

            turns = {}

            def turn(m, b, src, ready, value, bank=None):
                turns[m, b] = len(turns) + 1
                pe.wait_ge(sem(ready), value)
                for j in range(HT):
                    ins = tp(PS[:, 6 + b if bank is None else bank, j * P:(j + 1) * P], src[:, HT * b + j, :], ident)
                ins.then_inc(sem("tp_done"), 1)

            def turned(m, b):
                pe.wait_ge(sem("tr_ready"), turns[m, b])

            def tile_of(a, b, j):
                return a[:, (HT * b + j) * P:(HT * b + j + 1) * P]

            def cross_kv(k, r, chunks, wk, wv, keys):
                lo, hi = 3 * r, min(3 * r + 3, chunks)
                if r:
                    pe.wait_ge(sem(f"kv{k}_raw"), r)
                for ch in range(lo, hi):
                    at = (ch - lo) * B * C
                    mm(PS[:, 6, at:at + B * C], wk[:, ch * D:(ch + 1) * D], keys, start=True, stop=True)
                    ins = mm(PS[:, 7, at:at + B * C], wv[:, ch * D:(ch + 1) * D], w("ctxT"), start=True, stop=True)
                ins.then_inc(sem(f"kv{k}_done"), 1)

            def cross_vw(k, n, units, wo):
                x = CROSS[k]
                b, u = n // units, n % units
                if n == 0:
                    pe.wait_ge(sem(f"kv{k}_masked"), 1)
                    pe.wait_ge(sem(f"kv{k}_raw"), 1 if k < 3 else 3)
                else:
                    pe.wait_ge(sem(f"vw{k}_ready"), n)
                for i in range(UB):
                    out_i = PS[:, 6, i * D:(i + 1) * D] if i < 3 else PS[:, 7, (i - 3) * D:(i - 2) * D]
                    if k < 3:
                        ins = mm(out_i, x["vt"][0][:, b, u, i * P:(i + 1) * P], wo, start=True, stop=True)
                        continue
                    pairs = sorted({min(i * P // (2 * C), 3), min((i * P + P - 1) // (2 * C), 3)})
                    for pair in pairs:
                        ch = 4 * u + pair
                        ins = mm(out_i, x["vt"][ch % 2][:, b, u, i * P:(i + 1) * P], wo[:, ch * D:(ch + 1) * D],
                                 start=(pair == pairs[0]), stop=(pair == pairs[-1]))
                ins.then_inc(sem(f"vw{k}_done"), 1)

            def cross_tiles(k, heads, chunks, wq, tm, norms):
                x = CROSS[k]
                per = heads // 8
                units = NT * per

                def query(j, bank):
                    mm(PS[:, bank, :], wq[:, (j % chunks) * D:(j % chunks + 1) * D], HTR[:, cols(j // chunks)],
                       start=True, stop=True).then_inc(sem(f"q{k}_done"), 1)

                if k == 1:
                    pe.wait_ge(sem("vw1_ready"), B)
                    turn(tm, 0, XH, "xh_ready", norms + 1)
                turned(tm, 0)
                if k > 1:
                    pe.wait_ge(sem("moe_summed"), 16 * (k - 1))
                for j in range(chunks):
                    query(j, j)
                pe.wait_ge(sem(f"q{k}_ready"), chunks)
                pe.wait_ge(sem(f"vw{k}_ready"), B * per)
                pe.wait_ge(sem("pads_ready"), k)
                for s in range(units + 5):
                    if s < units:
                        t, hh = s // per, s % per
                        b, j = t // HT, t % HT
                        if b:
                            pe.wait_ge(sem(f"q{k}_ready"), B * chunks)
                        if s >= 2:
                            pe.wait_ge(sem(f"s{k}_exp"), s - 1)
                        for n in range(2):
                            h0 = 8 * hh + 4 * n
                            if chunks == 1:
                                ins = mm(PS[:, 2 * (s % 2) + n, 0:4 * C], x["qc"][:, b, 0, j * P:(j + 1) * P],
                                         x["kt"][:, b, h0:h0 + 4, :].rearrange("p h k -> p (h k)"), start=True, stop=True)
                                continue
                            for m in range(2):
                                ins = mm(PS[:, 2 * (s % 2) + n, m * 2 * C:(m + 1) * 2 * C],
                                         x["qc"][:, b, h0 // 2 + m, j * P:(j + 1) * P],
                                         x["kt"][:, b, h0 + 2 * m:h0 + 2 * m + 2, :].rearrange("p h k -> p (h k)"),
                                         start=True, stop=True)
                        ins.then_inc(sem(f"s{k}_done"), 1)
                    if s >= 5:
                        u = s - 5
                        t, hh = u // per, u % per
                        pe.wait_ge(sem(f"pt{k}_ready"), 2 * u + 2)
                        if u == 0 and chunks > 1:
                            pe.wait_ge(sem(f"q{k}_ready"), chunks + 4)
                        if t and hh == 0:
                            pe.wait_ge(sem("o_read"), NT * (k - 1) + t)
                        for i in range(UB):
                            ins = mm(PS[:, 7, 0:D], x["pt"][u % 3][:, i * P:(i + 1) * P], x["vw"][:, t // HT, hh, i, :],
                                     start=(hh == 0 and i == 0), stop=(hh == per - 1 and i == UB - 1))
                        ins.then_inc(sem(f"pv{k}_done"), 1)
                    if 3 <= s < units + 3:
                        u = s - 3
                        pe.wait_ge(sem(f"p{k}_normed"), u + 1)
                        for i in range(UB):
                            n = i // 3
                            if u and i in (0, 3):
                                pe.wait_ge(sem(f"pt{k}_ready"), 2 * (u - 1) + n + 1)
                            ins = tp(PS[:, 4 + n, (i - 3 * n) * P:(i - 3 * n + 1) * P], x["sc"][u % 4][:, i * P:(i + 1) * P], ident)
                            if i in (2, 4):
                                ins.then_inc(sem(f"p{k}_turned"), 1)
                    if s == TURN_STEP[k]:
                        turn(tm, 1, XH, "xh_ready", norms + 2, bank=6)
                    for n, j in enumerate(second_queries(k, s, chunks)):
                        if j == 0:
                            turned(tm, 1)
                        else:
                            pe.wait_ge(sem(f"q{k}_ready"), chunks + j)
                        query(chunks + j, query_bank(s, n))
                    if k > 1 and s == HALF_STEP + 2:
                        turn(tm + 1, 0, XH, "xh_ready", norms + 3)

            for b in range(B):
                ct = w("ctxT")[:, b * C:(b + 1) * C]
                mm(PS[0:C, 0, b * D:(b + 1) * D], ct, w("L0_WkT"), start=True, stop=True)
                ins = mm(PS[0:C, 1, b * D:(b + 1) * D], ct, w("L0_WvT"), start=True, stop=True)
            ins.then_inc(sem("l0_kv"), 1)
            for b in range(B):
                turn(0, b, XH, "xh_ready", b + 1)
            for b in range(B):
                turned(0, b)
                for j in range(HT):
                    ins = mm(PS[:, 4 + b, j * P:(j + 1) * P], tile_of(HTR, b, j), w("L0_WqT"), start=True, stop=True)
                ins.then_inc(sem("l0_q"), 1)
            pe.wait_ge(sem("l0_k_ready"), 1)
            for b in range(B):
                mm(PS[:, 2 + b, 0:D + 1], KF[:, b, :], VA[:, b, 0:D + 1], start=True, stop=True).then_inc(sem("l0_sums"), 1)
            for b in range(B):
                turn(1, b, QF, "qf_ready", b + 1)
            for b in range(B):
                turned(1, b)
                pe.wait_ge(sem("l0_state_ready"), 2)
                for j in range(HT):
                    ins = mm(PS[:, 2 * b + j // 2, (j % 2) * 256:(j % 2) * 256 + D + 16], tile_of(QT, b, j), KVM[:, b, :],
                             start=True, stop=True)
                ins.then_inc(sem("l0_y"), 1)
            for b in range(B):
                turn(2, b, Y, "y_ready", b + 1)
            for b in range(B):
                turned(2, b)
                for j in range(HT):
                    ins = mm(PS[:, 4 + b, j * P:(j + 1) * P], tile_of(YT, b, j), w("L0_WpT"), start=True, stop=True)
                ins.then_inc(sem("l0_o"), 1)
            rest_ready(pe)
            for b in range(B):
                turn(3, b, XH, "xn_ready", b + 1)
            for b in range(B):
                turned(3, b)
                mm(PS[0:E0, b, :], w("L0_routerT"), HTR[:, cols(b)], start=True, stop=True).then_inc(sem("l0_logits"), 1)
            pe.wait_ge(sem("l0_logits_ready"), 2)
            for t in range(NT):
                ins = tp(PS[:, 2, t * E0:(t + 1) * E0], LG[:, t * P:(t + 1) * P], ident[0:E0, 0:E0])
            ins.then_inc(sem("l0_logits_turned"), 1)
            pe.wait_ge(sem("ctx_normed"), 1)
            for b in range(B):
                ins = tp(PS[:, 5, b * C:(b + 1) * C], CTXH[:, b, :], ident[0:C, 0:C])
            ins.then_inc(sem("ctx_turned"), 1)
            pe.wait_ge(sem("ctxn_ready"), 1)
            cross_kv(1, 0, 1, w("L1x_Wk"), w("L1x_Wv"), CTXN[:, :])
            pe.wait_ge(sem("places_ready"), 1)
            for t in range(NT):
                ins = tp(PS[:, 3, t * E0:(t + 1) * E0], CUM[:, t * P:(t + 1) * P], ident[0:E0, 0:E0])
            ins.then_inc(sem("places_turned"), 1)
            pe.wait_ge(sem("xp_ready"), 1)
            for t in range(NT):
                pe.wait_ge(sem("slots_ready"), t + 1)
                for n in range(2):
                    for i in range(3):
                        ins = mm(PS[:, 4 + n, :], XP[:, t, i, :], S0[:, t, cols(n)], start=(t == 0 and i == 0),
                                 stop=(t == NT - 1 and i == 2))
                    if t == NT - 1:
                        ins.then_inc(sem("gathered"), 1)
            pe.wait_ge(sem("shares_ready"), 1)
            pe.wait_ge(sem("kv1_raw"), 1)
            for n in range(2):
                for t in range(NT):
                    ins = mm(PS[0:48, 6 + n, :], WP[:, t, :, :].rearrange("p i e -> p (i e)"), S0[:, t, cols(n)],
                             start=(t == 0), stop=(t == NT - 1))
                ins.then_inc(sem("shares_gathered"), 1)
            pe.wait_ge(sem("idb_ready"), 1)
            pe.wait_ge(sem("gathered_ready"), 2)

            def slots_turn(q):
                if q >= 2:
                    pe.wait_ge(sem("slots_turned_ready"), q - 1)
                for t in range(NT):
                    ins = tp(PS[:, 4 + q % 2, :].bitcast(BF16)[:, t * P:(t + 1) * P], S0[:, t, q * P:(q + 1) * P], IDB[:, :])
                ins.then_inc(sem("slots_turned"), 1)

            def hidden0(q):
                sel = c("pairsel", E0)[:, q * P:(q + 1) * P]
                mm(PS[:, q % 2, :], sel, B0[:, 0:F], start=True, stop=False)
                for j in range(2):
                    n = 2 * q + j
                    expert_ready(pe, n)
                    ins = mm(PS[64 * j:64 * j + 64, q % 2, :], XET[:, n * SLOTS:(n + 1) * SLOTS],
                             RINGW[:, n % RING, 0:F], start=False, stop=True)
                ins.then_inc(sem("l0_hidden"), 1)

            hidden0(0)
            pe.wait_ge(sem("shares_own"), 2)
            for q in range(PAIRS):
                ins = mm(PS[:, 7, q:q + 1], GM48[:, q * P:(q + 1) * P], c("iota", 48)[:, 0:1], start=True, stop=True)
            ins.then_inc(sem("shares_turned"), 1)
            for q in range(PAIRS):
                pe.wait_ge(sem("l0_gelu"), q + 1)
                for ch in range(FC):
                    ins = tp(PS[:, 2, ch * P:(ch + 1) * P], HS[:, ch * P:(ch + 1) * P], ident)
                ins.then_inc(sem("l0_hidden_turned"), 1)
                if q + 1 < PAIRS:
                    hidden0(q + 1)
                pe.wait_ge(sem("l0_hidden_ready"), q + 1)
                if q:
                    pe.wait_ge(sem("yp_ready"), q)
                sel = c("pairsel", E0)[:, q * P:(q + 1) * P]
                mm(PS[:, 3, 0:D], sel, B0[:, F:F + D], start=True, stop=False)
                for ch in range(FC):
                    for j in range(2):
                        n = 2 * q + j
                        ins = mm(PS[64 * j:64 * j + 64, 3, 0:D], HST[:, ch * P + 64 * j:ch * P + 64 * j + 64],
                                 RINGW[:, n % RING, F + ch * D:F + (ch + 1) * D], start=False, stop=(ch == FC - 1))
                ins.then_inc(sem("expert_used"), 2)
                slots_turn(q)
                if 0 <= q - VALUES_AT < B:
                    cross_vw(1, q - VALUES_AT, 1, ident)
            pe.wait_ge(sem("yp_ready"), PAIRS)
            pe.wait_ge(sem("slots_turned_ready"), PAIRS)
            for t in range(NT):
                for q in range(PAIRS):
                    for i in range(3):
                        ins = mm(PS[:, 4 + t // HT, (t % HT) * D:(t % HT + 1) * D], S0T[:, q, t * P:(t + 1) * P],
                                 YP[:, q, i, :], start=(q == 0 and i == 0), stop=(q == PAIRS - 1 and i == 2))
                if t % HT == HT - 1:
                    ins.then_inc(sem("scattered"), 1)

            def moe(k, router_w, n, second, norms, next_m, next_norm):
                m = {1: 8, 2: 10, 3: 12}[k]

                def logits(b):
                    turned(m, b)
                    for t in range(HT * b, HT * b + HT):
                        ins = mm(PS[:, 6, t * 16:t * 16 + n], HTR[:, t * P:(t + 1) * P], router_w, start=True, stop=True)
                    return ins

                logits(0)

                def hidden(i):
                    e, b = MOE_ORDER[i]
                    g, slot = 16 * (k - 1) + i, (E0 + E * (k - 1) + e) % RING
                    if b == 0:
                        expert_ready(pe, E0 + E * (k - 1) + e)
                    for ch in range(FC):
                        if g >= 1:
                            pe.wait_ge(sem("moe_gelu"), 4 * (g - 1) + ch + 1)
                        mm(PS[:, ch, :], RINGW[:, slot, ch * P:(ch + 1) * P], HTR[:, cols(b)], start=True, stop=True)\
                            .then_inc(sem("moe_hidden"), 1)

                hidden(0)
                for i in range(2 * E):
                    e, b = MOE_ORDER[i]
                    g, slot = 16 * (k - 1) + i, (E0 + E * (k - 1) + e) % RING
                    if i + 1 < 2 * E:
                        hidden(i + 1)
                    pe.wait_ge(sem("moe_gelu"), 4 * g + 4)
                    if i == BIAS_AT:
                        pe.wait_ge(sem("comb_ready"), k)
                    if i >= 2:
                        pe.wait_ge(sem("moe_summed"), g - 1)
                    for j in range(HT):
                        for ch in range(FC):
                            ins = mm(PS[:, 4 + g % 2, j * D:(j + 1) * D], HB[g % 2][:, ch, j * P:(j + 1) * P],
                                     RINGW[:, slot, F + ch * D:F + (ch + 1) * D], start=(ch == 0), stop=(ch == FC - 1))
                    ins.then_inc(sem("moe_out"), 1)
                    if i == 0:
                        turn(m, 1, XH, "xh_ready", norms)
                        logits(1).then_inc(sem("router_done"), 1)
                    if b:
                        pe.wait_ge(sem("moe_out"), g + 1)
                        nc.tensor.nop().then_inc(sem("expert_used"), 1)
                    if i == BIAS_AT and second is not None:
                        for b2 in range(B):
                            for j in range(HT):
                                ins = tp(PS[0:E, 6 + b2, j * P:(j + 1) * P], GC[:, HT * b2 + j, 0:E], ident)
                            ins.then_inc(sem("comb_turned"), 1)
                        for b2 in range(B):
                            pe.wait_ge(sem("combt_ready"), 2 * second + b2 + 1)
                            for j in range(HT):
                                ins = mm(PS[:, 6 + b2, j * D:(j + 1) * D], COMBT[0:E, (HT * b2 + j) * P:(HT * b2 + j + 1) * P],
                                         B2[:, second, :], start=True, stop=True)
                            ins.then_inc(sem("moe_bias"), 1)
                    if k < 3:
                        chunks = 1 if k == 1 else 8
                        if i == PREPARE_AT and second is not None:
                            pe.wait_ge(sem("bias_added"), 2)
                        if 0 <= i - PREPARE_AT < (chunks + 2) // 3:
                            wk, wv = (("L2x_Wk", "L2x_Wv"), ("L3x_wk", "L3x_wv"))[k - 1]
                            cross_kv(k + 1, i - PREPARE_AT, chunks, w(wk), w(wv), w("ctxT"))
                        if 0 <= i - VW_AT < 4:
                            cross_vw(k + 1, i - VW_AT, 2, w(("L2x_Wo", "L3x_wout")[k - 1]))
                        if i == NEXT_AT:
                            pe.wait_ge(sem(f"vw{k + 1}_ready"), 4)
                            turn(next_m, 0, XH, "xh_ready", next_norm)

            cross_tiles(1, 8, 1, w("L1x_Wq"), 4, 2)
            for b in range(B):
                turn(5, b, XH, "xh_ready", 4 + b + 1)
                turned(5, b)
                for j in range(HT):
                    ins = mm(PS[:, b, j * D:(j + 1) * D], tile_of(YT, b, j), w("L1x_Wo"), start=True, stop=True)
                ins.then_inc(sem("l1_wo"), 1)
            for b in range(B):
                turn(6, b, XH, "xh_ready", 6 + b + 1)
                turned(6, b)
                for which, names in enumerate((("L1f_Wq", "L1f_WqR"), ("L1f_Wk", "L1f_WkR"))):
                    if b and which:
                        pe.wait_ge(sem("qk_pieces"), 1)
                    for n, name in enumerate(names):
                        ins = mm(PS[:, QK_BANKS[b][which] + n, :], w(name), HTR[:, cols(b)], start=True, stop=True)
                    ins.then_inc(sem("qk_done"), 1)
                for j in range(HT):
                    ins = mm(PS[:, 4 + b, j * D:(j + 1) * D], tile_of(HTR, b, j), w("L1f_Wv"), start=True, stop=True)
                ins.then_inc(sem("v_done"), 1)

            def max_scores(g, un):
                b = g // 4
                i = 8 * g + un
                h = 4 * (g % 4) + un // 2
                if un == 0 and g % 4 == 0:
                    pe.wait_ge(sem(f"stacked{b}"), 16 * 6)
                    pe.wait_ge(sem("k_turned"), 1)
                if i >= 2:
                    pe.wait_ge(sem("max_done"), i - 1)
                for x in range(2):
                    q0 = N * b + (2 * (un % 2) + x) * P
                    ins = mm(PS[:, 2 * (i % 2) + x, :], QS[0:72, h, q0:q0 + P], KS[0:72, h, cols(b)], start=True, stop=True)
                ins.then_inc(sem("max_scores"), 1)

            def turn_max(g):
                pe.wait_ge(sem("max_pieces"), g + 1)
                if g >= 3:
                    pe.wait_ge(sem("heads_ready"), g - 2)
                elif g:
                    pe.wait_ge(sem("max_rows"), g)
                for t in range(HT):
                    ins = tp(PS[0:12, 7, 0:256].bitcast(BF16)[:, t * P:(t + 1) * P],
                             MPB[:, t, :, :].rearrange("p i h -> p (i h)"), IDB[:, :])
                ins.then_inc(sem("max_turned"), 1)

            def attend(g, p):
                b = g // 4
                if g % 4 == 0 and p == 0:
                    pe.wait_ge(sem("v_ready"), 2)
                    pe.wait_ge(sem("ones_stacked"), 16)
                if p == 0:
                    pe.wait_ge(sem(f"max_stacked{g % 2}"), 16 * (g // 2 + 1))
                for i in (2 * p, 2 * p + 1):
                    idx = 16 * g + i
                    h = 4 * (g % 4) + i % 4
                    if idx >= 2:
                        pe.wait_ge(sem("probs"), idx - 1)
                    k0 = N * b + (i // 4) * P
                    mm(PS[:, 4 + idx % 2, :], KS[0:75, h, k0:k0 + P], QS[0:75, h, cols(b)], start=True, stop=True)\
                        .then_inc(sem("scores"), 1)

            def values(g, kt):
                b = g // 4
                pe.wait_ge(sem("probs"), 16 * g + 4 * kt + 4)
                if g and kt == 0:
                    pe.wait_ge(sem("heads_copied"), g)
                for j in range(4):
                    idx = 16 * g + 4 * kt + j
                    ins = mm(PS[32 * j:32 * j + 32, 6, :], VS[:, HT * b + kt, 4 * (g % 4) + j, :], PR[idx % 8],
                             start=(kt == 0), stop=(kt == 3))
                ins.then_inc(sem("pv_done"), 1)

            def turn_heads(g):
                pe.wait_ge(sem("heads_copied"), g + 1)
                pe.wait_ge(sem("max_rows"), min(g + 3, 8))
                if g >= 6:
                    pe.wait_ge(sem("heads_ready"), g)
                for t in range(HT):
                    ins = tp(PS[:, 7, t * P:(t + 1) * P], OT[:, t * P:(t + 1) * P], ident)
                ins.then_inc(sem("heads_turned"), 1)

            def attention_out(b):
                turned(7, b)
                for j in range(HT):
                    ins = mm(PS[:, 5 * b, j * D:(j + 1) * D], tile_of(HTR, b, j), w("L1f_Wo"), start=True, stop=True)
                ins.then_inc(sem("l1f_o"), 1)

            for un in range(8):
                max_scores(0, un)
            turn_max(0)
            for g in range(8):
                for p in range(8):
                    for g2, un in MAX_AHEAD(g, p):
                        max_scores(g2, un)
                    attend(g, p)
                    if p == 1 and g:
                        values(g - 1, 3)
                    if p % 2 and p > 1:
                        values(g, p // 2 - 1)
                    if p == (2 if g else 5) and g <= 6:
                        turn_max(g + 1)
                    if p == 4 and g:
                        turn_heads(g - 1)
                    if (g, p) == (6, 1):
                        pe.wait_ge(sem("max_done"), 64)
                        turn(7, 0, Y, "heads_ready", 4, bank=2)
                    if (g, p) == (6, 3):
                        attention_out(0)
                    if (g, p) == (7, 3):
                        turn(8, 0, XH, "xh_ready", 9, bank=3)
            values(7, 3)
            turn_heads(7)
            turn(7, 1, Y, "heads_ready", 8)
            attention_out(1)
            moe(1, w("L1f_Wg"), E, 0, 10, 9, 11)
            cross_tiles(2, 16, 1, w("L2x_Wq"), 9, 10)
            moe(2, w("L2f_router"), E + 1, None, 14, 11, 15)
            cross_tiles(3, 16, 8, w("L3x_wq"), 11, 14)
            moe(3, w("L3f_router"), E, 1, 18, None, None)


def kernel(**inputs):
    import concourse.bacc as bacc
    from concourse.bass_utils import run_bass_kernel_spmd as run

    a = {n: np.asarray(x) for n, x in inputs.items()}
    turn = np.array([8 * (i // 8) + (i % 8 + 4) % 8 for i in range(D)])
    order = np.array([8 * (i % 16) + i // 16 for i in range(D)])

    def chunked(m):
        return m.reshape(-1, P, m.shape[1]).transpose(1, 0, 2).reshape(P, -1)

    def col(vec):
        return vec.reshape(-1, 1)

    parts = {
        "L0_WqT": a["L0_xattn_Wq"].T, "L0_WkT": a["L0_xattn_Wk"].T, "L0_WvT": a["L0_xattn_Wv"].T,
        "L0_WpT": a["L0_xattn_Wp"].T, "L0_routerT": a["L0_ffn_router_weight"].T,
        "L1x_Wq": a["L1_xattn_Wq"], "L1x_Wk": a["L1_xattn_Wk"], "L1x_Wv": a["L1_xattn_Wv"], "L1x_Wo": a["L1_xattn_Wo"],
        "L1f_Wq": a["L1_ffn_Wq"][:, order], "L1f_WqR": a["L1_ffn_Wq"][:, turn[order]], "L1f_Wk": a["L1_ffn_Wk"][:, order],
        "L1f_WkR": a["L1_ffn_Wk"][:, turn[order]], "L1f_Wv": a["L1_ffn_Wv"], "L1f_Wo": a["L1_ffn_Wo"], "L1f_Wg": a["L1_ffn_Wg"],
        "L2x_Wq": a["L2_xattn_W_q"], "L2x_Wk": a["L2_xattn_W_k"], "L2x_Wv": a["L2_xattn_W_v"], "L2x_Wo": a["L2_xattn_W_o"],
        "L2f_router": a["L2_ffn_router_w"],
        "L3x_wq": a["L3_xattn_w_q"], "L3x_wk": a["L3_xattn_w_kv"][:, :1024], "L3x_wv": a["L3_xattn_w_kv"][:, 1024:],
        "L3x_wout": chunked(a["L3_xattn_w_out"]), "L3f_router": a["L3_ffn_w_router"],
        "pre_g": col(a["L1_xattn_pre_g"]), "pre_b": col(a["L1_xattn_pre_b"]),
        "L3_gamma": col(a["L3_xattn_ln_gamma"]), "L3_beta": col(a["L3_xattn_ln_beta"]),
        "bq": col(a["L1_ffn_bq"][order]), "bqR": col(a["L1_ffn_bq"][turn[order]]),
        "bk": col(a["L1_ffn_bk"][order]), "bkR": col(a["L1_ffn_bk"][turn[order]]),
        "L1_b1": a["L1_ffn_b1"].reshape(E * FC, P).T, "L3_b1": a["L3_ffn_b1"].reshape(E * FC, P).T,
        "ctxT": a["ctx_1024"].reshape(B * C, D).T,
    }
    rows = {
        "g_xattn": a["g_xattn"], "g_ffn": a["g_ffn"], "gate": a["L3_xattn_gate"], "focus": a["L0_xattn_focusing_factor"].reshape(1),
        "norm_weight": a["L0_ffn_norm_weight"], "ln_g": a["L1_xattn_ln_g"], "ln_b": a["L1_xattn_ln_b"],
        "bv": a["L1_ffn_bv"], "bo": a["L1_ffn_bo"], "g1": a["L1_ffn_g1"], "be1": a["L1_ffn_be1"],
        "g2": a["L1_ffn_g2"], "be2": a["L1_ffn_be2"], "bg": a["L1_ffn_bg"], "L2_bo": a["L2_xattn_b_o"],
        "L2_router_b": a["L2_ffn_router_b"], "b_out": a["L3_xattn_b_out"],
    }

    def experts(w1, w2):
        n = w1.shape[0]
        second = w2.reshape(n, FC, P, D).transpose(0, 2, 1, 3).reshape(n, P, FC * D)
        return np.concatenate([w1, second], 2)

    arrays = {
        "wpack": np.concatenate([parts[n] for n, _ in W_PARTS], 1),
        "rpack": np.concatenate([rows[n] for n, _ in R_PARTS])[None],
        "cpack": shape_constants(),
        "ones": np.full((3, 16 * T // 2), 0x3F803F80, np.uint32).view(np.float32),
        "ctx_rows": a["ctx_1024"].transpose(1, 0, 2),
        "x": a["x"].reshape(NT, P, D).transpose(1, 0, 2),
        "up0": experts(a["L0_ffn_fc1_weight"].transpose(0, 2, 1), a["L0_ffn_fc2_weight"].transpose(0, 2, 1)),
        "up": np.concatenate([experts(a["L1_ffn_W1"], a["L1_ffn_W2"]), experts(a["L2_ffn_w1"], a["L2_ffn_w2"]),
                              experts(a["L3_ffn_w1"], a["L3_ffn_w2"])]),
        "b_l0": np.concatenate([a["L0_ffn_fc1_bias"], a["L0_ffn_fc2_bias"], a["L0_ffn_router_bias"][:, None]], 1),
        "b2_l1": a["L1_ffn_b2"], "b2_l3": a["L3_ffn_b2"],
    }
    nc = bacc.Bacc("TRN2", target_bir_lowering=False, num_devices=1)
    arrays = {n: np.ascontiguousarray(x) for n, x in arrays.items()}
    t = {n: nc.dram_tensor(n, x.shape, F32, kind="ExternalInput").ap() for n, x in arrays.items()}
    out = nc.dram_tensor("out", (P, NT, D), F32, kind="ExternalOutput").ap()
    scratch = nc.dram_tensor("scratch", (6, P, T), BF16).ap()
    build(nc, t["wpack"], t["rpack"], t["cpack"], t["ones"], t["ctx_rows"], t["x"], t["up0"], t["up"], t["b_l0"],
          t["b2_l1"], t["b2_l3"], scratch, out)
    r = run(nc, [arrays], core_ids=[0])
    return r.results[0]["out"].transpose(1, 0, 2).reshape(B, N, D)
```
